# Optimizing a Trainium2 kernel written in Bass

```python
import numpy as np
import jax
import jax.numpy as jnp

def _softmax(x, axis=-1):
    return jax.nn.softmax(x, axis=axis)

def _gelu(x):
    return jax.nn.gelu(x, approximate=True)

def _silu(x):
    return jax.nn.silu(x)

def _sigmoid(x):
    return jax.nn.sigmoid(x)

def _layernorm(x, axis=-1, eps=1e-05):
    m = jnp.mean(x, axis=axis, keepdims=True)
    v = jnp.var(x, axis=axis, keepdims=True)
    return (x - m) / jnp.sqrt(v + eps)

def _scatter_add(tgt, idx, src, axis=0):
    return tgt.at[idx].add(src)

def _segment_sum(src, seg, n):
    return jax.ops.segment_sum(src, seg, n)
kernel_name = 'mk_seq_postln_d2_jaxref_r8_1fc8ea'

def setup_inputs(seed: int=0):
    np.random.seed(seed)
    _w = jnp.asarray

    def _L0_attn_setup():
        import jax, jax.numpy as jnp
        import numpy as np
        D_MODEL = 128
        N_HEADS = 16
        D_HEAD = 64
        BATCH = 4
        SEQ = 256
        NEG = -1000000000.0
        key = jax.random.key(seed)
        k1, k2, k3, k4, k5 = jax.random.split(key, 5)
        x = jax.random.normal(k1, (BATCH, SEQ, D_MODEL), dtype=jnp.float32)
        std = 0.02
        wq = jax.random.normal(k2, (N_HEADS, D_HEAD, D_MODEL), dtype=jnp.float32) * std
        wk = jax.random.normal(k3, (N_HEADS, D_HEAD, D_MODEL), dtype=jnp.float32) * std
        wv = jax.random.normal(k4, (N_HEADS, D_HEAD, D_MODEL), dtype=jnp.float32) * std
        wo = jax.random.normal(k5, (D_MODEL, N_HEADS * D_HEAD), dtype=jnp.float32) * std
        return {'x': x, 'wq': wq, 'wk': wk, 'wv': wv, 'wo': wo}
    _L0_attn_in = _L0_attn_setup()

    def _L0_ffn_setup():
        import jax, jax.numpy as jnp
        import numpy as np
        TOP_K = 2
        key = jax.random.key(seed)
        k1, k2, k3, k4 = jax.random.split(key, 4)
        B, T, D, F, E = (2, 128, 128, 256, 8)
        x = jax.random.normal(k1, (B, T, D), dtype=jnp.float32)
        Wg = jax.random.normal(k2, (D, E), dtype=jnp.float32) * 0.02
        W1 = jax.random.normal(k3, (E, D, F), dtype=jnp.float32) * 0.02
        W2 = jax.random.normal(k4, (E, F, D), dtype=jnp.float32) * 0.02
        return {'x': x, 'Wg': Wg, 'W1': W1, 'W2': W2}
    _L0_ffn_in = _L0_ffn_setup()

    def _L1_attn_setup():
        import jax, jax.numpy as jnp
        import numpy as np
        EPS_RMS = 1e-06
        EPS_LN = 1e-05
        ETA_MIN = 1e-06
        B, T, D, F = (8, 64, 128, 64)

        def _rmsnorm(x, w):
            return x * jax.lax.rsqrt(jnp.mean(x * x, axis=-1, keepdims=True) + EPS_RMS) * w

        def _phi(x):
            return jax.nn.elu(x) + 1.0

        def _ln2(M):
            mu = jnp.mean(M, axis=(-2, -1), keepdims=True)
            var = jnp.mean((M - mu) ** 2, axis=(-2, -1), keepdims=True)
            return (M - mu) * jax.lax.rsqrt(var + EPS_LN)

        def _reference_tuple_inner(x, norm_weight, Wk, Wv, Wq, eta, Wout):
            b, t, d = x.shape
            f = Wk.shape[0]
            x_norm = _rmsnorm(x, norm_weight)
            k = _phi(jnp.einsum('btd,fd->btf', x_norm, Wk))
            v = jnp.einsum('btd,ed->bte', x_norm, Wv)
            eta_c = jnp.maximum(jnp.abs(eta), ETA_MIN)

            def step(M, kv):
                k_t, v_t = kv
                v_pred = jnp.einsum('bf,bfd->bd', k_t, M)
                surprise = jnp.linalg.norm(v_t - v_pred, axis=-1, keepdims=True)
                delta = k_t[:, :, None] * v_t[:, None, :]
                M = M + eta_c[None, :, None] * surprise[:, :, None] * delta
                return (_ln2(M), None)
            M0 = jnp.zeros((b, f, d), dtype=x.dtype)
            kT = jnp.transpose(k, (1, 0, 2))
            vT = jnp.transpose(v, (1, 0, 2))
            M, _ = jax.lax.scan(step, M0, (kT, vT))
            q = _phi(jnp.einsum('btd,fd->btf', x_norm, Wq))
            mem_out = jnp.einsum('btf,bfd->btd', q, M)
            out = jnp.einsum('btd,ed->bte', mem_out, Wout)
            output = x + out
            return (output, M)
        key = jax.random.key(seed)
        ks = jax.random.split(key, 5)
        x = jax.random.normal(ks[0], (B, T, D), dtype=jnp.float32)
        norm_weight = jnp.ones((D,), dtype=jnp.float32)
        Wk = jax.random.normal(ks[1], (F, D), dtype=jnp.float32) * 0.02
        Wv = jax.random.normal(ks[2], (D, D), dtype=jnp.float32) * 0.02
        Wq = jax.random.normal(ks[3], (F, D), dtype=jnp.float32) * 0.02
        Wout = jax.random.normal(ks[4], (D, D), dtype=jnp.float32) * 0.02
        eta = jnp.ones((F,), dtype=jnp.float32) * 0.01
        return {'x': x, 'norm_weight': norm_weight, 'Wk': Wk, 'Wv': Wv, 'Wq': Wq, 'eta': eta, 'Wout': Wout}
    _L1_attn_in = _L1_attn_setup()

    def _L1_ffn_setup():
        import jax, jax.numpy as jnp
        import numpy as np
        B, T, D, E, H, K = (2, 256, 128, 8, 512, 2)
        key = jax.random.key(seed)
        ks = jax.random.split(key, 8)
        s = 0.02
        return {'x': jax.random.normal(ks[0], (B, T, D), jnp.float32), 'rw1': jax.random.normal(ks[1], (D, D), jnp.float32) * s, 'rb1': jnp.zeros((D,), jnp.float32), 'rw2': jax.random.normal(ks[2], (D, E), jnp.float32) * s, 'rb2': jnp.zeros((E,), jnp.float32), 'we1': jax.random.normal(ks[3], (E, D, H), jnp.float32) * s, 'be1': jnp.zeros((E, H), jnp.float32), 'we2': jax.random.normal(ks[4], (E, H, D), jnp.float32) * s, 'be2': jnp.zeros((E, D), jnp.float32)}
    _L1_ffn_in = _L1_ffn_setup()
    _d = {'L0_attn_x': _L0_attn_in['x'], 'L0_attn_wq': _L0_attn_in['wq'], 'L0_attn_wk': _L0_attn_in['wk'], 'L0_attn_wv': _L0_attn_in['wv'], 'L0_attn_wo': _L0_attn_in['wo'], 'L0_ffn_Wg': _L0_ffn_in['Wg'], 'L0_ffn_W1': _L0_ffn_in['W1'], 'L0_ffn_W2': _L0_ffn_in['W2'], 'L1_attn_norm_weight': _L1_attn_in['norm_weight'], 'L1_attn_Wk': _L1_attn_in['Wk'], 'L1_attn_Wv': _L1_attn_in['Wv'], 'L1_attn_Wq': _L1_attn_in['Wq'], 'L1_attn_eta': _L1_attn_in['eta'], 'L1_attn_Wout': _L1_attn_in['Wout'], 'L1_ffn_rw1': _L1_ffn_in['rw1'], 'L1_ffn_rb1': _L1_ffn_in['rb1'], 'L1_ffn_rw2': _L1_ffn_in['rw2'], 'L1_ffn_rb2': _L1_ffn_in['rb2'], 'L1_ffn_we1': _L1_ffn_in['we1'], 'L1_ffn_be1': _L1_ffn_in['be1'], 'L1_ffn_we2': _L1_ffn_in['we2'], 'L1_ffn_be2': _L1_ffn_in['be2']}
    _x0 = _d['L0_attn_x']
    _d['L0_attn_x'] = jax.random.normal(jax.random.fold_in(jax.random.key(seed), 1), (4, 512, 128), dtype=_x0.dtype)
    del _x0
    return _d

def reference(L0_attn_x, L0_attn_wq, L0_attn_wk, L0_attn_wv, L0_attn_wo, L0_ffn_Wg, L0_ffn_W1, L0_ffn_W2, L1_attn_norm_weight, L1_attn_Wk, L1_attn_Wv, L1_attn_Wq, L1_attn_eta, L1_attn_Wout, L1_ffn_rw1, L1_ffn_rb1, L1_ffn_rw2, L1_ffn_rb2, L1_ffn_we1, L1_ffn_be1, L1_ffn_we2, L1_ffn_be2):

    def _L0_attn_ref(x, wq, wk, wv, wo):
        import jax, jax.numpy as jnp
        import numpy as np
        D_MODEL = 128
        N_HEADS = 16
        D_HEAD = 64
        BATCH = 4
        SEQ = 256
        NEG = -1000000000.0
        b, s, _ = x.shape
        scale = jnp.sqrt(jnp.asarray(D_HEAD, x.dtype))
        q = jnp.einsum('bsd,hed->bhse', x, wq)
        k = jnp.einsum('bsd,hed->bhse', x, wk)
        v = jnp.einsum('bsd,hed->bhse', x, wv)
        scores = jnp.einsum('bhse,bhte->bhst', q, k) / scale
        causal_mask = jnp.triu(jnp.ones((s, s), dtype=bool), k=1)
        scores = jnp.where(causal_mask, jnp.asarray(NEG, scores.dtype), scores)
        weights = jax.nn.softmax(scores, axis=-1)
        heads = jnp.einsum('bhst,bhte->bhse', weights, v)
        concat = heads.transpose(0, 2, 1, 3).reshape(b, s, N_HEADS * D_HEAD)
        return concat @ wo.T

    def _L0_ffn_ref(x, Wg, W1, W2):
        import jax, jax.numpy as jnp
        import numpy as np
        TOP_K = 2
        B, T, D = x.shape
        E = Wg.shape[-1]
        xt = x.reshape(B * T, D)
        logits = xt @ Wg
        probs = jax.nn.softmax(logits, axis=-1)
        topw, topi = jax.lax.top_k(probs, TOP_K)
        topw = topw / jnp.sum(topw, axis=-1, keepdims=True)
        combine = jnp.sum(jax.nn.one_hot(topi, E, dtype=xt.dtype) * topw[..., None], axis=1)
        h = jax.nn.relu(jnp.einsum('nd,edf->enf', xt, W1))
        y = jnp.einsum('enf,efd->end', h, W2)
        out = jnp.einsum('ne,end->nd', combine, y)
        return out.reshape(B, T, D)

    def _L1_attn_ref(x, norm_weight, Wk, Wv, Wq, eta, Wout):
        import jax, jax.numpy as jnp
        import numpy as np
        EPS_RMS = 1e-06
        EPS_LN = 1e-05
        ETA_MIN = 1e-06
        B, T, D, F = (8, 64, 128, 64)

        def _rmsnorm(x, w):
            return x * jax.lax.rsqrt(jnp.mean(x * x, axis=-1, keepdims=True) + EPS_RMS) * w

        def _phi(x):
            return jax.nn.elu(x) + 1.0

        def _ln2(M):
            mu = jnp.mean(M, axis=(-2, -1), keepdims=True)
            var = jnp.mean((M - mu) ** 2, axis=(-2, -1), keepdims=True)
            return (M - mu) * jax.lax.rsqrt(var + EPS_LN)

        def _reference_tuple_inner(x, norm_weight, Wk, Wv, Wq, eta, Wout):
            b, t, d = x.shape
            f = Wk.shape[0]
            x_norm = _rmsnorm(x, norm_weight)
            k = _phi(jnp.einsum('btd,fd->btf', x_norm, Wk))
            v = jnp.einsum('btd,ed->bte', x_norm, Wv)
            eta_c = jnp.maximum(jnp.abs(eta), ETA_MIN)

            def step(M, kv):
                k_t, v_t = kv
                v_pred = jnp.einsum('bf,bfd->bd', k_t, M)
                surprise = jnp.linalg.norm(v_t - v_pred, axis=-1, keepdims=True)
                delta = k_t[:, :, None] * v_t[:, None, :]
                M = M + eta_c[None, :, None] * surprise[:, :, None] * delta
                return (_ln2(M), None)
            M0 = jnp.zeros((b, f, d), dtype=x.dtype)
            kT = jnp.transpose(k, (1, 0, 2))
            vT = jnp.transpose(v, (1, 0, 2))
            M, _ = jax.lax.scan(step, M0, (kT, vT))
            q = _phi(jnp.einsum('btd,fd->btf', x_norm, Wq))
            mem_out = jnp.einsum('btf,bfd->btd', q, M)
            out = jnp.einsum('btd,ed->bte', mem_out, Wout)
            output = x + out
            return (output, M)
        return _reference_tuple_inner(x, norm_weight, Wk, Wv, Wq, eta, Wout)[0]

    def _L1_ffn_ref(x, rw1, rb1, rw2, rb2, we1, be1, we2, be2):
        import jax, jax.numpy as jnp
        import numpy as np
        B, T, D, E, H, K = (2, 256, 128, 8, 512, 2)
        b, t, d = x.shape
        xt = x.reshape(b * t, d)
        n = xt.shape[0]
        logits = jax.nn.silu(xt @ rw1 + rb1) @ rw2 + rb2
        _, idx = jax.lax.top_k(logits, K)
        mask = jnp.zeros((n, E), bool).at[jnp.arange(n)[:, None], idx].set(True)
        w = jax.nn.softmax(jnp.where(mask, logits, -jnp.inf), axis=1)
        h = jax.nn.silu(jnp.einsum('nd,edh->enh', xt, we1) + be1[:, None, :])
        eo = jnp.einsum('enh,ehd->end', h, we2) + be2[:, None, :]
        y = xt + jnp.einsum('ne,end->nd', w, eo)
        return y.reshape(b, t, d)
    x = L0_attn_x
    x = _layernorm(x + _L0_attn_ref(x, L0_attn_wq, L0_attn_wk, L0_attn_wv, L0_attn_wo), axis=-1)
    x = _layernorm(x + _L0_ffn_ref(x, L0_ffn_Wg, L0_ffn_W1, L0_ffn_W2), axis=-1)
    x = _layernorm(x + _L1_attn_ref(x, L1_attn_norm_weight, L1_attn_Wk, L1_attn_Wv, L1_attn_Wq, L1_attn_eta, L1_attn_Wout), axis=-1)
    x = _layernorm(x + _L1_ffn_ref(x, L1_ffn_rw1, L1_ffn_rb1, L1_ffn_rw2, L1_ffn_rb2, L1_ffn_we1, L1_ffn_be1, L1_ffn_we2, L1_ffn_be2), axis=-1)
    return x

_drawn_inputs = setup_inputs


def setup_inputs(seed=0):
    import zlib

    import numpy as np

    out = dict(_drawn_inputs(seed))
    spreads = {'L1_attn_norm_weight': (1.0, 0.2),
     'L1_attn_eta': (0.009999999776482582, 0.6),
     'L1_ffn_rb1': (0.0, 0.8),
     'L1_ffn_rb2': (0.0, 0.1),
     'L1_ffn_be1': (0.0, 0.8),
     'L1_ffn_be2': (0.0, 0.1)}
    factors = {'L0_attn_wq': 8.0,
     'L0_attn_wk': 8.0,
     'L0_attn_wv': 5.522,
     'L0_attn_wo': 5.432,
     'L1_attn_Wq': 8.0,
     'L1_ffn_rw1': 8.0,
     'L1_ffn_rw2': 8.0,
     'L1_ffn_we1': 3.26,
     'L1_ffn_we2': 3.135}
    for name, (base, spread) in spreads.items():
        noise = np.random.default_rng([zlib.crc32(name.encode()), seed]).standard_normal(out[name].shape)
        drawn = base * np.exp(spread * noise) if base else spread * noise
        out[name] = jnp.asarray(drawn.astype(out[name].dtype))
    for name, factor in factors.items():
        out[name] = (out[name] * factor).astype(out[name].dtype)
    return out
```

```python
import concourse.bass as bass
from concourse import mybir
from contextlib import ExitStack


def seq_postln_kernel(nc, ins, out, scratch):
    f32 = mybir.dt.float32
    u32 = mybir.dt.uint32
    ALU = mybir.AluOpType
    ACT = mybir.ActivationFunctionType
    AX = mybir.AxisListType
    ds = bass.ds

    B, S, D, H, E_DIM = 4, 512, 128, 16, 64
    P = 128
    ST = S // P
    NT = B * ST
    HP = H // 2
    UNITS = 2 * ST
    EX = 8
    F1, F2 = 256, 512
    F = 64
    EPS_LN, EPS_RMS, ETA_MIN = 1e-5, 1e-6, 1e-6
    CH = 16
    NCH = S // CH
    DC = P // B
    DD = D // DC
    MN = 4

    with ExitStack() as ctx:
        def sb(name, shape, dt=f32, scope=ctx):
            return scope.enter_context(nc.sbuf_tensor(name, shape, dt))

        def sem(name):
            return ctx.enter_context(nc.semaphore(name))

        ident = sb("ident", [P, P])
        x_rows = sb("x_rows", [P, NT, D])
        xT = sb("xT", [P, B * S])
        norm_rows = sb("norm_rows", [P, ST, D])
        seqT = sb("seqT", [P, S])
        bn = sb("bn", [P, ST, 6])
        mv = sb("mv", [P, ST, 2])
        var_eps = sb("var_eps", [P, ST])
        rstd = sb("rstd", [P, ST])
        neg_half = sb("neg_half", [P, ST])
        iota8 = sb("iota8", [P, EX])
        logits = sb("logits", [P, NT, EX])
        top8 = sb("top8", [P, NT, 8])
        top_i = sb("top_i", [P, NT, 8], u32)
        top_f = sb("top_f", [P, NT, 2])
        hot = sb("hot", [P, 2, NT, EX])
        gate = sb("gate", [P, NT, EX])
        gate_sum = sb("gate_sum", [P, NT])
        wg = sb("wg", [P, EX])
        w1 = sb("w1", [P, 2, F2])
        w2 = sb("w2", [P, 2, F2 // P, D])
        hidden = sb("hidden", [P, 2, F2 // P, S])

        with ExitStack() as A:
            mask = sb("mask", [P, S], scope=A)
            wq = sb("wq", [E_DIM, H, D], scope=A)
            wk = sb("wk", [E_DIM, H, D], scope=A)
            wvT = sb("wvT", [P, H * E_DIM], scope=A)
            woT = sb("woT", [P, HP, D], scope=A)
            qk_all = sb("qk_all", [P, H * D], scope=A)
            qk_pair = sb("qk_pair", [P, 2, D], scope=A)
            query = sb("query", [P, 2, S], scope=A)
            v_pair = sb("v_pair", [P, ST, P], scope=A)
            masked = sb("masked", [P, 2, S], scope=A)
            probs = sb("probs", [P, 3, S], scope=A)
            row_stats = sb("row_stats", [P, UNITS, 4], scope=A)
            probsT = sb("probsT", [P, 2, ST, S], scope=A)
            headsT = sb("headsT", [P, S], scope=A)
            xT_b = sb("xT_b", [P, S], scope=A)
        with ExitStack() as A:
            wkT = sb("wkT", [P, F], scope=A)
            wqT = sb("wqT", [P, F], scope=A)
            wvT1 = sb("wvT1", [P, D], scope=A)
            woutT = sb("woutT", [P, D], scope=A)
            norm_w = sb("norm_w", [P, 1], scope=A)
            eta = sb("eta", [P, F], scope=A)
            blocks = sb("blocks", [P, P], scope=A)
            rms_rows = sb("rms_rows", [P, ST, D], scope=A)
            ms = sb("ms", [P, ST], scope=A)
            junk = sb("junk", [P, D], scope=A)
            qT = sb("qT", [F, B * S], scope=A)
            q_exp = sb("q_exp", [F, S], scope=A)
            k_rows = sb("k_rows", [P, ST, F], scope=A)
            k_exp = sb("k_exp", [P, ST, F], scope=A)
            g_rows = sb("g_rows", [P, ST, F], scope=A)
            v_rows = sb("v_rows", [P, ST, D], scope=A)
            g_mv = sb("g_mv", [P, ST, 2], scope=A)
            v_mv = sb("v_mv", [P, ST, 2], scope=A)
            cm = sb("cm", [P, ST, 2], scope=A)
            cm_t = sb("cm_t", [P, 2, ST], scope=A)
            k_rep = sb("k_rep", [P, 2, CH, F], scope=A)
            g_rep = sb("g_rep", [P, 2, CH, F], scope=A)
            v_rep = sb("v_rep", [P, 2, CH, DD], scope=A)
            cm_rep = sb("cm_rep", [P, 2, CH, 2], scope=A)
            mem = sb("mem", [P, DD, F], scope=A)
            outer = sb("outer", [P, 2, DD, F], scope=A)
            prod = sb("prod", [P, DD, F], scope=A)
            prod2 = sb("prod2", [P, DD * F], scope=A)
            pred = sb("pred", [P, DD], scope=A)
            err = sb("err", [P, DD], scope=A)
            err2 = sb("err2", [P, DD], scope=A)
            sums = sb("sums", [P, 2], scope=A)
            state = sb("state", [P, CH + 1, MN], scope=A)
            coef = sb("coef", [P, CH, MN], scope=A)
            junk4 = sb("junk4", [P, MN], scope=A)
            tau = sb("tau", [P, CH + 1], scope=A)
            rho = sb("rho", [P, 2], scope=A)
            memT = sb("memT", [P, B, F], scope=A)
            mw = sb("mw", [F, B, D], scope=A)
        with ExitStack() as A:
            be1T = sb("be1T", [P, EX, F2 // P], scope=A)
            be2 = sb("be2", [EX, D], scope=A)
            gate_b = sb("gate_b", [P, ST, EX], scope=A)
            gateT = sb("gateT", [EX, ST, P], scope=A)
            h1T = sb("h1T", [P, S], scope=A)
            rw1 = sb("rw1", [P, D], scope=A)
            rw2 = sb("rw2", [P, EX], scope=A)
            rb1 = sb("rb1", [P, 1], scope=A)
            rb2 = sb("rb2", [P, EX], scope=A)

        banks = [ctx.enter_context(nc.psum_tensor(f"bank{i}", [P, 512], f32)) for i in range(8)]
        s_bank, t_bank = banks[0:3], banks[3:5]
        proj_bank, pv_bank, y_bank = banks[5], banks[6], banks[7]

        loaded, qk_made, qk_kept, seq_staged, pair_staged = map(sem, "loaded qk_made qk_kept seq_staged pair_staged".split())
        proj_done, proj_kept, scores_done, dve_seen, pool_seen, act_seen, masked_done = map(
            sem, "proj_done proj_kept scores_done dve_seen pool_seen act_seen masked_done".split())
        exp_done, recip_done, probs_done, transposed, probsT_kept = map(
            sem, "exp_done recip_done probs_done transposed probsT_kept".split())
        heads_done, heads_kept, y_pair_done, y_kept, chain = map(
            sem, "heads_done heads_kept y_pair_done y_kept chain".split())
        consts_set, var_made, rstd_made, rows_normed, rows_T, seqT_kept, xT_stored, rows_stored = map(
            sem, "consts_set var_made rstd_made rows_normed rows_T seqT_kept xT_stored rows_stored".split())
        logits_done, logits_kept, shifted, gate_exp, gate_made = map(
            sem, "logits_done logits_kept shifted gate_exp gate_made".split())
        mem_loaded, kv_done, k_low, k_exped, kv_kept, q_done, q_low, q_exped, q_kept, kv_sent = map(
            sem, "mem_loaded kv_done k_low k_exped kv_kept q_done q_low q_exped q_kept kv_sent".split())
        rep_used, outer_made, outer_used, sums_made, sums_out, w_made, T_made, tau_made, mem_done = map(
            sem, "rep_used outer_made outer_used sums_made sums_out w_made T_made tau_made mem_done".split())
        rep_in = [sem("rep_in0"), sem("rep_in1")]
        mem_sent, memT_in, mw_done, mw_kept, mo_done, mo_kept, pool_chain = map(
            sem, "mem_sent memT_in mw_done mw_kept mo_done mo_kept pool_chain".split())
        d_loaded, h1_done, h1_kept, gate_b_staged, gateT_done, gateT_kept, be_done, be_kept, stored, eta_made, rms_var, rms_normed = map(
            sem, "d_loaded h1_done h1_kept gate_b_staged gateT_done gateT_kept be_done be_kept stored eta_made rms_var rms_normed".split())

        class Mixture:
            def __init__(self, n, width, func, w1_d, w2_d):
                self.tiles, self.func, self.w1_d, self.w2_d, self.width = width // P, func, w1_d, w2_d, width
                self.got = [sem(f"mix{n}_weights0"), sem(f"mix{n}_weights1")]
                self.h_done, self.h_kept = sem(f"mix{n}_h_done"), sem(f"mix{n}_h_kept")
                self.y_done, self.y_kept = sem(f"mix{n}_y_done"), sem(f"mix{n}_y_kept")

        mix1 = Mixture(1, F1, ACT.Relu, ins["W1"], ins["W2"])
        mix2 = Mixture(2, F2, ACT.Silu, ins["we1"], ins["we2"])
        MIX_UNITS = 2 * B

        def unit_width(u):
            return P * (u % ST + 1)

        def flat(ap):
            return ap.rearrange("p a d -> p (a d)")

        class Chain:
            def __init__(self, eng, counter):
                self.eng, self.counter, self.base, self.n = eng, counter, 0, 0

            def __call__(self, instruction):
                self.n += 1
                instruction.then_inc(self.counter, 1)
                self.eng.wait_ge(self.counter, self.base + self.n)

        LOADS = 10 * 16
        block = ctx.enter_context(nc.Block())

        @block.sync
        def _(sp):
            for dst, src in ((wq[:, :, :], "wq"), (wk[:, :, :], "wk"), (xT[:, :], "xT"), (ident[:, :], "ident"),
                             (mask[:, :], "mask"), (wvT[:, :], "wvT"), (woT[:, :, :], "woT"),
                             (x_rows[:, :, :], "x_rows"), (wg[:, :], "wg"), (iota8[:, :], "iota8")):
                sp.dma_start(dst, ins[src]).then_inc(loaded, 16)

            def mixture_weights(m):
                with sp.Fori(0, EX // 2) as ep:
                    for slot in range(2):
                        sp.wait_ge(m.y_done, ep * MIX_UNITS + 1)
                        sp.dma_start(w1[:, slot, 0:m.width],
                                     m.w1_d[:, ds(ep * 2 + slot, 1), :].rearrange("p e f -> p (e f)")).then_inc(m.got[slot], 16)
                        sp.dma_start(w2[:, slot, 0:m.tiles, :],
                                     m.w2_d[:, ds(ep * 2 + slot, 1), :, :].rearrange("p e a d -> p (e a) d")).then_inc(m.got[slot], 16)

            sp.sem_inc(mix1.y_done, 1)
            mixture_weights(mix1)
            sp.wait_ge(mix1.y_done, EX * B + 1)
            for dst, src in ((wkT[:, :], "wkT"), (wqT[:, :], "wqT"), (wvT1[:, :], "wvT1"), (woutT[:, :], "woutT"),
                             (norm_w[:, :], "norm_w"), (eta[:, :], "eta"), (blocks[:, :], "blocks")):
                sp.dma_start(dst, ins[src]).then_inc(mem_loaded, 16)
            sp.sem_inc(kv_sent, 1)
            with sp.Fori(0, B) as b:
                sp.wait_ge(kv_kept, b + 1)
                for dst, src in (("k", k_rows), ("v", v_rows), ("cm", cm)):
                    sp.dma_start(scratch[dst][ds(b * S, S), :].rearrange("(s p) f -> p s f", p=P), src[:, :, :]).then_inc(kv_sent, 16)
            sp.wait_ge(kv_sent, B * 48 + 1)
            with sp.Fori(0, NCH // 2) as cp:
                for half in range(2):
                    sp.wait_ge(rep_used, cp * 2 + (half + 1))
                    for b in range(B):
                        rows = slice(b * DC, (b + 1) * DC)
                        t0 = cp * (2 * CH) + half * CH
                        for dst, src in ((k_rep, "k"), (cm_rep, "cm")):
                            steps = scratch[src][ds(t0 + b * S, CH), :]
                            sp.dma_start(dst[rows, half, :, :], steps.unsqueeze(0).to_broadcast([DC, *steps.shape]))\
                              .then_inc(rep_in[half], 16)
                        sp.dma_start(v_rep[rows, half, :, :],
                                     scratch["v"][ds(t0 + b * S, CH), :].rearrange("t (c e) -> c t e", e=DD))\
                          .then_inc(rep_in[half], 16)
            sp.wait_ge(mem_done, 1)
            sp.dma_start(scratch["m"].rearrange("(p a) f -> p a f", p=P), mem[:, :, :]).then_inc(mem_sent, 16)
            sp.wait_ge(mem_sent, 16)
            sp.dma_start(memT[:, :, :], scratch["m"].rearrange("(b d) f -> d b f", b=B)).then_inc(memT_in, 16)
            sp.wait_ge(mo_kept, B)
            for dst, src in ((be1T[:, :, :], "be1T"), (be2[:, :], "be2"), (rw1[:, :], "rw1"), (rw2[:, :], "rw2"),
                             (rb1[:, :], "rb1"), (rb2[:, :], "rb2")):
                sp.dma_start(dst, ins[src]).then_inc(d_loaded, 16)
            sp.sem_inc(mix2.y_done, 1)
            mixture_weights(mix2)
            sp.wait_ge(rows_stored, 4 * B + 1)
            sp.dma_start(out, x_rows[:, :, :]).then_inc(stored, 16)
            sp.wait_ge(stored, 16)

        @block.gpsimd
        def _(pool):
            pool.memset(neg_half[:, :], -0.5).then_inc(consts_set, 1)
            pool.wait_ge(loaded, LOADS)
            pool.wait_ge(qk_kept, 4)
            pool.wait_ge(consts_set, 1)

            def norm_sequence(n, b, keep_T):
                pool.wait_ge(var_made, n * B + b + 1)
                pool.tensor_tensor(rstd[:, :], var_eps[:, :], neg_half[:, :], ALU.pow).then_inc(rstd_made, 1)
                pool.wait_ge(rows_normed, n * B + b + 1)
                pool.sem_inc(pool_seen, 1)
                pool.tensor_copy(x_rows[:, ds(b * ST, ST), :], norm_rows[:, :, :]).then_inc(rows_stored, 1)
                if keep_T is not None:
                    pool.wait_ge(seqT_kept, keep_T * B + b + 1)
                    pool.sem_inc(pool_seen, 1)
                    pool.tensor_copy(xT[:, ds(b * S, S)], seqT[:, :]).then_inc(xT_stored, 1)

            for free in (seq_staged, xT_stored, rows_stored):
                pool.sem_inc(free, 1)
            with pool.Fori(0, B) as b:
                pool.wait_ge(scores_done, b * (HP * UNITS) + 1)
                pool.sem_inc(pool_seen, 1)
                pool.tensor_copy(xT_b[:, :], xT[:, ds(b * S, S)]).then_inc(seq_staged, 1)
                with pool.Fori(0, HP) as p:
                    pool.wait_ge(proj_done, (b * HP + p) * 3 + 1)
                    pool.sem_inc(pool_seen, 1)
                    pool.tensor_copy(flat(qk_pair[:, :, :]), qk_all[:, ds(p * (2 * D), 2 * D)]).then_inc(pair_staged, 1)
                norm_sequence(0, b, 0)
            with pool.Fori(0, B) as b:
                norm_sequence(1, b, None)
                pool.wait_ge(rms_var, b + 1)
                pool.tensor_tensor(rstd[:, :], var_eps[:, :], neg_half[:, :], ALU.pow).then_inc(rstd_made, 1)
            pool.wait_ge(eta_made, 1)
            with pool.Fori(0, NCH // 2) as cp:
                for half in range(2):
                    pool.wait_ge(rep_in[half], cp * (3 * B * 16) + 3 * B * 16)
                    pool.tensor_tensor(g_rep[:, half, :, :], k_rep[:, half, :, :],
                                       eta[:, :].unsqueeze(1).to_broadcast([P, CH, F]), ALU.mult).then_inc(pool_chain, 1)
                    n0 = cp * (2 * CH) + half * CH
                    for t in range(CH):
                        pool.wait_ge(pool_chain, (cp * 2 + half) * (CH + 1) + t + 1)
                        pool.wait_ge(outer_used, n0 + t + 1)
                        pool.tensor_tensor(outer[:, t % 2, :, :],
                                           g_rep[:, half, t, :].unsqueeze(1).to_broadcast([P, DD, F]),
                                           v_rep[:, half, t, :].unsqueeze(2).to_broadcast([P, DD, F]),
                                           ALU.mult).then_inc(pool_chain, 1)
                        pool.wait_ge(pool_chain, (cp * 2 + half) * (CH + 1) + t + 2)
                        pool.sem_inc(pool_seen, 1)
                        pool.tensor_scalar(outer[:, t % 2, :, :], outer[:, t % 2, :, :], cm_rep[:, half, t, 0:1], None,
                                           ALU.subtract).then_inc(outer_made, 1)
            with pool.Fori(0, B) as b:
                norm_sequence(2, b, 2)
            with pool.Fori(0, B) as b:
                pool.wait_ge(gate_made, 2)
                pool.wait_ge(gateT_done, b + 1)
                pool.sem_inc(pool_seen, 1)
                pool.tensor_copy(gate_b[:, :, :], gate[:, ds(b * ST, ST), :]).then_inc(gate_b_staged, 1)
            with pool.Fori(0, B) as b:
                norm_sequence(3, b, None)

        @block.tensor
        def _(pe):
            def transpose_rows(src, bank, n, b):
                for st in range(ST):
                    t = pe.transpose(bank[:, st * P:(st + 1) * P], src[:, st, :], ident[:, :])
                t.then_inc(rows_T, 1)

            pe.wait_ge(loaded, LOADS)
            for g in range(4):
                for j in range(4):
                    h = 4 * g + j
                    m = pe.matmul(banks[g][:, j * D:(j + 1) * D], wq[:, h, :], wk[:, h, :], start=True, stop=True)
                m.then_inc(qk_made, 1)
            pe.wait_ge(qk_kept, 4)
            for free in (scores_done, proj_done, gateT_done, logits_done, rows_T, q_done):
                pe.sem_inc(free, 1)
            with pe.Fori(0, B) as b:
                with pe.Fori(0, HP) as p:
                    it = b * HP + p
                    pe.wait_ge(seq_staged, b + 2)

                    def scores(u):
                        hh, qt = divmod(u, ST)
                        if u >= 3:
                            pe.wait_ge(masked_done, it * UNITS + (u - 2))
                        pe.matmul(s_bank[u % 3][:, 0:unit_width(u)], query[:, hh, qt * P:(qt + 1) * P],
                                  xT_b[:, 0:unit_width(u)], start=True, stop=True).then_inc(scores_done, 1)

                    def transposes(u):
                        pe.wait_ge(probs_done, it * UNITS + (u + 1))
                        if u >= 2:
                            pe.wait_ge(probsT_kept, it * UNITS + (u - 1))
                        for k in range(u % ST + 1):
                            t = pe.transpose(t_bank[u % 2][:, k * P:(k + 1) * P], probs[:, u % 3, k * P:(k + 1) * P],
                                             ident[:, :])
                        t.then_inc(transposed, 1)

                    pe.wait_ge(pair_staged, it + 1)
                    for hh in range(2):
                        pe.wait_ge(proj_kept, it * 3 + (hh + 1))
                        pe.matmul(proj_bank[:, :], qk_pair[:, hh, :], xT_b[:, :], start=True,
                                  stop=True).then_inc(proj_done, 1)
                    pe.wait_ge(proj_kept, it * 3 + 3)
                    for k in range(ST):
                        m = pe.matmul(proj_bank[:, k * P:(k + 1) * P], xT_b[:, k * P:(k + 1) * P],
                                      wvT[:, ds(p * P, P)], start=True, stop=True)
                    m.then_inc(proj_done, 1)
                    for u in range(UNITS + 2):
                        if u < UNITS:
                            scores(u)
                        if u >= 2:
                            transposes(u - 2)
                    pe.wait_ge(proj_kept, it * 3 + 4)
                    pe.wait_ge(probsT_kept, it * UNITS + UNITS)
                    for k in range(ST):
                        for hh in range(2):
                            m = pe.matmul(pv_bank[hh * 64:(hh + 1) * 64, k * P:S], v_pair[:, k, hh * 64:(hh + 1) * 64],
                                          probsT[:, hh, k, k * P:S], start=(k == 0), stop=(k == ST - 1))
                    m.then_inc(heads_done, 1)
                    pe.wait_ge(heads_kept, it + 1)
                    pe.wait_ge(y_kept, it + 1)
                    for st in range(ST):
                        m = pe.matmul(y_bank[:, st * D:(st + 1) * D], headsT[:, st * P:(st + 1) * P],
                                      woT[:, ds(p, 1), :].rearrange("p a d -> p (a d)"), start=True, stop=True)
                    m.then_inc(y_pair_done, 1)
                pe.wait_ge(rows_normed, b + 1)
                transpose_rows(norm_rows, y_bank, 0, b)
                pe.wait_ge(seqT_kept, b + 1)
                for st in range(ST):
                    m = pe.matmul(pv_bank[:, st * EX:(st + 1) * EX], seqT[:, st * P:(st + 1) * P], wg[:, :], start=True,
                                  stop=True)
                m.then_inc(logits_done, 1)
                pe.wait_ge(logits_kept, b + 1)

            def mixture(m):
                H_BANKS = 4
                with pe.Fori(0, EX // 2) as ep:
                    for j in range(MIX_UNITS + 1):
                        slot, nb = divmod(j, B)
                        if j < MIX_UNITS:
                            if nb == 0:
                                pe.wait_ge(m.got[slot], ep * 32 + 32)
                            for ft in range(m.tiles):
                                n = j * m.tiles + ft
                                pe.wait_ge(m.h_kept, ep * (MIX_UNITS * m.tiles) + n + 1)
                                pe.matmul(banks[n % H_BANKS][:, :], w1[:, slot, ft * P:(ft + 1) * P],
                                          xT[:, nb * S:(nb + 1) * S], start=True, stop=True).then_inc(m.h_done, 1)
                        if j >= 1:
                            slot = (j - 1) // B
                            pe.wait_ge(m.h_kept, ep * (MIX_UNITS * m.tiles) + (j * m.tiles + H_BANKS))
                            pe.wait_ge(m.y_kept, ep * MIX_UNITS + j)
                            for st in range(ST):
                                for ft in range(m.tiles):
                                    y = pe.matmul(banks[4 + (j - 1) % 2][:, st * D:(st + 1) * D],
                                                  hidden[:, (j - 1) % 2, ft, st * P:(st + 1) * P], w2[:, slot, ft, :],
                                                  start=(ft == 0), stop=(ft == m.tiles - 1))
                            y.then_inc(m.y_done, 1)

            pe.wait_ge(xT_stored, B + 1)
            mixture(mix1)
            pe.wait_ge(mem_loaded, 7 * 16)
            with pe.Fori(0, B) as b:
                pe.wait_ge(rms_normed, b + 1)
                transpose_rows(rms_rows, y_bank, 1, b)
                pe.wait_ge(seqT_kept, B + b + 1)
                for st in range(ST):
                    pe.matmul(proj_bank[:, st * F:(st + 1) * F], seqT[:, st * P:(st + 1) * P], wkT[:, :], start=True,
                              stop=True)
                for st in range(ST):
                    m = pe.matmul(pv_bank[:, st * D:(st + 1) * D], seqT[:, st * P:(st + 1) * P], wvT1[:, :], start=True,
                                  stop=True)
                m.then_inc(kv_done, 1)
                pe.matmul(t_bank[0][0:F, :], wqT[:, :], seqT[:, :], start=True, stop=True).then_inc(q_done, 1)
            with pe.Fori(0, NCH // 2) as cp:
                for n in range(2 * CH):
                    pe.wait_ge(sums_made, cp * (2 * CH) + n + 1)
                    pe.matmul(banks[n % 2][:, 0:2], blocks[:, :], sums[:, :], start=True, stop=True).then_inc(sums_out, 1)
            pe.wait_ge(memT_in, 16)
            for b in range(B):
                m = pe.matmul(banks[4][0:F, b * D:(b + 1) * D], memT[:, b, :], woutT[:, :], start=True, stop=True)
            m.then_inc(mw_done, 1)
            pe.wait_ge(mw_kept, 1)
            pe.wait_ge(q_kept, B)
            for b in range(B):
                for st in range(ST):
                    i = b * ST + st
                    m = pe.matmul(banks[b][:, st * D:(st + 1) * D], qT[:, i * P:(i + 1) * P], mw[:, b, :], start=True,
                                  stop=True)
                m.then_inc(mo_done, 1)
            pe.wait_ge(d_loaded, 6 * 16)
            with pe.Fori(0, B) as b:
                pe.wait_ge(rows_normed, 2 * B + b + 1)
                transpose_rows(norm_rows, y_bank, 2, b)
                pe.wait_ge(seqT_kept, 2 * B + b + 1)
                pe.matmul(proj_bank[:, :], rw1[:, :], seqT[:, :], start=True, stop=True).then_inc(h1_done, 1)
                pe.wait_ge(h1_kept, b + 1)
                for st in range(ST):
                    m = pe.matmul(pv_bank[:, st * EX:(st + 1) * EX], h1T[:, st * P:(st + 1) * P], rw2[:, :], start=True,
                                  stop=True)
                m.then_inc(logits_done, 1)
                pe.wait_ge(logits_kept, B + b + 1)
            with pe.Fori(0, B) as b:
                pe.wait_ge(gate_b_staged, b + 1)
                for st in range(ST):
                    m = pe.transpose(proj_bank[0:EX, st * P:(st + 1) * P], gate_b[:, st, :], ident[:, :])
                m.then_inc(gateT_done, 1)
                pe.wait_ge(gateT_kept, b + 1)
                for st in range(ST):
                    m = pe.matmul(pv_bank[:, st * D:(st + 1) * D], gateT[:, st, :], be2[:, :], start=True, stop=True)
                m.then_inc(be_done, 1)
                pe.wait_ge(be_kept, b + 1)
            pe.wait_ge(xT_stored, 2 * B + 1)
            mixture(mix2)

        @block.vector
        def _(dve):
            link = Chain(dve, chain)

            def norm_sequence(n, b):
                rows = x_rows[:, ds(b * ST, ST), :]
                for st in range(ST):
                    i = dve.bn_stats(bn[:, st, :], x_rows[:, ds(b * ST + st, 1), :].rearrange("p a d -> p (a d)"))
                link(i)
                dve.sem_inc(dve_seen, 1)
                for st in range(ST):
                    i = dve.bn_aggr(mv[:, st, :], bn[:, st, :])
                link(i)
                dve.tensor_scalar(var_eps[:, :], mv[:, :, 1], EPS_LN, None, ALU.add).then_inc(var_made, 1)
                dve.wait_ge(rows_stored, n * B + b + 1)
                dve.wait_ge(rows_T, n * B + b + 1 if n < 3 else 3 * B + 1)
                dve.wait_ge(rstd_made, rstds(n, b))
                for st in range(ST):
                    i = dve.tensor_scalar(norm_rows[:, st, :],
                                          x_rows[:, ds(b * ST + st, 1), :].rearrange("p a d -> p (a d)"), mv[:, st, 0:1],
                                          rstd[:, st:st + 1], ALU.subtract, ALU.mult)
                i.then_inc(rows_normed, 1)

            def rstds(n, b):
                return (b + 1) if n == 0 else (B + 2 * b + 1) if n == 1 else (n + 1) * B + b + 1

            def make_gate(n):
                for t in range(NT):
                    i = dve.max(top8[:, t, :], logits[:, t, :])
                link(i)
                for t in range(NT):
                    i = dve.max_index(top_i[:, t, :], top8[:, t, :], logits[:, t, :])
                link(i)
                dve.tensor_tensor(gate[:, :, :], logits[:, :, :], top8[:, :, 0:1].to_broadcast([P, NT, EX]),
                                  ALU.subtract).then_inc(shifted, 1)
                link(dve.tensor_copy(top_f[:, :, :], top_i[:, :, 0:2]))
                for k in range(2):
                    i = dve.tensor_tensor(hot[:, k, :, :], iota8[:, :].unsqueeze(1).to_broadcast([P, NT, EX]),
                                          top_f[:, :, k:k + 1].to_broadcast([P, NT, EX]), ALU.is_equal)
                link(i)
                link(dve.tensor_tensor(hot[:, 0, :, :], hot[:, 0, :, :], hot[:, 1, :, :], ALU.add))
                dve.wait_ge(gate_exp, n + 1)
                link(dve.tensor_tensor(gate[:, :, :], gate[:, :, :], hot[:, 0, :, :], ALU.mult))
                link(dve.tensor_reduce(out=gate_sum[:, :], in_=gate[:, :, :], axis=AX.X, op=ALU.add))
                link(dve.reciprocal(gate_sum[:, :], gate_sum[:, :]))
                dve.tensor_tensor(gate[:, :, :], gate[:, :, :], gate_sum[:, :].unsqueeze(2).to_broadcast([P, NT, EX]),
                                  ALU.mult).then_inc(gate_made, 1)
                dve.wait_ge(gate_made, n + 1)

            def mixture(m):
                with dve.Fori(0, EX // 2) as ep:
                    for j in range(MIX_UNITS):
                        slot, nb = divmod(j, B)
                        dve.wait_ge(m.y_done, ep * MIX_UNITS + j + 2)
                        dve.wait_ge(m.y_kept, ep * MIX_UNITS + max(j - 3, 0) + 2)
                        for st in range(ST):
                            i = nb * ST + st
                            y = dve.scalar_tensor_tensor(out=x_rows[:, i, :], in0=banks[4 + j % 2][:, st * D:(st + 1) * D],
                                                         scalar=gate[:, i, ds(ep * 2 + slot, 1)], in1=x_rows[:, i, :],
                                                         op0=ALU.mult, op1=ALU.add)
                        y.then_inc(m.y_kept, 1)

            dve.wait_ge(loaded, LOADS)
            for g in range(4):
                dve.wait_ge(qk_made, g + 1)
                dve.tensor_copy(qk_all[:, g * 512:(g + 1) * 512], banks[g][:, :]).then_inc(qk_kept, 1)
            for free in (proj_kept, y_kept):
                dve.sem_inc(free, 1)
            with dve.Fori(0, B) as b:
                with dve.Fori(0, HP) as p:
                    it = b * HP + p

                    def mask_max(u):
                        W = unit_width(u)
                        if u >= 2:
                            dve.wait_ge(exp_done, it * UNITS + (u - 1))
                        dve.wait_ge(scores_done, it * UNITS + (u + 2))
                        dve.sem_inc(dve_seen, 1)
                        dve.tensor_tensor_reduce(out=masked[:, u % 2, 0:W], in0=s_bank[u % 3][:, 0:W],
                                                 in1=mask[:, S - W:S], scale=-0.125, scalar=3.0e38, op0=ALU.add,
                                                 op1=ALU.min, accum_out=row_stats[:, u, 0:1]).then_inc(masked_done, 1)

                    def normalise(u):
                        W = unit_width(u)
                        dve.wait_ge(exp_done, it * UNITS + (u + 1))
                        dve.reciprocal(row_stats[:, u, 2:3], row_stats[:, u, 1:2]).then_inc(recip_done, 1)
                        dve.wait_ge(recip_done, it * UNITS + (u + 1))
                        dve.tensor_scalar(probs[:, u % 3, 0:W], probs[:, u % 3, 0:W], row_stats[:, u, 2:3], None,
                                          ALU.mult).then_inc(probs_done, 1)

                    for hh in range(2):
                        dve.wait_ge(proj_done, it * 3 + (hh + 2))
                        dve.tensor_copy(query[:, hh, :], proj_bank[:, :]).then_inc(proj_kept, 1)
                    dve.wait_ge(proj_done, it * 3 + 4)
                    dve.tensor_copy(flat(v_pair[:, :, :]), proj_bank[:, :]).then_inc(proj_kept, 1)
                    for u in range(UNITS + 1):
                        if u < UNITS:
                            mask_max(u)
                        if u >= 1:
                            normalise(u - 1)
                    dve.wait_ge(heads_done, it + 1)
                    dve.tensor_copy(headsT[:, :], pv_bank[:, :]).then_inc(heads_kept, 1)
                    dve.wait_ge(y_pair_done, it + 1)
                    dve.wait_ge(y_kept, it + 1)
                    dst = flat(x_rows[:, ds(b * ST, ST), :])
                    dve.tensor_tensor(dst, y_bank[:, :], dst, ALU.add).then_inc(y_kept, 1)
                dve.wait_ge(y_kept, (b + 1) * HP + 1)
                link.base, link.n = b * 2, 0
                norm_sequence(0, b)
                dve.wait_ge(logits_done, b + 2)
                dve.tensor_copy(logits[:, ds(b * ST, ST), :], pv_bank[:, 0:ST * EX].rearrange("p (a d) -> p a d", d=EX))\
                   .then_inc(logits_kept, 1)
            link.base, link.n = 2 * B, 0
            dve.wait_ge(logits_kept, B)
            make_gate(0)
            dve.wait_ge(rows_stored, B + 1)
            dve.sem_inc(mix1.y_kept, 2)
            mixture(mix1)
            dve.wait_ge(mix1.y_kept, EX * B + 2)
            base = 2 * B + link.n
            dve.memset(coef[:, :, :], 1.0)
            dve.memset(state[:, :, :], 1.0)
            dve.memset(tau[:, :], 1.0)
            dve.memset(mem[:, :, :], 0.0)
            link.base, link.n = base, 0
            link(dve.memset(junk4[:, :], 0.0))
            dve.memset(coef[:, :, 3:4], EPS_LN)
            link(dve.memset(state[:, 0, 2:3], 0.0))
            dve.wait_ge(mem_loaded, 7 * 16)
            link(dve.scalar_tensor_tensor(out=eta[:, :], in0=eta[:, :], scalar=-1.0, in1=eta[:, :], op0=ALU.mult, op1=ALU.max))
            dve.tensor_scalar(eta[:, :], eta[:, :], ETA_MIN, None, ALU.max).then_inc(eta_made, 1)
            dve.wait_ge(eta_made, 1)
            base = base + 3
            L1 = 17
            with dve.Fori(0, B) as b:
                link.base, link.n = base + b * L1, 0
                norm_sequence(1, b)
                dve.wait_ge(rows_normed, B + b + 1)
                for st in range(ST):
                    link(dve.tensor_tensor_reduce(out=junk[:, :], in0=norm_rows[:, st, :], in1=norm_rows[:, st, :],
                                                  scale=1.0, scalar=0.0, op0=ALU.mult, op1=ALU.add,
                                                  accum_out=ms[:, st:st + 1]))
                dve.tensor_scalar(var_eps[:, :], ms[:, :], 1.0 / D, EPS_RMS, ALU.mult, ALU.add).then_inc(rms_var, 1)
                dve.wait_ge(rstd_made, B + 2 * b + 2)
                for st in range(ST):
                    i = dve.tensor_scalar(rms_rows[:, st, :], norm_rows[:, st, :], rstd[:, st:st + 1], None, ALU.mult)
                i.then_inc(rms_normed, 1)
                dve.wait_ge(kv_done, b + 1)
                dve.tensor_scalar(flat(k_exp[:, :, :]), proj_bank[:, 0:ST * F], 0.0, None, ALU.min).then_inc(k_low, 1)
                dve.wait_ge(k_exped, 2 * b + 1)
                dve.wait_ge(kv_sent, b * 48 + 1)
                link(dve.scalar_tensor_tensor(out=flat(k_rows[:, :, :]), in0=proj_bank[:, 0:ST * F], scalar=0.0,
                                              in1=flat(k_exp[:, :, :]), op0=ALU.max, op1=ALU.add))
                dve.tensor_copy(flat(v_rows[:, :, :]), pv_bank[:, :])
                link(dve.tensor_tensor(g_rows[:, :, :], k_rows[:, :, :],
                                       eta[:, :].unsqueeze(1).to_broadcast([P, ST, F]), ALU.mult))
                for src, dst in ((g_rows, g_mv), (v_rows, v_mv)):
                    for st in range(ST):
                        i = dve.bn_stats(bn[:, st, :], src[:, st, :])
                    link(i)
                    dve.sem_inc(dve_seen, 1)
                    for st in range(ST):
                        i = dve.bn_aggr(dst[:, st, :], bn[:, st, :])
                    link(i)
                link(dve.tensor_tensor(cm_t[:, 0, :], v_mv[:, :, 0], v_mv[:, :, 0], ALU.mult))
                link(dve.tensor_tensor(cm_t[:, 0, :], cm_t[:, 0, :], v_mv[:, :, 1], ALU.add))
                link(dve.tensor_tensor(cm_t[:, 0, :], cm_t[:, 0, :], g_mv[:, :, 1], ALU.mult))
                link(dve.tensor_tensor(cm_t[:, 1, :], g_mv[:, :, 0], g_mv[:, :, 0], ALU.mult))
                link(dve.tensor_tensor(cm_t[:, 1, :], cm_t[:, 1, :], v_mv[:, :, 1], ALU.mult))
                dve.tensor_tensor(cm[:, :, 1], cm_t[:, 0, :], cm_t[:, 1, :], ALU.add)
                dve.tensor_tensor(cm[:, :, 0], g_mv[:, :, 0], v_mv[:, :, 0], ALU.mult).then_inc(kv_kept, 1)
                assert link.n == L1, link.n
                dve.wait_ge(q_done, b + 2)
                dve.tensor_scalar(q_exp[:, :], t_bank[0][0:F, :], 0.0, None, ALU.min).then_inc(k_low, 1)
                dve.wait_ge(k_exped, 2 * b + 2)
                dve.scalar_tensor_tensor(out=qT[:, ds(b * S, S)], in0=t_bank[0][0:F, :], scalar=0.0, in1=q_exp[:, :],
                                         op0=ALU.max, op1=ALU.add).then_inc(q_kept, 1)
            PER_HALF = 1 + 5 * CH + 3
            base = base + B * L1
            dve.sem_inc(rep_used, 2)
            dve.sem_inc(outer_used, 2)
            with dve.Fori(0, NCH // 2) as cp:
                link.base, link.n = base + cp * (2 * PER_HALF), 0
                for half in range(2):
                    n0 = cp * (2 * CH) + half * CH
                    dve.wait_ge(rep_in[half], cp * (3 * B * 16) + 3 * B * 16)
                    link(dve.tensor_copy(coef[:, :, 1], cm_rep[:, half, :, 1]))
                    for t in range(CH):
                        n = n0 + t
                        bank = banks[t % 2]
                        link(dve.tensor_tensor(prod[:, :, :], mem[:, :, :],
                                               k_rep[:, half, t, :].unsqueeze(1).to_broadcast([P, DD, F]), ALU.mult))
                        link(dve.tensor_reduce(out=pred[:, :], in_=prod[:, :, :], axis=AX.X, op=ALU.add))
                        dve.wait_ge(tau_made, n + 1)
                        link(dve.scalar_tensor_tensor(out=err[:, :], in0=v_rep[:, half, t, :], scalar=tau[:, t:t + 1],
                                                      in1=pred[:, :], op0=ALU.mult, op1=ALU.subtract))
                        dve.tensor_tensor_reduce(out=err2[:, :], in0=err[:, :], in1=err[:, :], scale=1.0, scalar=0.0,
                                                 op0=ALU.mult, op1=ALU.add, accum_out=sums[:, 0:1])
                        dve.wait_ge(outer_made, n + 1)
                        dve.tensor_tensor_reduce(out=prod2[:, :], in0=flat(mem[:, :, :]), in1=flat(outer[:, t % 2, :, :]),
                                                 scale=1.0, scalar=0.0, op0=ALU.mult, op1=ALU.add,
                                                 accum_out=sums[:, 1:2]).then_inc(sums_made, 1)
                        dve.wait_ge(w_made, n + 1)
                        dve.tensor_copy(state[:, t, 1:2], bank[:, 0:1])
                        link(dve.tensor_scalar(coef[:, t, 0:1], bank[:, 1:2], 2.0 / (F * D), None, ALU.mult))
                        dve.tensor_tensor_reduce(out=junk4[:, :], in0=state[:, t, :], in1=coef[:, t, :], scale=1.0,
                                                 scalar=0.0, op0=ALU.mult, op1=ALU.add,
                                                 accum_out=state[:, t + 1, 3:4]).then_inc(T_made, 1)
                        dve.scalar_tensor_tensor(out=mem[:, :, :], in0=outer[:, t % 2, :, :], scalar=state[:, t, 0:1],
                                                 in1=mem[:, :, :], op0=ALU.mult, op1=ALU.add).then_inc(outer_used, 1)
                        dve.wait_ge(T_made, n + 1)
                        link(dve.scalar_tensor_tensor(out=state[:, t + 1, 2:3], in0=state[:, t, 3:4], scalar=-EPS_LN,
                                                      in1=state[:, t + 1, 3:4], op0=ALU.mult, op1=ALU.add))
                    dve.wait_ge(tau_made, n0 + CH + 1)
                    link(dve.reciprocal(rho[:, 0:1], tau[:, CH:CH + 1]))
                    link(dve.tensor_tensor(rho[:, 1:2], rho[:, 0:1], rho[:, 0:1], ALU.mult))
                    dve.tensor_scalar(state[:, 0, 2:4], state[:, CH, 2:4], rho[:, 1:2], None, ALU.mult)
                    dve.tensor_scalar(tau[:, 0:1], tau[:, CH:CH + 1], rho[:, 0:1], None, ALU.mult)
                    link(dve.tensor_scalar(flat(mem[:, :, :]), flat(mem[:, :, :]), rho[:, 0:1], None, ALU.mult))
                    dve.sem_inc(rep_used, 1)
            assert link.n == 2 * PER_HALF
            base = base + (NCH // 2) * 2 * PER_HALF
            dve.wait_ge(rep_used, NCH + 2)
            dve.sem_inc(mem_done, 1)
            dve.wait_ge(mw_done, 1)
            dve.tensor_copy(flat(mw[:, :, :]), banks[4][0:F, :]).then_inc(mw_kept, 1)
            dve.wait_ge(rows_stored, 2 * B + 1)
            for b in range(B):
                dve.wait_ge(mo_done, b + 1)
                dst = flat(x_rows[:, b * ST:(b + 1) * ST, :])
                dve.scalar_tensor_tensor(out=dst, in0=dst, scalar=2.0, in1=banks[b][:, :], op0=ALU.mult,
                                         op1=ALU.add).then_inc(mo_kept, 1)
            dve.wait_ge(mo_kept, B)
            with dve.Fori(0, B) as b:
                link.base, link.n = base + b * 2, 0
                norm_sequence(2, b)
                dve.wait_ge(logits_done, B + b + 2)
                dve.tensor_tensor(logits[:, ds(b * ST, ST), :], pv_bank[:, 0:ST * EX].rearrange("p (a d) -> p a d", d=EX),
                                  rb2[:, :].unsqueeze(1).to_broadcast([P, ST, EX]), ALU.add).then_inc(logits_kept, 1)
            link.base, link.n = base + 2 * B, 0
            dve.wait_ge(logits_kept, 2 * B)
            make_gate(1)
            base = base + 2 * B + link.n
            dve.wait_ge(rows_stored, 3 * B + 1)
            with dve.Fori(0, B) as b:
                dve.wait_ge(be_done, b + 1)
                dst = flat(x_rows[:, ds(b * ST, ST), :])
                dve.scalar_tensor_tensor(out=dst, in0=dst, scalar=2.0, in1=pv_bank[:, :], op0=ALU.mult,
                                         op1=ALU.add).then_inc(be_kept, 1)
            dve.wait_ge(be_kept, B)
            dve.sem_inc(mix2.y_kept, 2)
            mixture(mix2)
            dve.wait_ge(mix2.y_kept, EX * B + 2)
            with dve.Fori(0, B) as b:
                link.base, link.n = base + b * 2, 0
                norm_sequence(3, b)

        @block.scalar
        def _(act):
            act.preload_act_table(ACT.Exp)
            with act.Fori(0, B) as b:
                with act.Fori(0, HP) as p:
                    it = b * HP + p

                    def exps(u):
                        W = unit_width(u)
                        act.wait_ge(masked_done, it * UNITS + (u + 1))
                        act.activation(probs[:, u % 3, 0:W], masked[:, u % 2, 0:W], ACT.Exp, bias=row_stats[:, u, 0:1],
                                       scale=-1.0, accum_out=row_stats[:, u, 1:2]).then_inc(exp_done, 1)

                    def keepT(u):
                        hh, qt = divmod(u, ST)
                        act.wait_ge(transposed, it * UNITS + (u + 1))
                        act.activation(probsT[:, hh, 0:qt + 1, qt * P:(qt + 1) * P],
                                       t_bank[u % 2][:, 0:unit_width(u)].rearrange("p (k q) -> p k q", q=P),
                                       ACT.Copy).then_inc(probsT_kept, 1)

                    for u in range(UNITS + 2):
                        if u < UNITS:
                            exps(u)
                        if u >= 2:
                            keepT(u - 2)
                act.wait_ge(xT_stored, b + 1)
                act.wait_ge(logits_done, b + 1)
                act.wait_ge(rows_T, b + 2)
                act.activation(seqT[:, :], y_bank[:, :], ACT.Copy).then_inc(seqT_kept, 1)
            act.wait_ge(shifted, 1)
            act.activation(gate[:, :, :], gate[:, :, :], ACT.Exp).then_inc(gate_exp, 1)

            def mixture(m):
                act.preload_act_table(m.func)
                act.sem_inc(m.h_kept, 4)
                with act.Fori(0, EX // 2) as ep:
                    for j in range(MIX_UNITS):
                        slot = j // B
                        for ft in range(m.tiles):
                            n = j * m.tiles + ft
                            if ft == 0:
                                act.wait_ge(m.y_done, ep * MIX_UNITS + max(j, 1))
                            act.wait_ge(m.h_done, ep * (MIX_UNITS * m.tiles) + n + 1)
                            if m is mix2:
                                act.sem_inc(act_seen, 1)
                                act.activation(hidden[:, j % 2, ft, :], banks[n % 4][:, :], m.func,
                                               bias=be1T[:, ds(ep * 2 + slot, 1), ft:ft + 1].rearrange("p a d -> p (a d)"))\
                                   .then_inc(m.h_kept, 1)
                            else:
                                act.activation(hidden[:, j % 2, ft, :], banks[n % 4][:, :], m.func).then_inc(m.h_kept, 1)

            mixture(mix1)
            act.wait_ge(mem_loaded, 7 * 16)
            act.preload_act_table(ACT.Exp)
            with act.Fori(0, B) as b:
                act.wait_ge(q_done, b + 1)
                act.wait_ge(rows_T, B + b + 2)
                act.activation(seqT[:, :], y_bank[:, :], ACT.Copy, scale=norm_w[:, 0:1]).then_inc(seqT_kept, 1)
                act.wait_ge(k_low, 2 * b + 1)
                act.activation(k_exp[:, :, :], k_exp[:, :, :], ACT.Exp).then_inc(k_exped, 1)
                act.wait_ge(k_low, 2 * b + 2)
                act.activation(q_exp[:, :], q_exp[:, :], ACT.Exp).then_inc(k_exped, 1)
            act.preload_act_table(ACT.Sqrt)
            act.sem_inc(tau_made, 1)
            with act.Fori(0, NCH // 2) as cp:
                for n in range(2 * CH):
                    t = n % CH
                    act.wait_ge(sums_out, cp * (2 * CH) + n + 1)
                    act.activation(state[:, t, 0:1], banks[t % 2][:, 0:1], ACT.Sqrt).then_inc(w_made, 1)
                    act.wait_ge(T_made, cp * (2 * CH) + n + 1)
                    act.activation(tau[:, t + 1:t + 2], state[:, t + 1, 3:4], ACT.Sqrt).then_inc(tau_made, 1)
            act.preload_act_table(ACT.Silu)
            act.wait_ge(d_loaded, 6 * 16)
            with act.Fori(0, B) as b:
                act.wait_ge(xT_stored, B + b + 1)
                act.wait_ge(logits_done, B + b + 1)
                act.wait_ge(rows_T, 2 * B + b + 2)
                act.activation(seqT[:, :], y_bank[:, :], ACT.Copy).then_inc(seqT_kept, 1)
                act.wait_ge(h1_done, b + 1)
                act.activation(h1T[:, :], proj_bank[:, :], ACT.Silu, bias=rb1[:, 0:1]).then_inc(h1_kept, 1)
            act.wait_ge(shifted, 2)
            act.activation(gate[:, :, :], gate[:, :, :], ACT.Exp).then_inc(gate_exp, 1)
            with act.Fori(0, B) as b:
                act.wait_ge(gateT_done, b + 2)
                act.activation(flat(gateT[:, :, :]), proj_bank[0:EX, :], ACT.Copy).then_inc(gateT_kept, 1)
            mixture(mix2)


_OUT = (128, 16, 128)


def kernel(**inputs):
    import numpy as np
    import concourse.bacc as bacc
    from concourse import mybir as mb
    from concourse.bass_utils import run_bass_kernel_spmd

    g = {k: np.asarray(v) for k, v in inputs.items()}
    P = 128
    x = g["L0_attn_x"].reshape(2048, P)
    laid = {
        "ident": np.eye(P, dtype=np.float32),
        "mask": np.concatenate([np.zeros((P, 3 * P), np.float32),
                                np.where(np.triu(np.ones((P, P), bool), 1), np.float32(-8e9), np.float32(0))], 1),
        "iota8": np.tile(np.arange(8, dtype=np.float32), (P, 1)),
        "blocks": np.kron(np.eye(4, dtype=np.float32), np.ones((32, 32), np.float32)),
        "xT": x.T,
        "x_rows": x.reshape(16, P, P).transpose(1, 0, 2),
        "wq": g["L0_attn_wq"].transpose(1, 0, 2),
        "wk": g["L0_attn_wk"].transpose(1, 0, 2),
        "wvT": g["L0_attn_wv"].reshape(1024, P).T,
        "woT": g["L0_attn_wo"].T.reshape(8, P, P).transpose(1, 0, 2),
        "wg": g["L0_ffn_Wg"],
        "W1": g["L0_ffn_W1"].transpose(1, 0, 2),
        "W2": g["L0_ffn_W2"].reshape(8, 2, P, P).transpose(2, 0, 1, 3),
        "wkT": g["L1_attn_Wk"].T,
        "wqT": g["L1_attn_Wq"].T,
        "wvT1": g["L1_attn_Wv"].T,
        "woutT": g["L1_attn_Wout"].T,
        "norm_w": g["L1_attn_norm_weight"].reshape(P, 1),
        "eta": np.tile(g["L1_attn_eta"], (P, 1)),
        "rw1": g["L1_ffn_rw1"],
        "rb1": g["L1_ffn_rb1"].reshape(P, 1),
        "rw2": g["L1_ffn_rw2"],
        "rb2": np.tile(g["L1_ffn_rb2"], (P, 1)),
        "we1": g["L1_ffn_we1"].transpose(1, 0, 2),
        "be1T": g["L1_ffn_be1"].reshape(8, 4, P).transpose(2, 0, 1),
        "we2": g["L1_ffn_we2"].reshape(8, 4, P, P).transpose(2, 0, 1, 3),
        "be2": g["L1_ffn_be2"],
    }
    nc = bacc.Bacc("TRN2", target_bir_lowering=False, num_devices=1)
    arrays, ins = {}, {}
    for name, a in laid.items():
        a = np.ascontiguousarray(a)
        arrays["in_" + name] = a
        ins[name] = nc.dram_tensor("in_" + name, a.shape, mb.dt.from_np(a.dtype), kind="ExternalInput").ap()
    scratch = {name: nc.dram_tensor("scratch_" + name, shape, mb.dt.float32, kind="Internal").ap()
               for name, shape in (("k", (2048, 64)), ("v", (2048, P)), ("cm", (2048, 2)), ("m", (512, 64)))}
    out = nc.dram_tensor("out_0", (P, 16, P), mb.dt.float32, kind="ExternalOutput").ap()
    seq_postln_kernel(nc, ins, out, scratch)
    r = run_bass_kernel_spmd(nc, [arrays], core_ids=[0])
    return np.asarray(r.results[0]["out_0"]).transpose(1, 0, 2).reshape(4, 512, P)
```

```python
import concourse.bass as bass
from concourse import mybir
from contextlib import ExitStack


def seq_postln_kernel(nc, ins, out, scratch):
    f32 = mybir.dt.float32
    u32 = mybir.dt.uint32
    ALU = mybir.AluOpType
    ACT = mybir.ActivationFunctionType
    AX = mybir.AxisListType
    ds = bass.ds

    B, S, D, H, E_DIM = 4, 512, 128, 16, 64
    P = 128
    ST = S // P
    NT = B * ST
    HP = H // 2
    UNITS = 2 * ST
    EX = 8
    F1, F2 = 256, 512
    F = 64
    EPS_LN, EPS_RMS, ETA_MIN = 1e-5, 1e-6, 1e-6
    CH = 16
    NCH = S // CH
    GC = CH + 2
    SC = CH + 4
    RHO_STEP = CH - 4
    START_TAU = 2.0 ** -13

    with ExitStack() as ctx:
        def sb(name, shape, dt=f32, scope=ctx):
            return scope.enter_context(nc.sbuf_tensor(name, shape, dt))

        def sem(name):
            return ctx.enter_context(nc.semaphore(name))

        ident = sb("ident", [P, P])
        x_rows = sb("x_rows", [P, NT, D])
        xT = sb("xT", [P, B * S])
        norm_rows = sb("norm_rows", [P, ST, D])
        seqT = sb("seqT", [P, S])
        bn = sb("bn", [P, ST, 6])
        mv = sb("mv", [P, ST, 2])
        var_eps = sb("var_eps", [P, ST])
        rstd = sb("rstd", [P, ST])
        neg_half = sb("neg_half", [P, ST])
        iota8 = sb("iota8", [P, EX])
        logits = sb("logits", [P, NT, EX])
        top8 = sb("top8", [P, NT, 8])
        top_i = sb("top_i", [P, NT, 8], u32)
        top_f = sb("top_f", [P, NT, 2])
        hot = sb("hot", [P, 2, NT, EX])
        gate = sb("gate", [P, NT, EX])
        gate_sum = sb("gate_sum", [P, NT])
        wg = sb("wg", [P, EX])
        w1 = sb("w1", [P, 2, F2])
        w2 = sb("w2", [P, 2, F2 // P, D])
        hidden = sb("hidden", [P, 2, F2 // P, S])

        with ExitStack() as A:
            mask = sb("mask", [P, S], scope=A)
            wq = sb("wq", [E_DIM, H, D], scope=A)
            wk = sb("wk", [E_DIM, H, D], scope=A)
            wvT = sb("wvT", [P, H * E_DIM], scope=A)
            woT = sb("woT", [P, HP, D], scope=A)
            qk_all = sb("qk_all", [P, H * D], scope=A)
            qk_pair = sb("qk_pair", [P, 2, D], scope=A)
            query = sb("query", [P, 2, S], scope=A)
            v_pair = sb("v_pair", [P, ST, P], scope=A)
            masked = sb("masked", [P, 2, S], scope=A)
            probs = sb("probs", [P, 3, S], scope=A)
            row_stats = sb("row_stats", [P, UNITS, 4], scope=A)
            probsT = sb("probsT", [P, 2, ST, S], scope=A)
            headsT = sb("headsT", [P, S], scope=A)
            xT_b = sb("xT_b", [P, S], scope=A)
        with ExitStack() as A:
            wkT = sb("wkT", [P, F], scope=A)
            wqT = sb("wqT", [P, F], scope=A)
            wvT1 = sb("wvT1", [P, D], scope=A)
            woutT = sb("woutT", [P, D], scope=A)
            norm_w = sb("norm_w", [P, 1], scope=A)
            eta = sb("eta", [P, F], scope=A)
            eta_col = sb("eta_col", [F, 1], scope=A)
            ones = sb("ones", [P, F], scope=A)
            col_scale = sb("col_scale", [P, 4], scope=A)
            rms_rows = sb("rms_rows", [P, ST, D], scope=A)
            ms = sb("ms", [P, ST], scope=A)
            junk = sb("junk", [P, D], scope=A)
            qT = sb("qT", [F, B * S], scope=A)
            q_exp = sb("q_exp", [F, 2, S], scope=A)
            k_exp = sb("k_exp", [P, ST, F], scope=A)
            k_rows = sb("k_rows", [P, ST, F], scope=A)
            g_rows = sb("g_rows", [P, ST, F], scope=A)
            gm_rows = sb("gm_rows", [P, ST, F], scope=A)
            v_rows = sb("v_rows", [P, ST, D], scope=A)
            vt_rows = sb("vt_rows", [P, ST, D], scope=A)
            g_mv = sb("g_mv", [P, ST, 2], scope=A)
            v_mv = sb("v_mv", [P, ST, 2], scope=A)
            means = sb("means", [P, ST, 3], scope=A)
            kg_b = sb("kg_b", [F, NCH, 2, CH], scope=A)
            vT_b = sb("vT_b", [P, S], scope=A)
            kg_all = sb("kg_all", [F, NCH, B, 2 * CH], scope=A)
            vT_all = sb("vT_all", [P, NCH, B, CH], scope=A)
            gram_kg = sb("gram_kg", [2 * CH, S], scope=A)
            gram_v = sb("gram_v", [CH, S], scope=A)
            tA, tG, tV, tVc, tH, tKg, tgg, tvv, tC, tB = (sb(n, [P, CH, CH], scope=A) for n in
                                                          "tA tG tV tVc tH tKg tgg tvv tC tB".split())
            tM = sb("tM", [P, CH, 3], scope=A)
            tZ = sb("tZ", [P, CH, CH, GC], scope=A)
            tmp_z = sb("tmp_z", [P, CH, CH, CH], scope=A)
            tR = sb("tR", [P, 2, CH, CH], scope=A)
            tVC = sb("tVC", [P, 2, CH], scope=A)
            zc = sb("zc", [B, 2, CH, CH, GC], scope=A)
            vc = sb("vc", [B, 2, 2, CH], scope=A)
            a_diag = sb("a_diag", [B * CH, 2, B, CH], scope=A)
            na = sb("na", [B * CH, 2, CH], scope=A)
            gg_rows = sb("gg_rows", [2 * CH, 2, B, F], scope=A)
            vv_rows = sb("vv_rows", [2 * CH, 2, B, D], scope=A)
            mem = sb("mem", [F, B, D], scope=A)
            prods = sb("prods", [P, 4, B, CH], scope=A)
            a_prod = sb("a_prod", [B * CH, B, CH], scope=A)
            a_sum = sb("a_sum", [B * CH, CH], scope=A)
            start = sb("start", [B * CH, SC], scope=A)
            spread = sb("spread", [B * CH, CH, SC], scope=A)
            of_step = sb("of_step", [B * CH, CH], scope=A)
            of_sequence = sb("of_sequence", [B * CH, B], scope=A)
            state = sb("state", [B, CH, SC], scope=A)
            tau, tau2, var_e, floor = (sb(n, [B, CH + 1], scope=A) for n in "tau tau2 var_e floor".split())
            var_m = sb("var_m", [B, 1], scope=A)
            y, w, w_sq, rest = (sb(n, [B, CH], scope=A) for n in "y w step_w2 rest".split())
            rho = sb("rho", [B, 2], scope=A)
            rho_diag = sb("rho_diag", [B, B], scope=A)
            rho_rep = sb("rho_rep", [F, B], scope=A)
            w_out = sb("w_out", [B, 2, CH], scope=A)
            w_rows = sb("w_rows", [2 * CH, B, F], scope=A)
            memT = sb("memT", [P, B, F], scope=A)
            mw = sb("mw", [F, B, D], scope=A)
        with ExitStack() as A:
            be1T = sb("be1T", [P, EX, F2 // P], scope=A)
            be2 = sb("be2", [EX, D], scope=A)
            gate_b = sb("gate_b", [P, ST, EX], scope=A)
            gateT = sb("gateT", [EX, ST, P], scope=A)
            h1T = sb("h1T", [P, S], scope=A)
            rw1 = sb("rw1", [P, D], scope=A)
            rw2 = sb("rw2", [P, EX], scope=A)
            rb1 = sb("rb1", [P, 1], scope=A)
            rb2 = sb("rb2", [P, EX], scope=A)

        banks = [ctx.enter_context(nc.psum_tensor(f"bank{i}", [P, 512], f32)) for i in range(8)]
        s_bank, t_bank = banks[0:3], banks[3:5]
        proj_bank, pv_bank, y_bank = banks[5], banks[6], banks[7]

        loaded, qk_made, qk_kept, seq_staged, pair_staged = map(sem, "loaded qk_made qk_kept seq_staged pair_staged".split())
        proj_done, proj_kept, scores_done, dve_seen, pool_seen, act_seen, masked_done = map(
            sem, "proj_done proj_kept scores_done dve_seen pool_seen act_seen masked_done".split())
        exp_done, recip_done, probs_done, transposed, probsT_kept = map(
            sem, "exp_done recip_done probs_done transposed probsT_kept".split())
        heads_done, heads_kept, y_pair_done, y_kept, chain = map(
            sem, "heads_done heads_kept y_pair_done y_kept chain".split())
        consts_set, var_made, rstd_made, rows_normed, rows_T, seqT_kept, xT_stored, rows_stored = map(
            sem, "consts_set var_made rstd_made rows_normed rows_T seqT_kept xT_stored rows_stored".split())
        logits_done, logits_kept, shifted, gate_exp, gate_made = map(
            sem, "logits_done logits_kept shifted gate_exp gate_made".split())
        mem_loaded, kv_done, k_low, k_exped, kv_kept, q_done, q_kept, kv_sent, T_kept, T_staged, gram_done, gram_kept = map(
            sem, "mem_loaded kv_done k_low k_exped kv_kept q_done q_kept kv_sent T_kept T_staged gram_done gram_kept".split())
        tabs_in, tabs_made, tabs_sent, rep_used, qn_done, prods_made, start_done, start_made, state_in = map(
            sem, "tabs_in tabs_made tabs_sent rep_used qn_done prods_made start_done start_made state_in".split())
        y_made, w2_made, w_made, T_made, tau_made, var_now, rho_made, rho_out, rho_kept, mem_scaled = map(
            sem, "y_made w2_made w_made T_made tau_made var_now rho_made rho_out rho_kept mem_scaled".split())
        pe_seen, w_scaled, wT_done, w_rows_made, mem_added, mem_made, mem_set, root_made, pool_steps = map(
            sem, "pe_seen w_scaled wT_done w_rows_made mem_added mem_made mem_set root_made pool_steps".split())
        rep_in = [sem("rep_in0"), sem("rep_in1")]
        memT_done, memT_kept, mw_done, mw_kept, mo_done, mo_kept = map(
            sem, "memT_done memT_kept mw_done mw_kept mo_done mo_kept".split())
        d_loaded, h1_done, h1_kept, gate_b_staged, gateT_done, gateT_kept, be_done, be_kept, stored, rms_var, rms_normed = map(
            sem, "d_loaded h1_done h1_kept gate_b_staged gateT_done gateT_kept be_done be_kept stored rms_var rms_normed".split())

        class Mixture:
            def __init__(self, n, width, func, w1_d, w2_d):
                self.tiles, self.func, self.w1_d, self.w2_d, self.width = width // P, func, w1_d, w2_d, width
                self.got = [sem(f"mix{n}_weights0"), sem(f"mix{n}_weights1")]
                self.h_done, self.h_kept = sem(f"mix{n}_h_done"), sem(f"mix{n}_h_kept")
                self.y_done, self.y_kept = sem(f"mix{n}_y_done"), sem(f"mix{n}_y_kept")

        mix1 = Mixture(1, F1, ACT.Relu, ins["W1"], ins["W2"])
        mix2 = Mixture(2, F2, ACT.Silu, ins["we1"], ins["we2"])
        MIX_UNITS = 2 * B
        FREE = B + 1

        def unit_width(u):
            return P * (u % ST + 1)

        def flat(ap):
            return ap.rearrange("p a d -> p (a d)")

        class Chain:
            def __init__(self, eng, counter):
                self.eng, self.counter, self.base, self.n = eng, counter, 0, 0

            def __call__(self, instruction):
                self.n += 1
                instruction.then_inc(self.counter, 1)
                self.eng.wait_ge(self.counter, self.base + self.n)

        LOADS = 10 * 16
        SENT = 6 * 16
        CHUNK_IN = (5 + 2 * B) * 16
        block = ctx.enter_context(nc.Block())

        @block.sync
        def _(sp):
            for dst, src in ((wq[:, :, :], "wq"), (wk[:, :, :], "wk"), (xT[:, :], "xT"), (ident[:, :], "ident"),
                             (mask[:, :], "mask"), (wvT[:, :], "wvT"), (woT[:, :, :], "woT"),
                             (x_rows[:, :, :], "x_rows"), (wg[:, :], "wg"), (iota8[:, :], "iota8")):
                sp.dma_start(dst, ins[src]).then_inc(loaded, 16)

            def mixture_weights(m):
                with sp.Fori(0, EX // 2) as ep:
                    for slot in range(2):
                        sp.wait_ge(m.y_done, ep * MIX_UNITS + (slot * B + 1))
                        sp.dma_start(w1[:, slot, 0:m.width],
                                     m.w1_d[:, ds(ep * 2 + slot, 1), :].rearrange("p e f -> p (e f)")).then_inc(m.got[slot], 16)
                        sp.dma_start(w2[:, slot, 0:m.tiles, :],
                                     m.w2_d[:, ds(ep * 2 + slot, 1), :, :].rearrange("p e a d -> p (e a) d")).then_inc(m.got[slot], 16)

            sp.sem_inc(mix1.y_done, FREE)
            mixture_weights(mix1)
            sp.wait_ge(mix1.y_done, EX * B + FREE)
            for dst, src in ((wkT[:, :], "wkT"), (wqT[:, :], "wqT"), (wvT1[:, :], "wvT1"), (woutT[:, :], "woutT"),
                             (norm_w[:, :], "norm_w"), (eta[:, :], "eta"), (eta_col[:, :], "eta_col")):
                sp.dma_start(dst, ins[src]).then_inc(mem_loaded, 16)
            sp.sem_inc(kv_sent, 1)
            with sp.Fori(0, B) as b:
                sp.wait_ge(kv_kept, b + 1)
                for dst, src in (("g", g_rows), ("gm", gm_rows), ("vt", vt_rows), ("means", means)):
                    sp.dma_start(scratch[dst][ds(b * S, S), :].rearrange("(s p) f -> p s f", p=P), src[:, :, :]).then_inc(kv_sent, 16)
                sp.wait_ge(gram_kept, b + 1)
                sp.dma_start(scratch["gram_kg"][ds(b, 1), :, :].rearrange("b u c -> (b u) c"), gram_kg[:, :]).then_inc(kv_sent, 16)
                sp.dma_start(scratch["gram_v"][ds(b, 1), :, :].rearrange("b u c -> (b u) c"), gram_v[:, :]).then_inc(kv_sent, 16)
            sp.wait_ge(kv_sent, B * SENT + 1)
            for b in range(B):
                rows = slice(b * NCH, (b + 1) * NCH)
                for dst, src, u0 in ((tA, "gram_kg", 0), (tG, "gram_kg", CH), (tV, "gram_v", 0)):
                    sp.dma_start(dst[rows, :, :], scratch[src][b, u0:u0 + CH, :].rearrange("u (c j) -> c u j", j=CH)).then_inc(tabs_in, 16)
            sp.dma_start(tM[:, :, :], scratch["means"].rearrange("(p j) s -> p j s", j=CH)).then_inc(tabs_in, 16)
            sp.wait_ge(tabs_made, 3)
            for dst, src in (("z", tZ[:, :, :, :].rearrange("p j u t -> p (j u t)")),
                             ("r", tR[:, :, :, :].rearrange("p a u j -> p (a u j)")),
                             ("vc", tVC[:, :, :].rearrange("p a u -> p (a u)"))):
                sp.dma_start(scratch[dst], src).then_inc(tabs_sent, 16)
            sp.wait_ge(tabs_sent, 3 * 16)
            with sp.Fori(0, NCH // 2) as cp:
                for half in range(2):
                    sp.wait_ge(rep_used, cp * 2 + (half + 1))
                    c = cp * 2 + half

                    def of_chunk(name):
                        a = scratch[name].rearrange("(b c) z -> c b z", b=B)[ds(c, 1), :, :]
                        return a.rearrange("c b z -> (c b) z")

                    sp.dma_start(zc[:, half, :, :, :].rearrange("p j u t -> p (j u t)"), of_chunk("z")).then_inc(rep_in[half], 16)
                    sp.dma_start(vc[:, half, :, :].rearrange("p a u -> p (a u)"), of_chunk("vc")).then_inc(rep_in[half], 16)
                    tables = scratch["r"].rearrange("(b c) (a u j) -> c b a u j", b=B, a=2, j=CH)
                    for b in range(B):
                        rows = slice(b * CH, (b + 1) * CH)
                        for a, dst in ((0, a_diag[rows, half, b, :]), (1, na[rows, half, :])):
                            sp.dma_start(dst, tables[ds(c, 1), b, a, :, :].rearrange("c u j -> (c u) j")).then_inc(rep_in[half], 16)
                    for dst, src in ((gg_rows[0:CH, half, :, :], "g"), (gg_rows[CH:2 * CH, half, :, :], "gm"),
                                     (vv_rows[0:CH, half, :, :], "vt")):
                        steps = scratch[src].rearrange("(b c j) f -> c j b f", b=B, j=CH)[ds(c, 1), :, :, :]
                        sp.dma_start(dst, steps.rearrange("c j b f -> (c j) b f")).then_inc(rep_in[half], 16)
            sp.wait_ge(mo_kept, B)
            for dst, src in ((be1T[:, :, :], "be1T"), (be2[:, :], "be2"), (rw1[:, :], "rw1"), (rw2[:, :], "rw2"),
                             (rb1[:, :], "rb1"), (rb2[:, :], "rb2")):
                sp.dma_start(dst, ins[src]).then_inc(d_loaded, 16)
            sp.sem_inc(mix2.y_done, FREE)
            mixture_weights(mix2)
            sp.wait_ge(rows_stored, 4 * B + 1)
            sp.dma_start(out, x_rows[:, :, :]).then_inc(stored, 16)
            sp.wait_ge(stored, 16)

        @block.gpsimd
        def _(pool):
            pool.memset(neg_half[:, :], -0.5).then_inc(consts_set, 1)
            pool.wait_ge(loaded, LOADS)
            pool.wait_ge(qk_kept, 4)
            pool.wait_ge(consts_set, 1)

            def norm_sequence(n, b, keep_T):
                pool.wait_ge(var_made, n * B + b + 1)
                pool.tensor_tensor(rstd[:, :], var_eps[:, :], neg_half[:, :], ALU.pow).then_inc(rstd_made, 1)
                pool.wait_ge(rows_normed, n * B + b + 1)
                pool.sem_inc(pool_seen, 1)
                pool.tensor_copy(x_rows[:, ds(b * ST, ST), :], norm_rows[:, :, :]).then_inc(rows_stored, 1)
                if keep_T is not None:
                    pool.wait_ge(seqT_kept, keep_T * B + b + 1)
                    pool.sem_inc(pool_seen, 1)
                    pool.tensor_copy(xT[:, ds(b * S, S)], seqT[:, :]).then_inc(xT_stored, 1)

            for free in (seq_staged, xT_stored, rows_stored, T_staged):
                pool.sem_inc(free, 1)
            with pool.Fori(0, B) as b:
                pool.wait_ge(scores_done, b * (HP * UNITS) + 1)
                pool.sem_inc(pool_seen, 1)
                pool.tensor_copy(xT_b[:, :], xT[:, ds(b * S, S)]).then_inc(seq_staged, 1)
                with pool.Fori(0, HP) as p:
                    pool.wait_ge(proj_done, (b * HP + p) * 3 + 1)
                    pool.sem_inc(pool_seen, 1)
                    pool.tensor_copy(flat(qk_pair[:, :, :]), qk_all[:, ds(p * (2 * D), 2 * D)]).then_inc(pair_staged, 1)
                norm_sequence(0, b, 0)
            with pool.Fori(0, B) as b:
                norm_sequence(1, b, None)
                pool.wait_ge(rms_var, b + 1)
                pool.tensor_tensor(rstd[:, :], var_eps[:, :], neg_half[:, :], ALU.pow).then_inc(rstd_made, 1)
                pool.wait_ge(T_kept, b + 1)
                pool.sem_inc(pool_seen, 1)
                pool.tensor_copy(kg_all[:, :, ds(b, 1), :].rearrange("p c b j -> p (c b) j"),
                                 kg_b[:, :, :, :].rearrange("p c a j -> p c (a j)"))
                pool.tensor_copy(vT_all[:, :, ds(b, 1), :].rearrange("p c b j -> p (c b) j"),
                                 vT_b[:, :].rearrange("p (c j) -> p c j", j=CH)).then_inc(T_staged, 1)
            pool.wait_ge(mem_set, 1)
            with pool.Fori(0, NCH // 2) as cp:
                for n in range(2 * CH):
                    t = n % CH
                    half = n // CH
                    col = slice(t, t + 1)
                    at = cp * (2 * CH) + n
                    pool.wait_ge(T_made, at + 1)
                    pool.sem_inc(pool_seen, 1)
                    pool.tensor_scalar(var_m[:, :], tau2[:, col], -EPS_LN, tau2[:, t + 1:t + 2], ALU.mult, ALU.add).then_inc(pool_steps, 1)
                    pool.wait_ge(pool_steps, at + 1)
                    pool.sem_inc(pool_seen, 1)
                    pool.tensor_scalar(var_e[:, t + 1:t + 2], tau2[:, t + 1:t + 2], EPS_LN, var_m[:, :], ALU.mult, ALU.add).then_inc(var_now, 1)
                    if t == RHO_STEP + 1:
                        pool.wait_ge(rho_kept, cp * 2 + n // CH + 1)
                        pool.tensor_tensor(mem[:, :, :], mem[:, :, :], rho_rep[:, :].unsqueeze(2).to_broadcast([F, B, D]),
                                           ALU.mult).then_inc(mem_scaled, 1)
            pool.wait_ge(rep_used, NCH + 2)
            pool.tensor_tensor(rho[:, 0:1], tau2[:, 0:1], neg_half[0:B, 0:1], ALU.pow).then_inc(root_made, 1)
            with pool.Fori(0, B) as b:
                norm_sequence(2, b, 2)
            with pool.Fori(0, B) as b:
                pool.wait_ge(gate_made, 2)
                pool.wait_ge(gateT_done, b + 1)
                pool.sem_inc(pool_seen, 1)
                pool.tensor_copy(gate_b[:, :, :], gate[:, ds(b * ST, ST), :]).then_inc(gate_b_staged, 1)
            with pool.Fori(0, B) as b:
                norm_sequence(3, b, None)

        @block.tensor
        def _(pe):
            def transpose_rows(src, bank, n, b):
                for st in range(ST):
                    t = pe.transpose(bank[:, st * P:(st + 1) * P], src[:, st, :], ident[:, :])
                t.then_inc(rows_T, 1)

            pe.wait_ge(loaded, LOADS)
            for g in range(4):
                for j in range(4):
                    h = 4 * g + j
                    m = pe.matmul(banks[g][:, j * D:(j + 1) * D], wq[:, h, :], wk[:, h, :], start=True, stop=True)
                m.then_inc(qk_made, 1)
            pe.wait_ge(qk_kept, 4)
            for free in (scores_done, proj_done, gateT_done, logits_done, rows_T, q_done, gram_done):
                pe.sem_inc(free, 1)
            with pe.Fori(0, B) as b:
                with pe.Fori(0, HP) as p:
                    it = b * HP + p
                    pe.wait_ge(seq_staged, b + 2)

                    def scores(u):
                        hh, qt = divmod(u, ST)
                        if u >= 3:
                            pe.wait_ge(masked_done, it * UNITS + (u - 2))
                        pe.matmul(s_bank[u % 3][:, 0:unit_width(u)], query[:, hh, qt * P:(qt + 1) * P],
                                  xT_b[:, 0:unit_width(u)], start=True, stop=True).then_inc(scores_done, 1)

                    def transposes(u):
                        pe.wait_ge(probs_done, it * UNITS + (u + 1))
                        if u >= 2:
                            pe.wait_ge(probsT_kept, it * UNITS + (u - 1))
                        for k in range(u % ST + 1):
                            t = pe.transpose(t_bank[u % 2][:, k * P:(k + 1) * P], probs[:, u % 3, k * P:(k + 1) * P],
                                             ident[:, :])
                        t.then_inc(transposed, 1)

                    pe.wait_ge(pair_staged, it + 1)
                    for hh in range(2):
                        pe.wait_ge(proj_kept, it * 3 + (hh + 1))
                        pe.matmul(proj_bank[:, :], qk_pair[:, hh, :], xT_b[:, :], start=True,
                                  stop=True).then_inc(proj_done, 1)
                    pe.wait_ge(proj_kept, it * 3 + 3)
                    for k in range(ST):
                        m = pe.matmul(proj_bank[:, k * P:(k + 1) * P], xT_b[:, k * P:(k + 1) * P],
                                      wvT[:, ds(p * P, P)], start=True, stop=True)
                    m.then_inc(proj_done, 1)
                    for u in range(UNITS + 2):
                        if u < UNITS:
                            scores(u)
                        if u >= 2:
                            transposes(u - 2)
                    pe.wait_ge(proj_kept, it * 3 + 4)
                    pe.wait_ge(probsT_kept, it * UNITS + UNITS)
                    for k in range(ST):
                        for hh in range(2):
                            m = pe.matmul(pv_bank[hh * 64:(hh + 1) * 64, k * P:S], v_pair[:, k, hh * 64:(hh + 1) * 64],
                                          probsT[:, hh, k, k * P:S], start=(k == 0), stop=(k == ST - 1))
                    m.then_inc(heads_done, 1)
                    pe.wait_ge(heads_kept, it + 1)
                    pe.wait_ge(y_kept, it + 1)
                    for st in range(ST):
                        m = pe.matmul(y_bank[:, st * D:(st + 1) * D], headsT[:, st * P:(st + 1) * P],
                                      woT[:, ds(p, 1), :].rearrange("p a d -> p (a d)"), start=True, stop=True)
                    m.then_inc(y_pair_done, 1)
                pe.wait_ge(rows_normed, b + 1)
                transpose_rows(norm_rows, y_bank, 0, b)
                pe.wait_ge(seqT_kept, b + 1)
                for st in range(ST):
                    m = pe.matmul(pv_bank[:, st * EX:(st + 1) * EX], seqT[:, st * P:(st + 1) * P], wg[:, :], start=True,
                                  stop=True)
                m.then_inc(logits_done, 1)
                pe.wait_ge(logits_kept, b + 1)

            def mixture(m):
                H_BANKS = 4
                with pe.Fori(0, EX // 2) as ep:
                    for j in range(MIX_UNITS + 1):
                        slot, nb = divmod(j, B)
                        if j < MIX_UNITS:
                            if nb == 0:
                                pe.wait_ge(m.got[slot], ep * 32 + 32)
                            for ft in range(m.tiles):
                                n = j * m.tiles + ft
                                pe.wait_ge(m.h_kept, ep * (MIX_UNITS * m.tiles) + n + 1)
                                pe.matmul(banks[n % H_BANKS][:, :], w1[:, slot, ft * P:(ft + 1) * P],
                                          xT[:, nb * S:(nb + 1) * S], start=True, stop=True).then_inc(m.h_done, 1)
                        if j >= 1:
                            slot = (j - 1) // B
                            pe.wait_ge(m.h_kept, ep * (MIX_UNITS * m.tiles) + (j * m.tiles + H_BANKS))
                            pe.wait_ge(m.y_kept, ep * MIX_UNITS + j)
                            for st in range(ST):
                                for ft in range(m.tiles):
                                    y = pe.matmul(banks[4 + (j - 1) % 2][:, st * D:(st + 1) * D],
                                                  hidden[:, (j - 1) % 2, ft, st * P:(st + 1) * P], w2[:, slot, ft, :],
                                                  start=(ft == 0), stop=(ft == m.tiles - 1))
                            y.then_inc(m.y_done, 1)

            pe.wait_ge(xT_stored, B + 1)
            mixture(mix1)
            pe.wait_ge(mem_loaded, 7 * 16)
            with pe.Fori(0, B) as b:
                pe.wait_ge(rms_normed, b + 1)
                transpose_rows(rms_rows, y_bank, 1, b)
                pe.wait_ge(seqT_kept, B + b + 1)
                for st in range(ST):
                    pe.matmul(proj_bank[:, st * F:(st + 1) * F], seqT[:, st * P:(st + 1) * P], wkT[:, :], start=True,
                              stop=True)
                for st in range(ST):
                    m = pe.matmul(pv_bank[:, st * D:(st + 1) * D], seqT[:, st * P:(st + 1) * P], wvT1[:, :], start=True,
                                  stop=True)
                m.then_inc(kv_done, 1)
                pe.matmul(t_bank[0][0:F, :], wqT[:, :], seqT[:, :], start=True, stop=True)
                pe.matmul(t_bank[1][0:F, :], wkT[:, :], seqT[:, :], start=True, stop=True)
                pe.matmul(banks[2][:, :], wvT1[:, :], seqT[:, :], start=True, stop=True).then_inc(q_done, 1)
                pe.wait_ge(T_kept, b + 1)
                pe.sem_inc(pe_seen, 1)
                for c in range(NCH):
                    steps = slice(c * CH, (c + 1) * CH)
                    pe.matmul(banks[0][0:2 * CH, steps], kg_b[:, c, :, :].rearrange("p a j -> p (a j)"), kg_b[:, c, 1, :],
                              start=True, stop=True)
                    m = pe.matmul(banks[1][0:CH, steps], vT_b[:, steps], vT_b[:, steps], start=True, stop=True)
                m.then_inc(gram_done, 1)
            pe.wait_ge(T_staged, B + 1)
            with pe.Fori(0, NCH // 2) as cp:
                for half in range(2):
                    c = cp * 2 + half
                    pe.wait_ge(mem_made, c + 1)
                    for b in range(B):
                        m = pe.matmul(banks[0][:, b * 2 * CH:(b + 1) * 2 * CH], mem[:, b, :],
                                      kg_all[:, ds(c, 1), b, :].rearrange("p c j -> p (c j)"), start=True, stop=True)
                    m.then_inc(qn_done, 1)
                    pe.wait_ge(prods_made, c + 1)
                    pe.matmul(banks[1][0:B * CH, 0:B * CH], prods[:, 0, :, :].rearrange("p b j -> p (b j)"),
                              vT_all[:, ds(c, 1), :, :].rearrange("p c b j -> p (c b j)"), start=True, stop=True)
                    for i in range(4):
                        m = pe.matmul(banks[1][0:B * CH, B * CH + i:B * CH + i + 1],
                                      prods[:, (i + 1) % 4, :, :].rearrange("p b j -> p (b j)"), col_scale[:, i:i + 1],
                                      start=True, stop=True)
                    m.then_inc(start_done, 1)
                    pe.wait_ge(start_made, c + 1)
                    pe.sem_inc(pe_seen, 1)
                    pe.matmul(banks[5][0:B, 0:CH * SC], of_sequence[:, :], spread[:, :, :].rearrange("p u s -> p (u s)"),
                              start=True, stop=True).then_inc(state_in, 1)
                    pe.wait_ge(rho_made, c + 1)
                    pe.sem_inc(pe_seen, 1)
                    pe.matmul(banks[2][0:F, 0:B], ones[0:B, :], rho_diag[:, :], start=True, stop=True).then_inc(rho_out, 1)
                    pe.wait_ge(w_scaled, c + 1)
                    pe.sem_inc(pe_seen, 1)
                    pe.transpose(banks[3][0:2 * CH, 0:B], w_out[:, :, :].rearrange("p a j -> p (a j)"),
                                 ident[0:B, 0:B]).then_inc(wT_done, 1)
                    pe.wait_ge(w_rows_made, c + 1)
                    pe.sem_inc(pe_seen, 1)
                    for b in range(B):
                        m = pe.matmul(banks[4][0:F, b * D:(b + 1) * D], w_rows[:, b, :], vv_rows[:, half, b, :], start=True,
                                      stop=True)
                    m.then_inc(mem_added, 1)
            pe.wait_ge(rho_made, NCH + 1)
            pe.matmul(banks[2][0:F, 0:B], ones[0:B, :], rho_diag[:, :], start=True, stop=True).then_inc(rho_out, 1)
            for b in range(B):
                m = pe.transpose(banks[5][:, b * F:(b + 1) * F], mem[:, b, :], ident[0:F, 0:F])
            m.then_inc(memT_done, 1)
            pe.wait_ge(memT_kept, 1)
            for b in range(B):
                m = pe.matmul(banks[4][0:F, b * D:(b + 1) * D], memT[:, b, :], woutT[:, :], start=True, stop=True)
            m.then_inc(mw_done, 1)
            pe.wait_ge(mw_kept, 1)
            pe.wait_ge(q_kept, B)
            for b in range(B):
                for st in range(ST):
                    i = b * ST + st
                    m = pe.matmul(banks[b][:, st * D:(st + 1) * D], qT[:, i * P:(i + 1) * P], mw[:, b, :], start=True,
                                  stop=True)
                m.then_inc(mo_done, 1)
            pe.wait_ge(d_loaded, 6 * 16)
            with pe.Fori(0, B) as b:
                pe.wait_ge(rows_normed, 2 * B + b + 1)
                transpose_rows(norm_rows, y_bank, 2, b)
                pe.wait_ge(seqT_kept, 2 * B + b + 1)
                pe.matmul(proj_bank[:, :], rw1[:, :], seqT[:, :], start=True, stop=True).then_inc(h1_done, 1)
                pe.wait_ge(h1_kept, b + 1)
                for st in range(ST):
                    m = pe.matmul(pv_bank[:, st * EX:(st + 1) * EX], h1T[:, st * P:(st + 1) * P], rw2[:, :], start=True,
                                  stop=True)
                m.then_inc(logits_done, 1)
                pe.wait_ge(logits_kept, B + b + 1)
            with pe.Fori(0, B) as b:
                pe.wait_ge(gate_b_staged, b + 1)
                for st in range(ST):
                    m = pe.transpose(proj_bank[0:EX, st * P:(st + 1) * P], gate_b[:, st, :], ident[:, :])
                m.then_inc(gateT_done, 1)
                pe.wait_ge(gateT_kept, b + 1)
                for st in range(ST):
                    m = pe.matmul(pv_bank[:, st * D:(st + 1) * D], gateT[:, st, :], be2[:, :], start=True, stop=True)
                m.then_inc(be_done, 1)
                pe.wait_ge(be_kept, b + 1)
            pe.wait_ge(xT_stored, 2 * B + 1)
            mixture(mix2)

        @block.vector
        def _(dve):
            link = Chain(dve, chain)

            def norm_sequence(n, b):
                rows = x_rows[:, ds(b * ST, ST), :]
                for st in range(ST):
                    i = dve.bn_stats(bn[:, st, :], x_rows[:, ds(b * ST + st, 1), :].rearrange("p a d -> p (a d)"))
                link(i)
                dve.sem_inc(dve_seen, 1)
                for st in range(ST):
                    i = dve.bn_aggr(mv[:, st, :], bn[:, st, :])
                link(i)
                dve.tensor_scalar(var_eps[:, :], mv[:, :, 1], EPS_LN, None, ALU.add).then_inc(var_made, 1)
                dve.wait_ge(rows_stored, n * B + b + 1)
                dve.wait_ge(rows_T, n * B + b + 1 if n < 3 else 3 * B + 1)
                dve.wait_ge(rstd_made, rstds(n, b))
                for st in range(ST):
                    i = dve.tensor_scalar(norm_rows[:, st, :],
                                          x_rows[:, ds(b * ST + st, 1), :].rearrange("p a d -> p (a d)"), mv[:, st, 0:1],
                                          rstd[:, st:st + 1], ALU.subtract, ALU.mult)
                i.then_inc(rows_normed, 1)

            def rstds(n, b):
                return (b + 1) if n == 0 else (B + 2 * b + 1) if n == 1 else (n + 1) * B + b + 1

            def make_gate(n):
                for t in range(NT):
                    i = dve.max(top8[:, t, :], logits[:, t, :])
                link(i)
                for t in range(NT):
                    i = dve.max_index(top_i[:, t, :], top8[:, t, :], logits[:, t, :])
                link(i)
                dve.tensor_tensor(gate[:, :, :], logits[:, :, :], top8[:, :, 0:1].to_broadcast([P, NT, EX]),
                                  ALU.subtract).then_inc(shifted, 1)
                link(dve.tensor_copy(top_f[:, :, :], top_i[:, :, 0:2]))
                for k in range(2):
                    i = dve.tensor_tensor(hot[:, k, :, :], iota8[:, :].unsqueeze(1).to_broadcast([P, NT, EX]),
                                          top_f[:, :, k:k + 1].to_broadcast([P, NT, EX]), ALU.is_equal)
                link(i)
                link(dve.tensor_tensor(hot[:, 0, :, :], hot[:, 0, :, :], hot[:, 1, :, :], ALU.add))
                dve.wait_ge(gate_exp, n + 1)
                link(dve.tensor_tensor(gate[:, :, :], gate[:, :, :], hot[:, 0, :, :], ALU.mult))
                link(dve.tensor_reduce(out=gate_sum[:, :], in_=gate[:, :, :], axis=AX.X, op=ALU.add))
                link(dve.reciprocal(gate_sum[:, :], gate_sum[:, :]))
                dve.tensor_tensor(gate[:, :, :], gate[:, :, :], gate_sum[:, :].unsqueeze(2).to_broadcast([P, NT, EX]),
                                  ALU.mult).then_inc(gate_made, 1)
                dve.wait_ge(gate_made, n + 1)

            def mixture(m):
                with dve.Fori(0, EX // 2) as ep:
                    for j in range(MIX_UNITS):
                        slot, nb = divmod(j, B)
                        dve.wait_ge(m.y_done, ep * MIX_UNITS + j + FREE + 1)
                        dve.wait_ge(m.y_kept, ep * MIX_UNITS + max(j - 3, 0) + 2)
                        for st in range(ST):
                            i = nb * ST + st
                            y = dve.scalar_tensor_tensor(out=x_rows[:, i, :], in0=banks[4 + j % 2][:, st * D:(st + 1) * D],
                                                         scalar=gate[:, i, ds(ep * 2 + slot, 1)], in1=x_rows[:, i, :],
                                                         op0=ALU.mult, op1=ALU.add)
                        y.then_inc(m.y_kept, 1)

            dve.wait_ge(loaded, LOADS)
            for g in range(4):
                dve.wait_ge(qk_made, g + 1)
                dve.tensor_copy(qk_all[:, g * 512:(g + 1) * 512], banks[g][:, :]).then_inc(qk_kept, 1)
            for free in (proj_kept, y_kept):
                dve.sem_inc(free, 1)
            with dve.Fori(0, B) as b:
                with dve.Fori(0, HP) as p:
                    it = b * HP + p

                    def mask_max(u):
                        W = unit_width(u)
                        if u >= 2:
                            dve.wait_ge(exp_done, it * UNITS + (u - 1))
                        dve.wait_ge(scores_done, it * UNITS + (u + 2))
                        dve.sem_inc(dve_seen, 1)
                        dve.tensor_tensor_reduce(out=masked[:, u % 2, 0:W], in0=s_bank[u % 3][:, 0:W],
                                                 in1=mask[:, S - W:S], scale=-0.125, scalar=3.0e38, op0=ALU.add,
                                                 op1=ALU.min, accum_out=row_stats[:, u, 0:1]).then_inc(masked_done, 1)

                    def normalise(u):
                        W = unit_width(u)
                        dve.wait_ge(exp_done, it * UNITS + (u + 1))
                        dve.reciprocal(row_stats[:, u, 2:3], row_stats[:, u, 1:2]).then_inc(recip_done, 1)
                        dve.wait_ge(recip_done, it * UNITS + (u + 1))
                        dve.tensor_scalar(probs[:, u % 3, 0:W], probs[:, u % 3, 0:W], row_stats[:, u, 2:3], None,
                                          ALU.mult).then_inc(probs_done, 1)

                    for hh in range(2):
                        dve.wait_ge(proj_done, it * 3 + (hh + 2))
                        dve.tensor_copy(query[:, hh, :], proj_bank[:, :]).then_inc(proj_kept, 1)
                    dve.wait_ge(proj_done, it * 3 + 4)
                    dve.tensor_copy(flat(v_pair[:, :, :]), proj_bank[:, :]).then_inc(proj_kept, 1)
                    for u in range(UNITS + 1):
                        if u < UNITS:
                            mask_max(u)
                        if u >= 1:
                            normalise(u - 1)
                    dve.wait_ge(heads_done, it + 1)
                    dve.tensor_copy(headsT[:, :], pv_bank[:, :]).then_inc(heads_kept, 1)
                    dve.wait_ge(y_pair_done, it + 1)
                    dve.wait_ge(y_kept, it + 1)
                    dst = flat(x_rows[:, ds(b * ST, ST), :])
                    dve.tensor_tensor(dst, y_bank[:, :], dst, ALU.add).then_inc(y_kept, 1)
                dve.wait_ge(y_kept, (b + 1) * HP + 1)
                link.base, link.n = b * 2, 0
                norm_sequence(0, b)
                dve.wait_ge(logits_done, b + 2)
                dve.tensor_copy(logits[:, ds(b * ST, ST), :], pv_bank[:, 0:ST * EX].rearrange("p (a d) -> p a d", d=EX))\
                   .then_inc(logits_kept, 1)
            link.base, link.n = 2 * B, 0
            dve.wait_ge(logits_kept, B)
            make_gate(0)
            dve.wait_ge(rows_stored, B + 1)
            dve.sem_inc(mix1.y_kept, 2)
            mixture(mix1)
            dve.wait_ge(mix1.y_kept, EX * B + 2)
            base = 2 * B + link.n
            for dst, value in ((ones, 1.0), (vv_rows, 1.0), (a_diag, 0.0), (mem, 0.0), (tau, 1.0), (tau2, 1.0), (var_e, EPS_LN)):
                dve.memset(dst[(slice(None),) * len(dst.shape)], value)
            for i, value in enumerate((-2.0, 2.0 / (F * D), -1.0, 1.0)):
                m = dve.memset(col_scale[:, i:i + 1], value)
            m.then_inc(mem_set, 1)
            dve.wait_ge(mem_set, 1)
            link.base, link.n = base, 0
            dve.wait_ge(mem_loaded, 7 * 16)
            link(dve.scalar_tensor_tensor(out=eta[:, :], in0=eta[:, :], scalar=-1.0, in1=eta[:, :], op0=ALU.mult, op1=ALU.max))
            link(dve.scalar_tensor_tensor(out=eta_col[:, :], in0=eta_col[:, :], scalar=-1.0, in1=eta_col[:, :], op0=ALU.mult, op1=ALU.max))
            link(dve.tensor_scalar(eta_col[:, :], eta_col[:, :], ETA_MIN, None, ALU.max))
            link(dve.tensor_scalar(eta[:, :], eta[:, :], ETA_MIN, None, ALU.max))
            base = base + link.n
            L1 = 13
            with dve.Fori(0, B) as b:
                link.base, link.n = base + b * L1, 0
                norm_sequence(1, b)
                dve.wait_ge(rows_normed, B + b + 1)
                for st in range(ST):
                    link(dve.tensor_tensor_reduce(out=junk[:, :], in0=norm_rows[:, st, :], in1=norm_rows[:, st, :],
                                                  scale=1.0, scalar=0.0, op0=ALU.mult, op1=ALU.add,
                                                  accum_out=ms[:, st:st + 1]))
                dve.tensor_scalar(var_eps[:, :], ms[:, :], 1.0 / D, EPS_RMS, ALU.mult, ALU.add).then_inc(rms_var, 1)
                dve.wait_ge(rstd_made, B + 2 * b + 2)
                for st in range(ST):
                    i = dve.tensor_scalar(rms_rows[:, st, :], norm_rows[:, st, :], rstd[:, st:st + 1], None, ALU.mult)
                i.then_inc(rms_normed, 1)
                dve.wait_ge(kv_done, b + 1)
                dve.tensor_scalar(flat(k_exp[:, :, :]), proj_bank[:, 0:ST * F], 0.0, None, ALU.min).then_inc(k_low, 1)
                dve.wait_ge(k_exped, 2 * b + 1)
                dve.wait_ge(kv_sent, b * SENT + 1)
                link(dve.scalar_tensor_tensor(out=flat(k_rows[:, :, :]), in0=proj_bank[:, 0:ST * F], scalar=0.0,
                                              in1=flat(k_exp[:, :, :]), op0=ALU.max, op1=ALU.add))
                dve.tensor_copy(flat(v_rows[:, :, :]), pv_bank[:, :])
                dve.wait_ge(q_done, b + 2)
                dve.tensor_scalar(q_exp[:, 0, :], t_bank[0][0:F, :], 0.0, None, ALU.min)
                dve.tensor_scalar(q_exp[:, 1, :], t_bank[1][0:F, :], 0.0, None, ALU.min).then_inc(k_low, 1)
                dve.wait_ge(T_staged, b + 1)
                dve.wait_ge(gram_done, b + 1)
                dve.sem_inc(dve_seen, 1)
                dve.tensor_copy(vT_b[:, :], banks[2][:, :])
                dve.tensor_tensor(g_rows[:, :, :], k_rows[:, :, :],
                                  eta[:, :].unsqueeze(1).to_broadcast([P, ST, F]), ALU.mult)
                link(dve.tensor_reduce(out=means[:, :, 0], in_=k_rows[:, :, :], axis=AX.X, op=ALU.add))
                dve.wait_ge(k_exped, 2 * b + 2)
                dve.scalar_tensor_tensor(out=qT[:, ds(b * S, S)], in0=t_bank[0][0:F, :], scalar=0.0, in1=q_exp[:, 0, :],
                                         op0=ALU.max, op1=ALU.add).then_inc(q_kept, 1)
                link(dve.scalar_tensor_tensor(out=kg_b[:, :, 0, :], in0=t_bank[1][0:F, :].rearrange("p (c j) -> p c j", j=CH),
                                              scalar=0.0, in1=q_exp[:, 1, :].rearrange("p (c j) -> p c j", j=CH),
                                              op0=ALU.max, op1=ALU.add))
                dve.tensor_scalar(kg_b[:, :, 1, :], kg_b[:, :, 0, :], eta_col[:, 0:1], None, ALU.mult).then_inc(T_kept, 1)
                for src, dst in ((g_rows, g_mv), (v_rows, v_mv)):
                    for st in range(ST):
                        i = dve.bn_stats(bn[:, st, :], src[:, st, :])
                    link(i)
                    dve.sem_inc(dve_seen, 1)
                    for st in range(ST):
                        i = dve.bn_aggr(dst[:, st, :], bn[:, st, :])
                    link(i)
                for st in range(ST):
                    dve.tensor_scalar(gm_rows[:, st, :], g_rows[:, st, :], g_mv[:, st, 0:1], v_mv[:, st, 0:1], ALU.subtract,
                                      ALU.mult)
                    dve.tensor_scalar(vt_rows[:, st, :], v_rows[:, st, :], v_mv[:, st, 0:1], None, ALU.subtract)
                dve.tensor_copy(means[:, :, 1], g_mv[:, :, 0])
                dve.tensor_copy(means[:, :, 2], v_mv[:, :, 0]).then_inc(kv_kept, 1)
                dve.wait_ge(gram_done, b + 2)
                dve.tensor_copy(gram_kg[:, :], banks[0][0:2 * CH, :])
                dve.tensor_copy(gram_v[:, :], banks[1][0:CH, :]).then_inc(gram_kept, 1)
                assert link.n == L1, link.n
            base = base + B * L1

            link.base, link.n = base, 0
            dve.wait_ge(tabs_in, (3 * B + 1) * 16)

            def by_u(ap):
                return ap.unsqueeze(2).to_broadcast([P, CH, CH])

            def by_j(ap):
                return ap.unsqueeze(1).to_broadcast([P, CH, CH])

            def tt(out, a, c, op):
                return dve.tensor_tensor(out, a, c, op)

            def stt(out, a, scalar, c, op0, op1):
                return dve.scalar_tensor_tensor(out=out, in0=a, scalar=scalar, in1=c, op0=op0, op1=op1)

            k_sum, g_mean, v_mean = (tM[:, :, i] for i in range(3))
            root_D = float(D) ** 0.5
            tt(tKg[:, :, :], by_u(k_sum), by_j(g_mean), ALU.mult)
            tt(tgg[:, :, :], by_u(g_mean), by_j(g_mean), ALU.mult)
            link(tt(tvv[:, :, :], by_u(v_mean), by_j(v_mean), ALU.mult))
            stt(tVc[:, :, :], tvv[:, :, :], -float(D), tV[:, :, :], ALU.mult, ALU.add)
            link(tt(tH[:, :, :], tA[:, :, :], tKg[:, :, :], ALU.subtract))
            stt(tH[:, :, :], tH[:, :, :], root_D, by_j(v_mean), ALU.mult, ALU.mult)
            stt(tR[:, 1, :, :], tKg[:, :, :], 2.0, by_j(v_mean), ALU.mult, ALU.mult)
            dve.tensor_scalar(tR[:, 0, :, :], tA[:, :, :], -2.0, None, ALU.mult)
            link(stt(tG[:, :, :], tgg[:, :, :], -float(F), tG[:, :, :], ALU.mult, ALU.add))
            dve.tensor_scalar(tKg[:, :, :], tH[:, :, :], -2.0, None, ALU.mult)
            tt(tC[:, :, :], tA[:, :, :], tVc[:, :, :], ALU.mult)
            tt(tG[:, :, :], tG[:, :, :], tV[:, :, :], ALU.mult)
            stt(tgg[:, :, :], tgg[:, :, :], float(F), tVc[:, :, :], ALU.mult, ALU.mult)
            link(stt(tB[:, :, :], tH[:, :, :], root_D, by_u(v_mean), ALU.mult, ALU.mult))
            link(tt(tC[:, :, :], tC[:, :, :], tB[:, :, :], ALU.add))
            link(tt(tB[:, :, :], tG[:, :, :], tgg[:, :, :], ALU.add))
            dve.tensor_scalar(tZ[:, :, :, CH].rearrange("p j u -> p u j"), tC[:, :, :], -2.0, None, ALU.mult)
            link(dve.tensor_scalar(tZ[:, :, :, CH + 1].rearrange("p j u -> p u j"), tB[:, :, :], 2.0 / (F * D), None, ALU.mult))

            def diagonal(ap):
                return ap[:, 0:CH * CH:CH + 1]

            dve.tensor_scalar(tVC[:, 0, :], diagonal(flat(tV[:, :, :])), -1.0, None, ALU.mult)
            dve.tensor_scalar(tVC[:, 1, :], diagonal(flat(tB[:, :, :])), 1.0 / (F * D), None, ALU.mult).then_inc(tabs_made, 1)
            CUBE = [P, CH, CH, CH]
            tt(tmp_z[:, :, :, :], tR[:, 0, :, :].rearrange("p u j -> p j u").unsqueeze(3).to_broadcast(CUBE),
               tA[:, :, :].unsqueeze(1).to_broadcast(CUBE), ALU.mult)
            link(tt(tZ[:, :, :, 0:CH], tKg[:, :, :].rearrange("p u j -> p j u").unsqueeze(3).to_broadcast(CUBE),
                    tH[:, :, :].unsqueeze(1).to_broadcast(CUBE), ALU.mult))
            link(tt(tmp_z[:, :, :, :], tmp_z[:, :, :, :], tVc[:, :, :].unsqueeze(2).to_broadcast(CUBE), ALU.mult))
            link(tt(tZ[:, :, :, 0:CH], tZ[:, :, :, 0:CH], tmp_z[:, :, :, :], ALU.add))
            for j in range(CH):
                i = dve.tensor_scalar(tZ[:, j, :, j], tZ[:, j, :, j], 0.5, None, ALU.mult)
            i.then_inc(tabs_made, 1)
            dve.wait_ge(tabs_made, 2)
            dve.sem_inc(tabs_made, 1)
            base = base + link.n

            both = ident[0:B * CH, 0:B * CH]
            dve.tensor_reduce(out=of_step[:, :], in_=both.rearrange("p (b u) -> p u b", b=B), axis=AX.X, op=ALU.add)
            dve.tensor_reduce(out=of_sequence[:, :], in_=both.rearrange("p (b u) -> p b u", b=B), axis=AX.X,
                              op=ALU.add).then_inc(mem_set, 1)
            dve.wait_ge(mem_set, 2)

            dve.wait_ge(T_staged, B + 1)
            PER_HALF = 6 + 5 * (CH - 1) + 1 + 3 + 1
            dve.sem_inc(rep_used, 2)
            dve.sem_inc(mem_made, 1)
            dve.sem_inc(tau_made, 1)
            dve.sem_inc(var_now, 1)
            with dve.Fori(0, NCH // 2) as cp:
                for half in range(2):
                    link.base, link.n = base + cp * (2 * PER_HALF) + half * PER_HALF, 0
                    c = cp * 2 + half
                    n0 = cp * (2 * CH) + half * CH
                    dve.wait_ge(qn_done, c + 1)
                    dve.sem_inc(dve_seen, 1)
                    qh = banks[0][:, 0:B * 2 * CH].rearrange("p (b a j) -> p b a j", a=2, j=CH)
                    v_now = vT_all[:, ds(c, 1), :, :].rearrange("p c b j -> p (c b) j")
                    tt(prods[:, 1, :, :], qh[:, :, 0, :], v_now, ALU.mult)
                    tt(prods[:, 2, :, :], qh[:, :, 1, :], v_now, ALU.mult)
                    link(dve.tensor_copy(prods[:, 0, :, :], qh[:, :, 0, :]))
                    tt(prods[:, 3, :, :], prods[:, 0, :, :], prods[:, 0, :, :], ALU.mult).then_inc(prods_made, 1)
                    dve.wait_ge(rep_in[half], cp * CHUNK_IN + CHUNK_IN)
                    dve.wait_ge(start_done, c + 1)
                    dve.sem_inc(dve_seen, 1)
                    dve.tensor_copy(start[:, CH:SC], banks[1][0:B * CH, B * CH:B * CH + 4])
                    link(tt(flat(a_prod[:, :, :]), banks[1][0:B * CH, 0:B * CH], flat(a_diag[:, half, :, :]), ALU.mult))
                    link(dve.tensor_reduce(out=a_sum[:, :], in_=a_prod[:, :, :].rearrange("p b j -> p j b"), axis=AX.X,
                                           op=ALU.add))
                    link(stt(start[:, 0:CH], na[:, half, :], start[:, SC - 1:SC], a_sum[:, :], ALU.mult, ALU.add))
                    tt(spread[:, :, :], start[:, :].unsqueeze(1).to_broadcast([B * CH, CH, SC]),
                       of_step[:, :].unsqueeze(2).to_broadcast([B * CH, CH, SC]), ALU.mult).then_inc(start_made, 1)
                    dve.wait_ge(state_in, c + 1)
                    dve.sem_inc(dve_seen, 1)
                    link(dve.tensor_copy(state[:, :, :].rearrange("p u s -> p (u s)"), banks[5][0:B, 0:CH * SC]))
                    link(stt(floor[:, 0:1], vc[:, half, 0, 0:1], tau2[:, 0:1], state[:, 0, CH + 2:CH + 3], ALU.mult, ALU.add))
                    for j in range(CH):
                        n = n0 + j
                        later = slice(j + 1, CH)
                        col = slice(j, j + 1)
                        dve.wait_ge(tau_made, n + 1)
                        if j > 0:
                            dve.wait_ge(chain, link.base + link.n)
                        stt(y[:, col], tau[:, col], state[:, j, CH:CH + 1], floor[:, col], ALU.mult, ALU.max).then_inc(y_made, 1)
                        dve.wait_ge(y_made, n + 1)
                        stt(w_sq[:, col], floor[:, col], -1.0, y[:, col], ALU.mult, ALU.add).then_inc(w2_made, 1)
                        dve.wait_ge(w2_made, n + 1)
                        dve.wait_ge(var_now, n + 1)
                        stt(rest[:, col], w_sq[:, col], vc[:, half, 1, col], var_e[:, col], ALU.mult, ALU.add).then_inc(chain, 1)
                        link.n += 1
                        if j < CH - 1:
                            stt(state[:, later, CH + 2], zc[:, half, j, later, j], w_sq[:, col], state[:, later, CH + 2],
                                ALU.mult, ALU.add).then_inc(chain, 1)
                            link.n += 1
                        dve.wait_ge(chain, link.base + link.n - (j < CH - 1))
                        dve.wait_ge(w_made, n + 1)
                        if j == CH - 1:
                            dve.tensor_scalar(w_out[:, :, :], w[:, :].unsqueeze(1).to_broadcast([B, 2, CH]), rho[:, 0:1], None,
                                              ALU.mult).then_inc(w_scaled, 1)
                        stt(tau2[:, j + 1:j + 2], w[:, col], state[:, j, CH + 1:CH + 2], rest[:, col], ALU.mult, ALU.add)\
                            .then_inc(T_made, 1)
                        if j < CH - 1:
                            dve.wait_ge(chain, link.base + link.n)
                            stt(state[:, later, CH + 2], state[:, later, j], w[:, col], state[:, later, CH + 2], ALU.mult,
                                ALU.add).then_inc(chain, 1)
                            stt(state[:, later, j + 1:GC], zc[:, half, j, later, j + 1:GC], w[:, col],
                                state[:, later, j + 1:GC], ALU.mult, ALU.add).then_inc(chain, 1)
                            link.n += 2
                            dve.wait_ge(T_made, n + 1)
                            dve.wait_ge(chain, link.base + link.n - 1)
                            stt(floor[:, j + 1:j + 2], tau2[:, j + 1:j + 2], vc[:, half, 0, j + 1:j + 2],
                                state[:, j + 1, CH + 2:CH + 3], ALU.mult, ALU.add).then_inc(chain, 1)
                            link.n += 1
                        if j == RHO_STEP:
                            dve.wait_ge(chain, link.base + link.n)
                            link(dve.reciprocal(rho[:, 0:1], tau[:, col]))
                            link(dve.tensor_scalar(rho[:, 0:1], rho[:, 0:1], START_TAU, None, ALU.mult))
                            tt(rho[:, 1:2], rho[:, 0:1], rho[:, 0:1], ALU.mult).then_inc(chain, 1)
                            link.n += 1
                            dve.tensor_scalar(rho_diag[:, :], ident[0:B, 0:B], rho[:, 0:1], None, ALU.mult).then_inc(rho_made, 1)
                    dve.wait_ge(T_made, n0 + CH)
                    dve.wait_ge(tau_made, n0 + CH + 1)
                    dve.wait_ge(var_now, n0 + CH + 1)
                    dve.sem_inc(dve_seen, 1)
                    dve.tensor_scalar(tau2[:, 0:1], tau2[:, CH:CH + 1], rho[:, 1:2], None, ALU.mult)
                    dve.tensor_scalar(var_e[:, 0:1], var_e[:, CH:CH + 1], rho[:, 1:2], None, ALU.mult)
                    link(dve.tensor_scalar(tau[:, 0:1], tau[:, CH:CH + 1], rho[:, 0:1], None, ALU.mult))
                    dve.wait_ge(wT_done, c + 1)
                    dve.sem_inc(dve_seen, 1)
                    tt(w_rows[:, :, :], gg_rows[:, half, :, :], banks[3][0:2 * CH, 0:B].unsqueeze(2).to_broadcast([2 * CH, B, F]),
                       ALU.mult).then_inc(w_rows_made, 1)
                    dve.wait_ge(mem_scaled, c + 1)
                    dve.wait_ge(mem_added, c + 1)
                    dve.sem_inc(dve_seen, 1)
                    tt(flat(mem[:, :, :]), flat(mem[:, :, :]), banks[4][0:F, :], ALU.add).then_inc(mem_made, 1)
                    dve.sem_inc(rep_used, 1)
            assert link.n == PER_HALF, link.n
            base = base + NCH * PER_HALF
            link.base, link.n = base, 0
            dve.wait_ge(root_made, 1)
            dve.tensor_scalar(rho_diag[:, :], ident[0:B, 0:B], rho[:, 0:1], None, ALU.mult).then_inc(rho_made, 1)
            dve.wait_ge(memT_done, 1)
            dve.tensor_copy(flat(memT[:, :, :]), banks[5][:, 0:B * F]).then_inc(memT_kept, 1)
            dve.wait_ge(mw_done, 1)
            dve.wait_ge(rho_kept, NCH + 1)
            tt(mw[:, :, :], banks[4][0:F, :].rearrange("p (b d) -> p b d", b=B),
               rho_rep[:, :].unsqueeze(2).to_broadcast([F, B, D]), ALU.mult).then_inc(mw_kept, 1)
            dve.wait_ge(rows_stored, 2 * B + 1)
            for b in range(B):
                dve.wait_ge(mo_done, b + 1)
                dst = flat(x_rows[:, b * ST:(b + 1) * ST, :])
                dve.scalar_tensor_tensor(out=dst, in0=dst, scalar=2.0, in1=banks[b][:, :], op0=ALU.mult,
                                         op1=ALU.add).then_inc(mo_kept, 1)
            dve.wait_ge(mo_kept, B)
            with dve.Fori(0, B) as b:
                link.base, link.n = base + b * 2, 0
                norm_sequence(2, b)
                dve.wait_ge(logits_done, B + b + 2)
                dve.tensor_tensor(logits[:, ds(b * ST, ST), :], pv_bank[:, 0:ST * EX].rearrange("p (a d) -> p a d", d=EX),
                                  rb2[:, :].unsqueeze(1).to_broadcast([P, ST, EX]), ALU.add).then_inc(logits_kept, 1)
            link.base, link.n = base + 2 * B, 0
            dve.wait_ge(logits_kept, 2 * B)
            make_gate(1)
            base = base + 2 * B + link.n
            dve.wait_ge(rows_stored, 3 * B + 1)
            with dve.Fori(0, B) as b:
                dve.wait_ge(be_done, b + 1)
                dst = flat(x_rows[:, ds(b * ST, ST), :])
                dve.scalar_tensor_tensor(out=dst, in0=dst, scalar=2.0, in1=pv_bank[:, :], op0=ALU.mult,
                                         op1=ALU.add).then_inc(be_kept, 1)
            dve.wait_ge(be_kept, B)
            dve.sem_inc(mix2.y_kept, 2)
            mixture(mix2)
            dve.wait_ge(mix2.y_kept, EX * B + 2)
            with dve.Fori(0, B) as b:
                link.base, link.n = base + b * 2, 0
                norm_sequence(3, b)

        @block.scalar
        def _(act):
            act.preload_act_table(ACT.Exp)
            with act.Fori(0, B) as b:
                with act.Fori(0, HP) as p:
                    it = b * HP + p

                    def exps(u):
                        W = unit_width(u)
                        act.wait_ge(masked_done, it * UNITS + (u + 1))
                        act.activation(probs[:, u % 3, 0:W], masked[:, u % 2, 0:W], ACT.Exp, bias=row_stats[:, u, 0:1],
                                       scale=-1.0, accum_out=row_stats[:, u, 1:2]).then_inc(exp_done, 1)

                    def keepT(u):
                        hh, qt = divmod(u, ST)
                        act.wait_ge(transposed, it * UNITS + (u + 1))
                        act.activation(probsT[:, hh, 0:qt + 1, qt * P:(qt + 1) * P],
                                       t_bank[u % 2][:, 0:unit_width(u)].rearrange("p (k q) -> p k q", q=P),
                                       ACT.Copy).then_inc(probsT_kept, 1)

                    for u in range(UNITS + 2):
                        if u < UNITS:
                            exps(u)
                        if u >= 2:
                            keepT(u - 2)
                act.wait_ge(xT_stored, b + 1)
                act.wait_ge(logits_done, b + 1)
                act.wait_ge(rows_T, b + 2)
                act.activation(seqT[:, :], y_bank[:, :], ACT.Copy).then_inc(seqT_kept, 1)
            act.wait_ge(shifted, 1)
            act.activation(gate[:, :, :], gate[:, :, :], ACT.Exp).then_inc(gate_exp, 1)

            def mixture(m):
                act.preload_act_table(m.func)
                act.sem_inc(m.h_kept, 4)
                with act.Fori(0, EX // 2) as ep:
                    for j in range(MIX_UNITS):
                        slot = j // B
                        for ft in range(m.tiles):
                            n = j * m.tiles + ft
                            if ft == 0:
                                act.wait_ge(m.y_done, ep * MIX_UNITS + max(j + FREE - 1, FREE))
                            act.wait_ge(m.h_done, ep * (MIX_UNITS * m.tiles) + n + 1)
                            if m is mix2:
                                act.sem_inc(act_seen, 1)
                                act.activation(hidden[:, j % 2, ft, :], banks[n % 4][:, :], m.func,
                                               bias=be1T[:, ds(ep * 2 + slot, 1), ft:ft + 1].rearrange("p a d -> p (a d)"))\
                                   .then_inc(m.h_kept, 1)
                            else:
                                act.activation(hidden[:, j % 2, ft, :], banks[n % 4][:, :], m.func).then_inc(m.h_kept, 1)

            mixture(mix1)
            act.wait_ge(mem_loaded, 7 * 16)
            act.preload_act_table(ACT.Exp)
            with act.Fori(0, B) as b:
                act.wait_ge(q_done, b + 1)
                act.wait_ge(rows_T, B + b + 2)
                act.activation(seqT[:, :], y_bank[:, :], ACT.Copy, scale=norm_w[:, 0:1]).then_inc(seqT_kept, 1)
                act.wait_ge(k_low, 2 * b + 1)
                act.activation(k_exp[:, :, :], k_exp[:, :, :], ACT.Exp).then_inc(k_exped, 1)
                act.wait_ge(k_low, 2 * b + 2)
                act.activation(q_exp[:, :, :], q_exp[:, :, :], ACT.Exp).then_inc(k_exped, 1)
            act.preload_act_table(ACT.Sqrt)
            with act.Fori(0, NCH // 2) as cp:
                for n in range(2 * CH):
                    half, t = divmod(n, CH)
                    act.wait_ge(y_made, cp * (2 * CH) + n + 1)
                    act.activation(w[:, t:t + 1], floor[:, t:t + 1], ACT.Sqrt, bias=y[:, t:t + 1], scale=-1.0).then_inc(w_made, 1)
                    act.wait_ge(T_made, cp * (2 * CH) + n + 1)
                    act.activation(tau[:, t + 1:t + 2], tau2[:, t + 1:t + 2], ACT.Sqrt).then_inc(tau_made, 1)
                    if t == RHO_STEP + 1:
                        act.wait_ge(rho_out, cp * 2 + half + 1)
                        act.activation(rho_rep[:, :], banks[2][0:F, 0:B], ACT.Copy).then_inc(rho_kept, 1)
            act.wait_ge(rho_out, NCH + 1)
            act.activation(rho_rep[:, :], banks[2][0:F, 0:B], ACT.Copy).then_inc(rho_kept, 1)
            act.preload_act_table(ACT.Silu)
            act.wait_ge(d_loaded, 6 * 16)
            with act.Fori(0, B) as b:
                act.wait_ge(xT_stored, B + b + 1)
                act.wait_ge(logits_done, B + b + 1)
                act.wait_ge(rows_T, 2 * B + b + 2)
                act.activation(seqT[:, :], y_bank[:, :], ACT.Copy).then_inc(seqT_kept, 1)
                act.wait_ge(h1_done, b + 1)
                act.activation(h1T[:, :], proj_bank[:, :], ACT.Silu, bias=rb1[:, 0:1]).then_inc(h1_kept, 1)
            act.wait_ge(shifted, 2)
            act.activation(gate[:, :, :], gate[:, :, :], ACT.Exp).then_inc(gate_exp, 1)
            with act.Fori(0, B) as b:
                act.wait_ge(gateT_done, b + 2)
                act.activation(flat(gateT[:, :, :]), proj_bank[0:EX, :], ACT.Copy).then_inc(gateT_kept, 1)
            mixture(mix2)


_OUT = (128, 16, 128)


def kernel(**inputs):
    import numpy as np
    import concourse.bacc as bacc
    from concourse import mybir as mb
    from concourse.bass_utils import run_bass_kernel_spmd

    g = {k: np.asarray(v) for k, v in inputs.items()}
    P = 128
    x = g["L0_attn_x"].reshape(2048, P)
    laid = {
        "ident": np.eye(P, dtype=np.float32),
        "mask": np.concatenate([np.zeros((P, 3 * P), np.float32),
                                np.where(np.triu(np.ones((P, P), bool), 1), np.float32(-8e9), np.float32(0))], 1),
        "iota8": np.tile(np.arange(8, dtype=np.float32), (P, 1)),
        "xT": x.T,
        "x_rows": x.reshape(16, P, P).transpose(1, 0, 2),
        "wq": g["L0_attn_wq"].transpose(1, 0, 2),
        "wk": g["L0_attn_wk"].transpose(1, 0, 2),
        "wvT": g["L0_attn_wv"].reshape(1024, P).T,
        "woT": g["L0_attn_wo"].T.reshape(8, P, P).transpose(1, 0, 2),
        "wg": g["L0_ffn_Wg"],
        "W1": g["L0_ffn_W1"].transpose(1, 0, 2),
        "W2": g["L0_ffn_W2"].reshape(8, 2, P, P).transpose(2, 0, 1, 3),
        "wkT": g["L1_attn_Wk"].T,
        "wqT": g["L1_attn_Wq"].T,
        "wvT1": g["L1_attn_Wv"].T,
        "woutT": g["L1_attn_Wout"].T,
        "norm_w": g["L1_attn_norm_weight"].reshape(P, 1),
        "eta": np.tile(g["L1_attn_eta"], (P, 1)),
        "eta_col": g["L1_attn_eta"].reshape(64, 1),
        "rw1": g["L1_ffn_rw1"],
        "rb1": g["L1_ffn_rb1"].reshape(P, 1),
        "rw2": g["L1_ffn_rw2"],
        "rb2": np.tile(g["L1_ffn_rb2"], (P, 1)),
        "we1": g["L1_ffn_we1"].transpose(1, 0, 2),
        "be1T": g["L1_ffn_be1"].reshape(8, 4, P).transpose(2, 0, 1),
        "we2": g["L1_ffn_we2"].reshape(8, 4, P, P).transpose(2, 0, 1, 3),
        "be2": g["L1_ffn_be2"],
    }
    nc = bacc.Bacc("TRN2", target_bir_lowering=False, num_devices=1)
    arrays, ins = {}, {}
    for name, a in laid.items():
        a = np.ascontiguousarray(a)
        arrays["in_" + name] = a
        ins[name] = nc.dram_tensor("in_" + name, a.shape, mb.dt.from_np(a.dtype), kind="ExternalInput").ap()
    scratch = {name: nc.dram_tensor("scratch_" + name, shape, mb.dt.float32, kind="Internal").ap()
               for name, shape in (("g", (2048, 64)), ("gm", (2048, 64)), ("vt", (2048, P)), ("means", (2048, 3)),
                                   ("gram_kg", (4, 32, 512)), ("gram_v", (4, 16, 512)), ("z", (P, 16 * 16 * 18)),
                                   ("r", (P, 512)), ("vc", (P, 32)))}
    out = nc.dram_tensor("out_0", (P, 16, P), mb.dt.float32, kind="ExternalOutput").ap()
    seq_postln_kernel(nc, ins, out, scratch)
    r = run_bass_kernel_spmd(nc, [arrays], core_ids=[0])
    return np.asarray(r.results[0]["out_0"]).transpose(1, 0, 2).reshape(4, 512, P)
```

```python
import concourse.bass as bass
from concourse import mybir
from contextlib import ExitStack


def seq_postln_kernel(nc, ins, out, scratch):
    f32 = mybir.dt.float32
    u32 = mybir.dt.uint32
    ALU = mybir.AluOpType
    ACT = mybir.ActivationFunctionType
    AX = mybir.AxisListType
    ds = bass.ds

    B, S, D, H, E_DIM = 4, 512, 128, 16, 64
    P = 128
    ST = S // P
    NT = B * ST
    HP = H // 2
    UNITS = 2 * ST
    EX = 8
    F1, F2 = 256, 512
    F = 64
    EPS_LN, EPS_RMS, ETA_MIN = 1e-5, 1e-6, 1e-6
    CH = 16
    NCH = S // CH
    GC = CH + 2
    SC = CH + 4
    HALF_CH = CH // 2
    RHO_STEP = 5
    RHO_READY = RHO_STEP + 3
    START_TAU = 2.0 ** -40

    with ExitStack() as ctx:
        def sb(name, shape, dt=f32, scope=ctx):
            return scope.enter_context(nc.sbuf_tensor(name, shape, dt))

        def sem(name):
            return ctx.enter_context(nc.semaphore(name))

        ident = sb("ident", [P, P])
        x_rows = sb("x_rows", [P, NT, D])
        xT = sb("xT", [P, B * S])
        norm_rows = sb("norm_rows", [P, ST, D])
        seqT = sb("seqT", [P, S])
        bn = sb("bn", [P, ST, 6])
        mv = sb("mv", [P, ST, 2])
        var_eps = sb("var_eps", [P, ST])
        rstd = sb("rstd", [P, ST])
        neg_half = sb("neg_half", [P, ST])
        iota8 = sb("iota8", [P, EX])
        logits = sb("logits", [P, NT, EX])
        top8 = sb("top8", [P, NT, 8])
        top_i = sb("top_i", [P, NT, 8], u32)
        top_f = sb("top_f", [P, NT, 2])
        hot = sb("hot", [P, 2, NT, EX])
        gate = sb("gate", [P, NT, EX])
        gate_sum = sb("gate_sum", [P, NT])
        wg = sb("wg", [P, EX])
        w1 = sb("w1", [P, 2, F2])
        w2 = sb("w2", [P, 2, F2 // P, D])
        hidden = sb("hidden", [P, 2, F2 // P, S])

        with ExitStack() as A:
            mask = sb("mask", [P, S], scope=A)
            wq = sb("wq", [E_DIM, H, D], scope=A)
            wk = sb("wk", [E_DIM, H, D], scope=A)
            wvT = sb("wvT", [P, (HP + 1) * P], scope=A)
            woT = sb("woT", [P, HP, D], scope=A)
            qk_all = sb("qk_all", [P, (HP + 1) * 2 * D], scope=A)
            qk_pair = sb("qk_pair", [P, 2, D], scope=A)
            query = sb("query", [P, 2, S], scope=A)
            v_pair = sb("v_pair", [P, ST, P], scope=A)
            masked = sb("masked", [P, 2, S], scope=A)
            probs = sb("probs", [P, 3, S], scope=A)
            row_stats = sb("row_stats", [P, UNITS, 4], scope=A)
            probsT = sb("probsT", [P, 2, ST, S], scope=A)
            headsT = sb("headsT", [P, S], scope=A)
            xT_b = sb("xT_b", [P, S], scope=A)
        with ExitStack() as A:
            wkT = sb("wkT", [P, F], scope=A)
            wqT = sb("wqT", [P, F], scope=A)
            wvT1 = sb("wvT1", [P, D], scope=A)
            woutT = sb("woutT", [P, D], scope=A)
            norm_w = sb("norm_w", [P, 1], scope=A)
            eta = sb("eta", [P, F], scope=A)
            eta_col = sb("eta_col", [F, 1], scope=A)
            ones = sb("ones", [P, F], scope=A)
            col_scale = sb("col_scale", [P, 4], scope=A)
            rms_rows = sb("rms_rows", [P, ST, D], scope=A)
            ms = sb("ms", [P, ST], scope=A)
            junk = sb("junk", [P, ST, D], scope=A)
            qT = sb("qT", [F, B * S], scope=A)
            q_exp = sb("q_exp", [F, 2, S], scope=A)
            k_exp = sb("k_exp", [P, ST, F], scope=A)
            k_rows = sb("k_rows", [P, ST, F], scope=A)
            g_rows = sb("g_rows", [P, ST, F], scope=A)
            gm_rows = sb("gm_rows", [P, ST, F], scope=A)
            v_rows = sb("v_rows", [P, ST, D], scope=A)
            vt_rows = sb("vt_rows", [P, ST, D], scope=A)
            g_mv = sb("g_mv", [P, ST, 2], scope=A)
            v_mv = sb("v_mv", [P, ST, 2], scope=A)
            means = sb("means", [P, ST, 3], scope=A)
            kg_b = sb("kg_b", [F, NCH, 2, CH], scope=A)
            vT_b = sb("vT_b", [P, S], scope=A)
            kg_all = sb("kg_all", [F, NCH + 1, B, 2 * CH], scope=A)
            vT_all = sb("vT_all", [P, NCH, B, CH], scope=A)
            gram_kg = sb("gram_kg", [2 * CH, S], scope=A)
            gram_v = sb("gram_v", [CH, S], scope=A)
            tA, tG, tV, tVc, tH, tKg, tgg, tvv, tC, tB = (sb(n, [P, CH, CH], scope=A) for n in
                                                          "tA tG tV tVc tH tKg tgg tvv tC tB".split())
            tM = sb("tM", [P, CH, 3], scope=A)
            tZ = sb("tZ", [P, CH, CH, GC], scope=A)
            tmp_z = hidden[:, :, :, :].rearrange("p a t s -> p (a t s)").rearrange("p (j u t) -> p j u t", j=CH, u=CH)
            tR = sb("tR", [P, 2, CH, CH], scope=A)
            tVC = sb("tVC", [P, 2, CH], scope=A)
            zc = sb("zc", [B, 2, CH, CH, GC], scope=A)
            vc = sb("vc", [B, 2, 2, CH], scope=A)
            a_diag = sb("a_diag", [B * CH, 2, B, CH], scope=A)
            na = sb("na", [B * CH, 2, CH], scope=A)
            gg_rows = sb("gg_rows", [2 * CH, 2, B, F], scope=A)
            vv_rows = sb("vv_rows", [2 * CH, 2, B, D], scope=A)
            mem = sb("mem", [F, B, D], scope=A)
            prods = sb("prods", [P, 4, B, CH], scope=A)
            a_prod = sb("a_prod", [B * CH, B, CH], scope=A)
            a_sum = sb("a_sum", [B * CH, CH], scope=A)
            start = sb("start", [B * CH, SC], scope=A)
            spread = sb("spread", [B * CH, CH, SC], scope=A)
            of_step = sb("of_step", [B * CH, CH], scope=A)
            of_sequence = sb("of_sequence", [B * CH, B], scope=A)
            state = sb("state", [B, CH, SC], scope=A)
            tau, tau2, var_e, floor = (sb(n, [B, CH + 1], scope=A) for n in "tau tau2 var_e floor".split())
            var_m = sb("var_m", [B, 1], scope=A)
            y, w, w_sq, rest = (sb(n, [B, CH], scope=A) for n in "y w step_w2 rest".split())
            rho = sb("rho", [B, 2], scope=A)
            rho_diag = sb("rho_diag", [B, B], scope=A)
            rho_rep = sb("rho_rep", [F, B], scope=A)
            w_out = sb("w_out", [B, 2, CH], scope=A)
            w_rows = sb("w_rows", [2 * CH, B, F], scope=A)
            ggT = sb("ggT", [F, B, 2 * CH], scope=A)
            wT = sb("wT", [2 * CH, B], scope=A)
            share = sb("share", [F, B * D], scope=A)
            kg_next = sb("kg_next", [F, B, 2 * CH], scope=A)
            cross = sb("cross", [2 * CH, B, 2 * CH], scope=A)
            xw = sb("xw", [2 * CH, B, 2 * CH], scope=A)
            old_qh = sb("old_qh", [P, B, 2 * CH], scope=A)
            g_mem = sb("g_mem", [P, B, CH], scope=A)
            memT = sb("memT", [P, B, F], scope=A)
            mw = sb("mw", [F, B, D], scope=A)
        with ExitStack() as A:
            be1T = sb("be1T", [P, EX, F2 // P], scope=A)
            be2 = sb("be2", [EX, D], scope=A)
            gate_b = sb("gate_b", [P, ST, EX], scope=A)
            gateT = sb("gateT", [EX, ST, P], scope=A)
            h1T = sb("h1T", [P, S], scope=A)
            rw1 = sb("rw1", [P, D], scope=A)
            rw2 = sb("rw2", [P, EX], scope=A)
            rb1 = sb("rb1", [P, 1], scope=A)
            rb2 = sb("rb2", [P, EX], scope=A)

        banks = [ctx.enter_context(nc.psum_tensor(f"bank{i}", [P, 512], f32)) for i in range(8)]
        s_bank, t_bank = banks[0:3], banks[3:5]
        proj_bank, pv_bank, y_bank = banks[5], banks[6], banks[7]

        loaded, qk_made, qk_kept, seq_staged, pair_staged = map(sem, "loaded qk_made qk_kept seq_staged pair_staged".split())
        proj_done, proj_kept, scores_done, dve_seen, pool_seen, act_seen, masked_done = map(
            sem, "proj_done proj_kept scores_done dve_seen pool_seen act_seen masked_done".split())
        exp_done, recip_done, probs_done, transposed, probsT_kept = map(
            sem, "exp_done recip_done probs_done transposed probsT_kept".split())
        heads_done, heads_kept, y_pair_done, y_kept, chain = map(
            sem, "heads_done heads_kept y_pair_done y_kept chain".split())
        consts_set, var_made, rstd_made, rows_normed, rows_T, seqT_kept, xT_stored, rows_stored = map(
            sem, "consts_set var_made rstd_made rows_normed rows_T seqT_kept xT_stored rows_stored".split())
        logits_done, logits_kept, shifted, gate_exp, gate_made = map(
            sem, "logits_done logits_kept shifted gate_exp gate_made".split())
        mem_loaded, kv_done, k_low, k_exped, kv_kept, q_done, q_kept, kv_sent, T_kept, T_staged, gram_done, gram_kept = map(
            sem, "mem_loaded kv_done k_low k_exped kv_kept q_done q_kept kv_sent T_kept T_staged gram_done gram_kept".split())
        tabs_in, tabs_made, tabs_sent, rep_used, qn_done, prods_made, start_done, start_made, state_in = map(
            sem, "tabs_in tabs_made tabs_sent rep_used qn_done prods_made start_done start_made state_in".split())
        y_made, w2_made, w_made, T_made, tau_made, var_now, rho_made, rho_out, rho_kept, mem_scaled = map(
            sem, "y_made w2_made w_made T_made tau_made var_now rho_made rho_out rho_kept mem_scaled".split())
        pe_seen, w_scaled, wT_done, w_rows_made, mem_added, mem_made, mem_set, root_made, pool_steps = map(
            sem, "pe_seen w_scaled wT_done w_rows_made mem_added mem_made mem_set root_made pool_steps".split())
        rep_in = [sem("rep_in0"), sem("rep_in1")]
        k_mem_made, kv_prods_done, tau_final, share_kept, kg_staged, wT_kept, ggT_done, ggT_kept, cross_done, cross_kept, old_done, old_kept, xw_made = map(
            sem, "k_mem_made kv_prods_done tau_final share_kept kg_staged wT_kept ggT_done ggT_kept cross_done cross_kept old_done old_kept xw_made".split())
        memT_done, memT_kept, mw_done, mw_kept, mo_done, mo_kept = map(
            sem, "memT_done memT_kept mw_done mw_kept mo_done mo_kept".split())
        d_loaded, h1_done, h1_kept, gate_b_staged, gateT_done, gateT_kept, be_done, be_kept, stored, rms_var, rms_normed = map(
            sem, "d_loaded h1_done h1_kept gate_b_staged gateT_done gateT_kept be_done be_kept stored rms_var rms_normed".split())

        class Mixture:
            def __init__(self, n, width, func, w1_d, w2_d):
                self.tiles, self.func, self.w1_d, self.w2_d, self.width = width // P, func, w1_d, w2_d, width
                self.got = [sem(f"mix{n}_weights0"), sem(f"mix{n}_weights1")]
                self.h_done, self.h_kept = sem(f"mix{n}_h_done"), sem(f"mix{n}_h_kept")
                self.y_done, self.y_kept = sem(f"mix{n}_y_done"), sem(f"mix{n}_y_kept")

        mix1 = Mixture(1, F1, ACT.Relu, ins["W1"], ins["W2"])
        mix2 = Mixture(2, F2, ACT.Silu, ins["we1"], ins["we2"])
        MIX_UNITS = 2 * B
        FREE = B + 1

        def unit_width(u):
            return P * (u % ST + 1)

        def flat(ap):
            return ap.rearrange("p a d -> p (a d)")

        class Chain:
            def __init__(self, eng, counter):
                self.eng, self.counter, self.base, self.n = eng, counter, 0, 0

            def __call__(self, instruction):
                self.n += 1
                instruction.then_inc(self.counter, 1)
                self.eng.wait_ge(self.counter, self.base + self.n)

        LOADS = 10 * 16
        SENT = 6 * 16
        CHUNK_IN = (5 + 2 * B) * 16
        block = ctx.enter_context(nc.Block())

        @block.sync
        def _(sp):
            for dst, src in ((wq[:, :, :], "wq"), (wk[:, :, :], "wk"), (xT[:, :], "xT"), (ident[:, :], "ident"),
                             (mask[:, :], "mask"), (wvT[:, 0:HP * P], "wvT"), (woT[:, :, :], "woT"),
                             (x_rows[:, :, :], "x_rows"), (wg[:, :], "wg"), (iota8[:, :], "iota8")):
                sp.dma_start(dst, ins[src]).then_inc(loaded, 16)

            def mixture_weights(m):
                with sp.Fori(0, EX // 2) as ep:
                    for slot in range(2):
                        sp.wait_ge(m.y_done, ep * MIX_UNITS + (slot * B + 1))
                        sp.dma_start(w1[:, slot, 0:m.width],
                                     m.w1_d[:, ds(ep * 2 + slot, 1), :].rearrange("p e f -> p (e f)")).then_inc(m.got[slot], 16)
                        sp.dma_start(w2[:, slot, 0:m.tiles, :],
                                     m.w2_d[:, ds(ep * 2 + slot, 1), :, :].rearrange("p e a d -> p (e a) d")).then_inc(m.got[slot], 16)

            sp.sem_inc(mix1.y_done, FREE)
            mixture_weights(mix1)
            sp.wait_ge(mix1.y_done, EX * B + FREE)
            for dst, src in ((wkT[:, :], "wkT"), (wqT[:, :], "wqT"), (wvT1[:, :], "wvT1"), (woutT[:, :], "woutT"),
                             (norm_w[:, :], "norm_w"), (eta[:, :], "eta"), (eta_col[:, :], "eta_col")):
                sp.dma_start(dst, ins[src]).then_inc(mem_loaded, 16)
            sp.sem_inc(kv_sent, 1)
            with sp.Fori(0, B) as b:
                sp.wait_ge(kv_kept, b + 1)
                for dst, src in (("g", g_rows), ("gm", gm_rows), ("vt", vt_rows), ("means", means)):
                    sp.dma_start(scratch[dst][ds(b * S, S), :].rearrange("(s p) f -> p s f", p=P), src[:, :, :]).then_inc(kv_sent, 16)
                sp.wait_ge(gram_kept, b + 2)
                sp.dma_start(scratch["gram_kg"][ds(b, 1), :, :].rearrange("b u c -> (b u) c"), gram_kg[:, :]).then_inc(kv_sent, 16)
                sp.dma_start(scratch["gram_v"][ds(b, 1), :, :].rearrange("b u c -> (b u) c"), gram_v[:, :]).then_inc(kv_sent, 16)
            sp.wait_ge(kv_sent, B * SENT + 1)
            for b in range(B):
                rows = slice(b * NCH, (b + 1) * NCH)
                for dst, src, u0 in ((tA, "gram_kg", 0), (tG, "gram_kg", CH), (tV, "gram_v", 0)):
                    sp.dma_start(dst[rows, :, :], scratch[src][b, u0:u0 + CH, :].rearrange("u (c j) -> c u j", j=CH)).then_inc(tabs_in, 16)
            sp.dma_start(tM[:, :, :], scratch["means"].rearrange("(p j) s -> p j s", j=CH)).then_inc(tabs_in, 16)
            sp.wait_ge(tabs_made, 3)
            for dst, src in (("z", tZ[:, :, :, :].rearrange("p j u t -> p (j u t)")),
                             ("r", tR[:, :, :, :].rearrange("p a u j -> p (a u j)")),
                             ("vc", tVC[:, :, :].rearrange("p a u -> p (a u)"))):
                sp.dma_start(scratch[dst], src).then_inc(tabs_sent, 16)
            sp.wait_ge(tabs_sent, 3 * 16)
            with sp.Fori(0, NCH // 2) as cp:
                for half in range(2):
                    sp.wait_ge(rep_used, cp * 2 + (half + 1))
                    c = cp * 2 + half

                    def of_chunk(name):
                        a = scratch[name].rearrange("(b c) z -> c b z", b=B)[ds(c, 1), :, :]
                        return a.rearrange("c b z -> (c b) z")

                    sp.dma_start(zc[:, half, :, :, :].rearrange("p j u t -> p (j u t)"), of_chunk("z")).then_inc(rep_in[half], 16)
                    sp.dma_start(vc[:, half, :, :].rearrange("p a u -> p (a u)"), of_chunk("vc")).then_inc(rep_in[half], 16)
                    tables = scratch["r"].rearrange("(b c) (a u j) -> c b a u j", b=B, a=2, j=CH)
                    for b in range(B):
                        rows = slice(b * CH, (b + 1) * CH)
                        for a, dst in ((0, a_diag[rows, half, b, :]), (1, na[rows, half, :])):
                            sp.dma_start(dst, tables[ds(c, 1), b, a, :, :].rearrange("c u j -> (c u) j")).then_inc(rep_in[half], 16)
                    for dst, src in ((gg_rows[0:CH, half, :, :], "g"), (gg_rows[CH:2 * CH, half, :, :], "gm"),
                                     (vv_rows[0:CH, half, :, :], "vt")):
                        steps = scratch[src].rearrange("(b c j) f -> c j b f", b=B, j=CH)[ds(c, 1), :, :, :]
                        sp.dma_start(dst, steps.rearrange("c j b f -> (c j) b f")).then_inc(rep_in[half], 16)
            sp.wait_ge(mo_kept, B)
            for dst, src in ((be1T[:, :, :], "be1T"), (be2[:, :], "be2"), (rw1[:, :], "rw1"), (rw2[:, :], "rw2"),
                             (rb1[:, :], "rb1"), (rb2[:, :], "rb2")):
                sp.dma_start(dst, ins[src]).then_inc(d_loaded, 16)
            sp.sem_inc(mix2.y_done, FREE)
            mixture_weights(mix2)
            sp.wait_ge(rows_stored, 4 * B + 1)
            sp.dma_start(out, x_rows[:, :, :]).then_inc(stored, 16)
            sp.wait_ge(stored, 16)

        @block.gpsimd
        def _(pool):
            pool.memset(neg_half[:, :], -0.5)
            pool.memset(wvT[:, HP * P:(HP + 1) * P], 0.0)
            pool.memset(qk_all[:, HP * 2 * D:(HP + 1) * 2 * D], 0.0).then_inc(consts_set, 1)
            pool.wait_ge(loaded, LOADS)
            pool.wait_ge(qk_kept, 4)
            pool.wait_ge(consts_set, 1)

            def norm_sequence(n, b, keep_T):
                pool.wait_ge(var_made, n * B + b + 1)
                pool.tensor_tensor(rstd[:, :], var_eps[:, :], neg_half[:, :], ALU.pow).then_inc(rstd_made, 1)
                pool.wait_ge(rows_normed, n * B + b + 1)
                pool.sem_inc(pool_seen, 1)
                pool.tensor_copy(x_rows[:, ds(b * ST, ST), :], norm_rows[:, :, :]).then_inc(rows_stored, 1)
                if keep_T is not None:
                    pool.wait_ge(seqT_kept, keep_T * B + b + 1)
                    pool.sem_inc(pool_seen, 1)
                    pool.tensor_copy(xT[:, ds(b * S, S)], seqT[:, :]).then_inc(xT_stored, 1)

            for free in (seq_staged, xT_stored, rows_stored, T_staged):
                pool.sem_inc(free, 1)
            with pool.Fori(0, B) as b:
                pool.wait_ge(scores_done, b * (HP * UNITS) + 1)
                pool.sem_inc(pool_seen, 1)
                pool.tensor_copy(xT_b[:, :], xT[:, ds(b * S, S)]).then_inc(seq_staged, 1)
                with pool.Fori(0, HP + 1) as p:
                    pool.wait_ge(proj_done, (b * (HP + 1) + p) * 3 + 1)
                    pool.sem_inc(pool_seen, 1)
                    pool.tensor_copy(flat(qk_pair[:, :, :]), qk_all[:, ds(p * (2 * D), 2 * D)]).then_inc(pair_staged, 1)
                norm_sequence(0, b, 0)
            with pool.Fori(0, B) as b:
                norm_sequence(1, b, None)
                pool.wait_ge(rms_var, b + 1)
                pool.tensor_tensor(rstd[:, :], var_eps[:, :], neg_half[:, :], ALU.pow).then_inc(rstd_made, 1)
                pool.wait_ge(T_kept, b + 1)
                pool.sem_inc(pool_seen, 1)
                pool.tensor_copy(kg_all[:, 0:NCH, ds(b, 1), :].rearrange("p c b j -> p (c b) j"),
                                 kg_b[:, :, :, :].rearrange("p c a j -> p c (a j)"))
                pool.tensor_copy(vT_all[:, :, ds(b, 1), :].rearrange("p c b j -> p (c b) j"),
                                 vT_b[:, :].rearrange("p (c j) -> p c j", j=CH)).then_inc(T_staged, 1)
            pool.memset(kg_all[:, NCH:NCH + 1, :, :], 0.0).then_inc(T_staged, 1)
            pool.wait_ge(mem_set, 1)
            with pool.Fori(0, NCH // 2) as cp:
                for n in range(2 * CH):
                    t = n % CH
                    half = n // CH
                    col = slice(t, t + 1)
                    at = cp * (2 * CH) + n
                    pool.wait_ge(T_made, at + 1)
                    pool.sem_inc(pool_seen, 1)
                    pool.tensor_scalar(var_m[:, :], tau2[:, col], -EPS_LN, tau2[:, t + 1:t + 2], ALU.mult, ALU.add).then_inc(pool_steps, 1)
                    pool.wait_ge(pool_steps, at + 1)
                    pool.sem_inc(pool_seen, 1)
                    pool.tensor_scalar(var_e[:, t + 1:t + 2], tau2[:, t + 1:t + 2], EPS_LN, var_m[:, :], ALU.mult, ALU.add).then_inc(var_now, 1)
                    if 2 <= t < 2 + B:
                        if t == 2:
                            pool.wait_ge(share_kept, cp * 2 + half + 1)
                        add = pool.tensor_tensor(mem[:, t - 2, :], mem[:, t - 2, :], share[:, (t - 2) * D:(t - 1) * D], ALU.add)
                        if t == 1 + B:
                            add.then_inc(rep_used, 1)
                    if t == 1:
                        pool.tensor_copy(kg_next[:, :, :], kg_all[:, ds(cp * 2 + half + 1, 1), :, :].rearrange("p c b j -> p (c b) j"))\
                            .then_inc(kg_staged, 1)
                    if t == CH - 1:
                        pool.wait_ge(wT_kept, cp * 2 + half + 1)
                        pool.tensor_tensor(w_rows[:, :, :], gg_rows[:, half, :, :],
                                           wT[:, :].unsqueeze(2).to_broadcast([2 * CH, B, F]), ALU.mult).then_inc(w_rows_made, 1)
                    if RHO_READY < t <= RHO_READY + B:
                        b = t - RHO_READY - 1
                        if b == 0:
                            pool.wait_ge(rep_used, cp * 2 + half + 2)
                            pool.wait_ge(rho_kept, cp * 2 + half + 1)
                        scaled = pool.tensor_tensor(mem[:, b, :], mem[:, b, :], rho_rep[:, b:b + 1].to_broadcast([F, D]), ALU.mult)
                        if b == B - 1:
                            scaled.then_inc(mem_scaled, 1)
            pool.wait_ge(share_kept, NCH + 1)
            pool.wait_ge(mem_scaled, NCH)
            pool.tensor_tensor(flat(mem[:, :, :]), flat(mem[:, :, :]), share[:, :], ALU.add).then_inc(mem_made, 1)
            pool.wait_ge(tau_final, 1)
            pool.tensor_tensor(rho[:, 0:1], tau2[:, 0:1], neg_half[0:B, 0:1], ALU.pow).then_inc(root_made, 1)
            with pool.Fori(0, B) as b:
                norm_sequence(2, b, 2)
            with pool.Fori(0, B) as b:
                pool.wait_ge(gate_made, 2)
                pool.wait_ge(gateT_done, b + 1)
                pool.sem_inc(pool_seen, 1)
                pool.tensor_copy(gate_b[:, :, :], gate[:, ds(b * ST, ST), :]).then_inc(gate_b_staged, 1)
            with pool.Fori(0, B) as b:
                norm_sequence(3, b, None)

        @block.tensor
        def _(pe):
            def transpose_rows(src, bank, n, b):
                for st in range(ST):
                    t = pe.transpose(bank[:, st * P:(st + 1) * P], src[:, st, :], ident[:, :])
                t.then_inc(rows_T, 1)

            pe.wait_ge(loaded, LOADS)
            for g in range(4):
                for j in range(4):
                    h = 4 * g + j
                    m = pe.matmul(banks[g][:, j * D:(j + 1) * D], wq[:, h, :], wk[:, h, :], start=True, stop=True)
                m.then_inc(qk_made, 1)
            pe.wait_ge(qk_kept, 4)
            for free in (scores_done, proj_done, gateT_done, logits_done, rows_T, q_done, gram_done, gram_kept):
                pe.sem_inc(free, 1)
            with pe.Fori(0, B) as b:

                def queries(p, hh):
                    n = b * (HP + 1) + p
                    if hh == 0:
                        pe.wait_ge(pair_staged, n + 1)
                    pe.wait_ge(proj_kept, n * 3 + (hh + 1))
                    pe.matmul(proj_bank[:, :], qk_pair[:, hh, :], xT_b[:, :], start=True,
                              stop=True).then_inc(proj_done, 1)

                def values(p):
                    pe.wait_ge(proj_kept, (b * (HP + 1) + p) * 3 + 3)
                    for k in range(ST):
                        m = pe.matmul(proj_bank[:, k * P:(k + 1) * P], xT_b[:, k * P:(k + 1) * P],
                                      wvT[:, ds(p * P, P)], start=True, stop=True)
                    m.then_inc(proj_done, 1)

                pe.wait_ge(seq_staged, b + 2)
                queries(0, 0)
                queries(0, 1)
                values(0)
                with pe.Fori(0, HP) as p:
                    it = b * HP + p
                    pe.wait_ge(proj_kept, (b * (HP + 1) + p) * 3 + 3)
                    pe.sem_inc(pe_seen, 1)

                    def scores(u):
                        hh, qt = divmod(u, ST)
                        if u >= 3:
                            pe.wait_ge(masked_done, it * UNITS + (u - 2))
                        pe.matmul(s_bank[u % 3][:, 0:unit_width(u)], query[:, hh, qt * P:(qt + 1) * P],
                                  xT_b[:, 0:unit_width(u)], start=True, stop=True).then_inc(scores_done, 1)

                    def transposes(u):
                        pe.wait_ge(probs_done, it * UNITS + (u + 1))
                        if u >= 2:
                            pe.wait_ge(probsT_kept, it * UNITS + (u - 1))
                        for k in range(u % ST + 1):
                            t = pe.transpose(t_bank[u % 2][:, k * P:(k + 1) * P], probs[:, u % 3, k * P:(k + 1) * P],
                                             ident[:, :])
                        t.then_inc(transposed, 1)

                    for u in range(UNITS + 2):
                        if u < UNITS:
                            scores(u)
                        if u == UNITS:
                            queries(p + 1, 0)
                        if u >= 2:
                            transposes(u - 2)
                    queries(p + 1, 1)
                    pe.wait_ge(proj_kept, (b * (HP + 1) + p) * 3 + 4)
                    pe.wait_ge(probsT_kept, it * UNITS + UNITS)
                    for k in range(ST):
                        for hh in range(2):
                            m = pe.matmul(pv_bank[hh * 64:(hh + 1) * 64, k * P:S], v_pair[:, k, hh * 64:(hh + 1) * 64],
                                          probsT[:, hh, k, k * P:S], start=(k == 0), stop=(k == ST - 1))
                    m.then_inc(heads_done, 1)
                    values(p + 1)
                    pe.wait_ge(heads_kept, it + 1)
                    pe.wait_ge(y_kept, it + 1)
                    for st in range(ST):
                        m = pe.matmul(y_bank[:, st * D:(st + 1) * D], headsT[:, st * P:(st + 1) * P],
                                      woT[:, ds(p, 1), :].rearrange("p a d -> p (a d)"), start=True, stop=True)
                    m.then_inc(y_pair_done, 1)
                pe.wait_ge(rows_normed, b + 1)
                transpose_rows(norm_rows, y_bank, 0, b)
                pe.wait_ge(seqT_kept, b + 1)
                for st in range(ST):
                    m = pe.matmul(pv_bank[:, st * EX:(st + 1) * EX], seqT[:, st * P:(st + 1) * P], wg[:, :], start=True,
                                  stop=True)
                m.then_inc(logits_done, 1)
                pe.wait_ge(logits_kept, b + 1)

            def mixture(m):
                H_BANKS = 4
                with pe.Fori(0, EX // 2) as ep:
                    for j in range(MIX_UNITS + 1):
                        slot, nb = divmod(j, B)
                        if j < MIX_UNITS:
                            if nb == 0:
                                pe.wait_ge(m.got[slot], ep * 32 + 32)
                            for ft in range(m.tiles):
                                n = j * m.tiles + ft
                                pe.wait_ge(m.h_kept, ep * (MIX_UNITS * m.tiles) + n + 1)
                                pe.matmul(banks[n % H_BANKS][:, :], w1[:, slot, ft * P:(ft + 1) * P],
                                          xT[:, nb * S:(nb + 1) * S], start=True, stop=True).then_inc(m.h_done, 1)
                        if j >= 1:
                            slot = (j - 1) // B
                            pe.wait_ge(m.h_kept, ep * (MIX_UNITS * m.tiles) + (j * m.tiles + H_BANKS))
                            pe.wait_ge(m.y_kept, ep * MIX_UNITS + j)
                            for st in range(ST):
                                for ft in range(m.tiles):
                                    y = pe.matmul(banks[4 + (j - 1) % 2][:, st * D:(st + 1) * D],
                                                  hidden[:, (j - 1) % 2, ft, st * P:(st + 1) * P], w2[:, slot, ft, :],
                                                  start=(ft == 0), stop=(ft == m.tiles - 1))
                            y.then_inc(m.y_done, 1)

            pe.wait_ge(xT_stored, B + 1)
            mixture(mix1)
            pe.wait_ge(mem_loaded, 7 * 16)
            with pe.Fori(0, B) as b:
                pe.wait_ge(rms_normed, b + 1)
                transpose_rows(rms_rows, y_bank, 1, b)
                pe.wait_ge(seqT_kept, B + b + 1)
                for st in range(ST):
                    pe.matmul(proj_bank[:, st * F:(st + 1) * F], seqT[:, st * P:(st + 1) * P], wkT[:, :], start=True,
                              stop=True)
                for st in range(ST):
                    m = pe.matmul(pv_bank[:, st * D:(st + 1) * D], seqT[:, st * P:(st + 1) * P], wvT1[:, :], start=True,
                                  stop=True)
                m.then_inc(kv_done, 1)
                pe.matmul(t_bank[0][0:F, :], wqT[:, :], seqT[:, :], start=True, stop=True)
                pe.matmul(t_bank[1][0:F, :], wkT[:, :], seqT[:, :], start=True, stop=True)
                pe.matmul(banks[2][:, :], wvT1[:, :], seqT[:, :], start=True, stop=True).then_inc(q_done, 1)
                pe.wait_ge(T_kept, b + 1)
                pe.wait_ge(gram_kept, b + 1)
                pe.sem_inc(pe_seen, 1)
                for c in range(NCH):
                    steps = slice(c * CH, (c + 1) * CH)
                    pe.matmul(banks[0][0:2 * CH, steps], kg_b[:, c, :, :].rearrange("p a j -> p (a j)"), kg_b[:, c, 1, :],
                              start=True, stop=True)
                    m = pe.matmul(banks[1][0:CH, steps], vT_b[:, steps], vT_b[:, steps], start=True, stop=True)
                m.then_inc(gram_done, 1)
            pe.wait_ge(T_staged, B + 2)

            def from_memory(bank, kg, done):
                for b in range(B):
                    m = pe.matmul(bank[:, b * 2 * CH:(b + 1) * 2 * CH], mem[:, b, :], kg[:, b, :], start=True, stop=True)
                m.then_inc(done, 1)

            def add_outer(half):
                for b in range(B):
                    m = pe.matmul(banks[4][0:F, b * D:(b + 1) * D], w_rows[:, b, :], vv_rows[:, half, b, :], start=True,
                                  stop=True)
                m.then_inc(mem_added, 1)

            pe.wait_ge(mem_set, 2)
            pe.wait_ge(gram_kept, B + 1)
            from_memory(banks[0], kg_all[:, 0, :, :], qn_done)
            with pe.Fori(0, NCH // 2) as cp:
                for half in range(2):
                    c = cp * 2 + half
                    pe.wait_ge(k_mem_made, c + 1)
                    pe.sem_inc(pe_seen, 1)
                    pe.matmul(banks[1][0:B * CH, 0:B * CH], prods[:, 0, :, :].rearrange("p b j -> p (b j)"),
                              vT_all[:, ds(c, 1), :, :].rearrange("p c b j -> p (c b j)"), start=True,
                              stop=True).then_inc(kv_prods_done, 1)
                    pe.wait_ge(prods_made, c + 1)
                    for i in range(4):
                        m = pe.matmul(banks[2][0:B * CH, 8 + i:9 + i],
                                      prods[:, (i + 1) % 4, :, :].rearrange("p b j -> p (b j)"), col_scale[:, i:i + 1],
                                      start=True, stop=True)
                    m.then_inc(start_done, 1)
                    for part in range(2):
                        pe.wait_ge(start_made, 2 * c + (part + 1))
                        pe.sem_inc(pe_seen, 1)
                        pe.matmul(banks[5 + part][0:B, 0:HALF_CH * SC], of_sequence[:, :],
                                  spread[:, part * HALF_CH:(part + 1) * HALF_CH, :].rearrange("p u s -> p (u s)"),
                                  start=True, stop=True).then_inc(state_in, 1)
                    pe.wait_ge(w_rows_made, c + 1)
                    pe.sem_inc(pe_seen, 1)
                    add_outer(1 - half)
                    for b in range(B):
                        m = pe.matmul(banks[7][0:F, b * 2 * CH:(b + 1) * 2 * CH], gg_rows[:, half, b, :],
                                      ident[0:2 * CH, 0:2 * CH], start=True, stop=True)
                    m.then_inc(ggT_done, 1)
                    pe.wait_ge(kg_staged, c + 1)
                    pe.wait_ge(ggT_kept, c + 1)
                    pe.sem_inc(pe_seen, 1)
                    for b in range(B):
                        m = pe.matmul(banks[7][0:2 * CH, (B + b) * 2 * CH:(B + b + 1) * 2 * CH], ggT[:, b, :],
                                      kg_next[:, b, :], start=True, stop=True)
                    m.then_inc(cross_done, 1)
                    pe.wait_ge(rho_made, c + 1)
                    pe.sem_inc(pe_seen, 1)
                    pe.matmul(banks[2][0:F, 0:B], ones[0:B, :], rho_diag[:, :], start=True, stop=True).then_inc(rho_out, 1)
                    pe.wait_ge(mem_scaled, c + 1)
                    pe.sem_inc(pe_seen, 1)
                    from_memory(banks[6], kg_next, old_done)
                    pe.wait_ge(w_scaled, c + 1)
                    pe.sem_inc(pe_seen, 1)
                    pe.transpose(banks[3][0:2 * CH, 0:B], w_out[:, :, :].rearrange("p a j -> p (a j)"),
                                 ident[0:B, 0:B]).then_inc(wT_done, 1)
                    pe.wait_ge(xw_made, c + 1)
                    pe.sem_inc(pe_seen, 1)
                    for b in range(B):
                        m = pe.matmul(banks[0][:, b * 2 * CH:(b + 1) * 2 * CH], vv_rows[:, half, b, :], xw[:, b, :], start=True,
                                      stop=True)
                    m.then_inc(qn_done, 1)
            pe.wait_ge(w_rows_made, NCH + 1)
            add_outer(1)
            pe.wait_ge(rho_made, NCH + 1)
            pe.matmul(banks[2][0:F, 0:B], ones[0:B, :], rho_diag[:, :], start=True, stop=True).then_inc(rho_out, 1)
            pe.wait_ge(mem_made, 1)
            for b in range(B):
                m = pe.transpose(banks[5][:, b * F:(b + 1) * F], mem[:, b, :], ident[0:F, 0:F])
            m.then_inc(memT_done, 1)
            pe.wait_ge(memT_kept, 1)
            for b in range(B):
                m = pe.matmul(banks[4][0:F, b * D:(b + 1) * D], memT[:, b, :], woutT[:, :], start=True, stop=True)
            m.then_inc(mw_done, 1)
            pe.wait_ge(mw_kept, 1)
            pe.wait_ge(q_kept, B)
            for b in range(B):
                for st in range(ST):
                    i = b * ST + st
                    m = pe.matmul(banks[b][:, st * D:(st + 1) * D], qT[:, i * P:(i + 1) * P], mw[:, b, :], start=True,
                                  stop=True)
                m.then_inc(mo_done, 1)
            pe.wait_ge(d_loaded, 6 * 16)
            with pe.Fori(0, B) as b:
                pe.wait_ge(rows_normed, 2 * B + b + 1)
                transpose_rows(norm_rows, y_bank, 2, b)
                pe.wait_ge(seqT_kept, 2 * B + b + 1)
                pe.matmul(proj_bank[:, :], rw1[:, :], seqT[:, :], start=True, stop=True).then_inc(h1_done, 1)
                pe.wait_ge(h1_kept, b + 1)
                for st in range(ST):
                    m = pe.matmul(pv_bank[:, st * EX:(st + 1) * EX], h1T[:, st * P:(st + 1) * P], rw2[:, :], start=True,
                                  stop=True)
                m.then_inc(logits_done, 1)
                pe.wait_ge(logits_kept, B + b + 1)
            with pe.Fori(0, B) as b:
                pe.wait_ge(gate_b_staged, b + 1)
                for st in range(ST):
                    m = pe.transpose(proj_bank[0:EX, st * P:(st + 1) * P], gate_b[:, st, :], ident[:, :])
                m.then_inc(gateT_done, 1)
                pe.wait_ge(gateT_kept, b + 1)
                for st in range(ST):
                    m = pe.matmul(pv_bank[:, st * D:(st + 1) * D], gateT[:, st, :], be2[:, :], start=True, stop=True)
                m.then_inc(be_done, 1)
                pe.wait_ge(be_kept, b + 1)
            pe.wait_ge(xT_stored, 2 * B + 1)
            mixture(mix2)

        @block.vector
        def _(dve):
            link = Chain(dve, chain)

            def norm_sequence(n, b):
                rows = x_rows[:, ds(b * ST, ST), :]
                for st in range(ST):
                    i = dve.bn_stats(bn[:, st, :], x_rows[:, ds(b * ST + st, 1), :].rearrange("p a d -> p (a d)"))
                link(i)
                dve.sem_inc(dve_seen, 1)
                for st in range(ST):
                    i = dve.bn_aggr(mv[:, st, :], bn[:, st, :])
                link(i)
                dve.tensor_scalar(var_eps[:, :], mv[:, :, 1], EPS_LN, None, ALU.add).then_inc(var_made, 1)
                dve.wait_ge(rows_stored, n * B + b + 1)
                dve.wait_ge(rows_T, n * B + b + 1 if n < 3 else 3 * B + 1)
                dve.wait_ge(rstd_made, rstds(n, b))
                for st in range(ST):
                    i = dve.tensor_scalar(norm_rows[:, st, :],
                                          x_rows[:, ds(b * ST + st, 1), :].rearrange("p a d -> p (a d)"), mv[:, st, 0:1],
                                          rstd[:, st:st + 1], ALU.subtract, ALU.mult)
                i.then_inc(rows_normed, 1)

            def rstds(n, b):
                return (b + 1) if n == 0 else (B + 2 * b + 1) if n == 1 else (n + 1) * B + b + 1

            def make_gate(n):
                for t in range(NT):
                    i = dve.max(top8[:, t, :], logits[:, t, :])
                link(i)
                for t in range(NT):
                    i = dve.max_index(top_i[:, t, :], top8[:, t, :], logits[:, t, :])
                link(i)
                dve.tensor_tensor(gate[:, :, :], logits[:, :, :], top8[:, :, 0:1].to_broadcast([P, NT, EX]),
                                  ALU.subtract).then_inc(shifted, 1)
                link(dve.tensor_copy(top_f[:, :, :], top_i[:, :, 0:2]))
                for k in range(2):
                    i = dve.tensor_tensor(hot[:, k, :, :], iota8[:, :].unsqueeze(1).to_broadcast([P, NT, EX]),
                                          top_f[:, :, k:k + 1].to_broadcast([P, NT, EX]), ALU.is_equal)
                link(i)
                link(dve.tensor_tensor(hot[:, 0, :, :], hot[:, 0, :, :], hot[:, 1, :, :], ALU.add))
                dve.wait_ge(gate_exp, n + 1)
                link(dve.tensor_tensor(gate[:, :, :], gate[:, :, :], hot[:, 0, :, :], ALU.mult))
                link(dve.tensor_reduce(out=gate_sum[:, :], in_=gate[:, :, :], axis=AX.X, op=ALU.add))
                link(dve.reciprocal(gate_sum[:, :], gate_sum[:, :]))
                dve.tensor_tensor(gate[:, :, :], gate[:, :, :], gate_sum[:, :].unsqueeze(2).to_broadcast([P, NT, EX]),
                                  ALU.mult).then_inc(gate_made, 1)
                dve.wait_ge(gate_made, n + 1)

            def mixture(m):
                with dve.Fori(0, EX // 2) as ep:
                    for j in range(MIX_UNITS):
                        slot, nb = divmod(j, B)
                        dve.wait_ge(m.y_done, ep * MIX_UNITS + j + FREE + 1)
                        dve.wait_ge(m.y_kept, ep * MIX_UNITS + max(j - 3, 0) + 2)
                        for st in range(ST):
                            i = nb * ST + st
                            y = dve.scalar_tensor_tensor(out=x_rows[:, i, :], in0=banks[4 + j % 2][:, st * D:(st + 1) * D],
                                                         scalar=gate[:, i, ds(ep * 2 + slot, 1)], in1=x_rows[:, i, :],
                                                         op0=ALU.mult, op1=ALU.add)
                        y.then_inc(m.y_kept, 1)

            dve.wait_ge(loaded, LOADS)
            for g in range(4):
                dve.wait_ge(qk_made, g + 1)
                dve.tensor_copy(qk_all[:, g * 512:(g + 1) * 512], banks[g][:, :]).then_inc(qk_kept, 1)
            for free in (proj_kept, y_kept):
                dve.sem_inc(free, 1)
            with dve.Fori(0, B) as b:

                def keep_queries(p):
                    for hh in range(2):
                        dve.wait_ge(proj_done, (b * (HP + 1) + p) * 3 + (hh + 2))
                        dve.tensor_copy(query[:, hh, :], proj_bank[:, :]).then_inc(proj_kept, 1)

                keep_queries(0)
                with dve.Fori(0, HP) as p:
                    it = b * HP + p

                    def mask_max(u):
                        W = unit_width(u)
                        if u >= 2:
                            dve.wait_ge(exp_done, it * UNITS + (u - 1))
                        dve.wait_ge(scores_done, it * UNITS + (u + 2))
                        dve.sem_inc(dve_seen, 1)
                        dve.tensor_tensor_reduce(out=masked[:, u % 2, 0:W], in0=s_bank[u % 3][:, 0:W],
                                                 in1=mask[:, S - W:S], scale=-0.125, scalar=3.0e38, op0=ALU.add,
                                                 op1=ALU.min, accum_out=row_stats[:, u, 0:1]).then_inc(masked_done, 1)

                    def normalise(u):
                        W = unit_width(u)
                        dve.wait_ge(exp_done, it * UNITS + (u + 1))
                        dve.reciprocal(row_stats[:, u, 2:3], row_stats[:, u, 1:2]).then_inc(recip_done, 1)
                        dve.wait_ge(recip_done, it * UNITS + (u + 1))
                        dve.tensor_scalar(probs[:, u % 3, 0:W], probs[:, u % 3, 0:W], row_stats[:, u, 2:3], None,
                                          ALU.mult).then_inc(probs_done, 1)

                    for u in range(UNITS + 1):
                        if u < UNITS:
                            mask_max(u)
                        if u >= 1:
                            normalise(u - 1)
                    keep_queries(p + 1)
                    dve.wait_ge(heads_done, it + 1)
                    dve.tensor_copy(headsT[:, :], pv_bank[:, :]).then_inc(heads_kept, 1)
                    dve.wait_ge(y_pair_done, it + 1)
                    dve.wait_ge(y_kept, it + 1)
                    dst = flat(x_rows[:, ds(b * ST, ST), :])
                    dve.tensor_tensor(dst, y_bank[:, :], dst, ALU.add).then_inc(y_kept, 1)
                dve.wait_ge(y_kept, (b + 1) * HP + 1)
                link.base, link.n = b * 2, 0
                norm_sequence(0, b)
            link.base, link.n = 2 * B, 0
            dve.wait_ge(logits_kept, B)
            make_gate(0)
            dve.wait_ge(rows_stored, B + 1)
            dve.sem_inc(mix1.y_kept, 2)
            mixture(mix1)
            dve.wait_ge(mix1.y_kept, EX * B + 2)
            base = 2 * B + link.n
            for dst, value in ((ones, 1.0), (vv_rows, 1.0), (a_diag, 0.0), (mem, 0.0), (old_qh, 0.0), (w_rows, 0.0), (tau, 1.0), (tau2, 1.0), (var_e, EPS_LN)):
                dve.memset(dst[(slice(None),) * len(dst.shape)], value)
            for i, value in enumerate((-2.0, 2.0 / (F * D), -1.0, 1.0)):
                m = dve.memset(col_scale[:, i:i + 1], value)
            m.then_inc(mem_set, 1)
            dve.wait_ge(mem_set, 1)
            link.base, link.n = base, 0
            dve.wait_ge(mem_loaded, 7 * 16)
            link(dve.scalar_tensor_tensor(out=eta[:, :], in0=eta[:, :], scalar=-1.0, in1=eta[:, :], op0=ALU.mult, op1=ALU.max))
            link(dve.scalar_tensor_tensor(out=eta_col[:, :], in0=eta_col[:, :], scalar=-1.0, in1=eta_col[:, :], op0=ALU.mult, op1=ALU.max))
            link(dve.tensor_scalar(eta_col[:, :], eta_col[:, :], ETA_MIN, None, ALU.max))
            link(dve.tensor_scalar(eta[:, :], eta[:, :], ETA_MIN, None, ALU.max))
            base = base + link.n
            L1 = 10
            with dve.Fori(0, B) as b:
                link.base, link.n = base + b * L1, 0
                norm_sequence(1, b)
                dve.wait_ge(rows_normed, B + b + 1)
                for st in range(ST):
                    i = dve.tensor_tensor_reduce(out=junk[:, st, :], in0=norm_rows[:, st, :], in1=norm_rows[:, st, :],
                                                  scale=1.0, scalar=0.0, op0=ALU.mult, op1=ALU.add,
                                                  accum_out=ms[:, st:st + 1])
                link(i)
                dve.tensor_scalar(var_eps[:, :], ms[:, :], 1.0 / D, EPS_RMS, ALU.mult, ALU.add).then_inc(rms_var, 1)
                dve.wait_ge(rstd_made, B + 2 * b + 2)
                for st in range(ST):
                    i = dve.tensor_scalar(rms_rows[:, st, :], norm_rows[:, st, :], rstd[:, st:st + 1], None, ALU.mult)
                i.then_inc(rms_normed, 1)
                dve.wait_ge(kv_done, b + 1)
                dve.tensor_scalar(flat(k_exp[:, :, :]), proj_bank[:, 0:ST * F], 0.0, None, ALU.min).then_inc(k_low, 1)
                dve.wait_ge(k_exped, 2 * b + 1)
                dve.wait_ge(kv_sent, b * SENT + 1)
                link(dve.scalar_tensor_tensor(out=flat(k_rows[:, :, :]), in0=proj_bank[:, 0:ST * F], scalar=0.0,
                                              in1=flat(k_exp[:, :, :]), op0=ALU.max, op1=ALU.add))
                dve.tensor_copy(flat(v_rows[:, :, :]), pv_bank[:, :])
                dve.wait_ge(q_done, b + 2)
                dve.tensor_scalar(q_exp[:, 0, :], t_bank[0][0:F, :], 0.0, None, ALU.min)
                dve.tensor_scalar(q_exp[:, 1, :], t_bank[1][0:F, :], 0.0, None, ALU.min).then_inc(k_low, 1)
                dve.wait_ge(T_staged, b + 1)
                dve.wait_ge(gram_done, b + 1)
                dve.sem_inc(dve_seen, 1)
                dve.tensor_copy(vT_b[:, :], banks[2][:, :])
                dve.tensor_tensor(g_rows[:, :, :], k_rows[:, :, :],
                                  eta[:, :].unsqueeze(1).to_broadcast([P, ST, F]), ALU.mult)
                link(dve.tensor_reduce(out=means[:, :, 0], in_=k_rows[:, :, :], axis=AX.X, op=ALU.add))
                dve.wait_ge(k_exped, 2 * b + 2)
                dve.scalar_tensor_tensor(out=qT[:, ds(b * S, S)], in0=t_bank[0][0:F, :], scalar=0.0, in1=q_exp[:, 0, :],
                                         op0=ALU.max, op1=ALU.add).then_inc(q_kept, 1)
                link(dve.scalar_tensor_tensor(out=kg_b[:, :, 0, :], in0=t_bank[1][0:F, :].rearrange("p (c j) -> p c j", j=CH),
                                              scalar=0.0, in1=q_exp[:, 1, :].rearrange("p (c j) -> p c j", j=CH),
                                              op0=ALU.max, op1=ALU.add))
                dve.tensor_scalar(kg_b[:, :, 1, :], kg_b[:, :, 0, :], eta_col[:, 0:1], None, ALU.mult).then_inc(T_kept, 1)
                for src, dst in ((g_rows, g_mv), (v_rows, v_mv)):
                    for st in range(ST):
                        i = dve.bn_stats(bn[:, st, :], src[:, st, :])
                    link(i)
                    dve.sem_inc(dve_seen, 1)
                    for st in range(ST):
                        i = dve.bn_aggr(dst[:, st, :], bn[:, st, :])
                    link(i)
                for st in range(ST):
                    dve.tensor_scalar(gm_rows[:, st, :], g_rows[:, st, :], g_mv[:, st, 0:1], v_mv[:, st, 0:1], ALU.subtract,
                                      ALU.mult)
                    dve.tensor_scalar(vt_rows[:, st, :], v_rows[:, st, :], v_mv[:, st, 0:1], None, ALU.subtract)
                dve.tensor_copy(means[:, :, 1], g_mv[:, :, 0])
                dve.tensor_copy(means[:, :, 2], v_mv[:, :, 0]).then_inc(kv_kept, 1)
                assert link.n == L1, link.n
            base = base + B * L1

            link.base, link.n = base, 0
            dve.wait_ge(tabs_in, (3 * B + 1) * 16)

            def by_u(ap):
                return ap.unsqueeze(2).to_broadcast([P, CH, CH])

            def by_j(ap):
                return ap.unsqueeze(1).to_broadcast([P, CH, CH])

            def tt(out, a, c, op):
                return dve.tensor_tensor(out, a, c, op)

            def stt(out, a, scalar, c, op0, op1):
                return dve.scalar_tensor_tensor(out=out, in0=a, scalar=scalar, in1=c, op0=op0, op1=op1)

            k_sum, g_mean, v_mean = (tM[:, :, i] for i in range(3))
            root_D = float(D) ** 0.5
            tt(tKg[:, :, :], by_u(k_sum), by_j(g_mean), ALU.mult)
            tt(tgg[:, :, :], by_u(g_mean), by_j(g_mean), ALU.mult)
            link(tt(tvv[:, :, :], by_u(v_mean), by_j(v_mean), ALU.mult))
            stt(tVc[:, :, :], tvv[:, :, :], -float(D), tV[:, :, :], ALU.mult, ALU.add)
            link(tt(tH[:, :, :], tA[:, :, :], tKg[:, :, :], ALU.subtract))
            stt(tH[:, :, :], tH[:, :, :], root_D, by_j(v_mean), ALU.mult, ALU.mult)
            stt(tR[:, 1, :, :], tKg[:, :, :], 2.0, by_j(v_mean), ALU.mult, ALU.mult)
            dve.tensor_scalar(tR[:, 0, :, :], tA[:, :, :], -2.0, None, ALU.mult)
            link(stt(tG[:, :, :], tgg[:, :, :], -float(F), tG[:, :, :], ALU.mult, ALU.add))
            dve.tensor_scalar(tKg[:, :, :], tH[:, :, :], -2.0, None, ALU.mult)
            tt(tC[:, :, :], tA[:, :, :], tVc[:, :, :], ALU.mult)
            tt(tG[:, :, :], tG[:, :, :], tV[:, :, :], ALU.mult)
            stt(tgg[:, :, :], tgg[:, :, :], float(F), tVc[:, :, :], ALU.mult, ALU.mult)
            link(stt(tB[:, :, :], tH[:, :, :], root_D, by_u(v_mean), ALU.mult, ALU.mult))
            link(tt(tC[:, :, :], tC[:, :, :], tB[:, :, :], ALU.add))
            link(tt(tB[:, :, :], tG[:, :, :], tgg[:, :, :], ALU.add))
            dve.tensor_scalar(tZ[:, :, :, CH].rearrange("p j u -> p u j"), tC[:, :, :], -2.0, None, ALU.mult)
            link(dve.tensor_scalar(tZ[:, :, :, CH + 1].rearrange("p j u -> p u j"), tB[:, :, :], 2.0 / (F * D), None, ALU.mult))

            def diagonal(ap):
                return ap[:, 0:CH * CH:CH + 1]

            dve.tensor_scalar(tVC[:, 0, :], diagonal(flat(tV[:, :, :])), -1.0, None, ALU.mult)
            dve.tensor_scalar(tVC[:, 1, :], diagonal(flat(tB[:, :, :])), 1.0 / (F * D), None, ALU.mult).then_inc(tabs_made, 1)
            CUBE = [P, CH, CH, CH]
            tt(tmp_z[:, :, :, :], tR[:, 0, :, :].rearrange("p u j -> p j u").unsqueeze(3).to_broadcast(CUBE),
               tA[:, :, :].unsqueeze(1).to_broadcast(CUBE), ALU.mult)
            link(tt(tZ[:, :, :, 0:CH], tKg[:, :, :].rearrange("p u j -> p j u").unsqueeze(3).to_broadcast(CUBE),
                    tH[:, :, :].unsqueeze(1).to_broadcast(CUBE), ALU.mult))
            link(tt(tmp_z[:, :, :, :], tmp_z[:, :, :, :], tVc[:, :, :].unsqueeze(2).to_broadcast(CUBE), ALU.mult))
            link(tt(tZ[:, :, :, 0:CH], tZ[:, :, :, 0:CH], tmp_z[:, :, :, :], ALU.add))
            for j in range(CH):
                i = dve.tensor_scalar(tZ[:, j, :, j], tZ[:, j, :, j], 0.5, None, ALU.mult)
            i.then_inc(tabs_made, 1)
            dve.wait_ge(tabs_made, 2)
            dve.sem_inc(tabs_made, 1)
            base = base + link.n

            both = ident[0:B * CH, 0:B * CH]
            dve.tensor_reduce(out=of_step[:, :], in_=both.rearrange("p (b u) -> p u b", b=B), axis=AX.X, op=ALU.add)
            dve.tensor_reduce(out=of_sequence[:, :], in_=both.rearrange("p (b u) -> p b u", b=B), axis=AX.X,
                              op=ALU.add).then_inc(mem_set, 1)
            dve.wait_ge(mem_set, 2)

            dve.wait_ge(T_staged, B + 1)
            PER_HALF = 8 + 5 * (CH - 1) + 1 + 3 + 1
            for free in (rep_used, old_kept, w_rows_made):
                dve.sem_inc(free, 1)
            dve.sem_inc(tau_made, 1)
            dve.sem_inc(var_now, 1)
            with dve.Fori(0, NCH // 2) as cp:
                for half in range(2):
                    link.base, link.n = base + cp * (2 * PER_HALF) + half * PER_HALF, 0
                    c = cp * 2 + half
                    n0 = cp * (2 * CH) + half * CH
                    dve.wait_ge(qn_done, c + 1)
                    dve.sem_inc(dve_seen, 1)
                    qh = banks[0][:, 0:B * 2 * CH].rearrange("p (b a j) -> p b a j", a=2, j=CH)
                    v_now = vT_all[:, ds(c, 1), :, :].rearrange("p c b j -> p (c b) j")
                    dve.wait_ge(old_kept, c + 1)
                    tt(prods[:, 0, :, :], qh[:, :, 0, :], old_qh[:, :, 0:CH], ALU.add).then_inc(k_mem_made, 1)
                    link(tt(g_mem[:, :, :], qh[:, :, 1, :], old_qh[:, :, CH:2 * CH], ALU.add))
                    tt(prods[:, 1, :, :], prods[:, 0, :, :], v_now, ALU.mult)
                    tt(prods[:, 2, :, :], g_mem[:, :, :], v_now, ALU.mult)
                    tt(prods[:, 3, :, :], prods[:, 0, :, :], prods[:, 0, :, :], ALU.mult).then_inc(prods_made, 1)
                    dve.wait_ge(rep_in[half], cp * CHUNK_IN + CHUNK_IN)
                    dve.wait_ge(kv_prods_done, c + 1)
                    dve.sem_inc(dve_seen, 1)
                    link(tt(flat(a_prod[:, :, :]), banks[1][0:B * CH, 0:B * CH], flat(a_diag[:, half, :, :]), ALU.mult))
                    link(dve.tensor_reduce(out=a_sum[:, :], in_=a_prod[:, :, :].rearrange("p b j -> p j b"), axis=AX.X,
                                           op=ALU.add))
                    dve.wait_ge(start_done, c + 1)
                    dve.sem_inc(dve_seen, 1)
                    link(dve.tensor_copy(start[:, CH:SC], banks[2][0:B * CH, 8:12]))
                    link(stt(start[:, 0:CH], na[:, half, :], start[:, SC - 1:SC], a_sum[:, :], ALU.mult, ALU.add))
                    for part in range(2):
                        steps = slice(part * HALF_CH, (part + 1) * HALF_CH)
                        tt(spread[:, steps, :], start[:, :].unsqueeze(1).to_broadcast([B * CH, HALF_CH, SC]),
                           of_step[:, steps].unsqueeze(2).to_broadcast([B * CH, HALF_CH, SC]), ALU.mult).then_inc(start_made, 1)
                    for part in range(2):
                        dve.wait_ge(state_in, 2 * c + (part + 1))
                        dve.sem_inc(dve_seen, 1)
                        i = dve.tensor_copy(state[:, part * HALF_CH:(part + 1) * HALF_CH, :].rearrange("p u s -> p (u s)"),
                                            banks[5 + part][0:B, 0:HALF_CH * SC])
                        if part == 0:
                            link(i)
                            stt(floor[:, 0:1], vc[:, half, 0, 0:1], tau2[:, 0:1], state[:, 0, CH + 2:CH + 3], ALU.mult,
                                ALU.add).then_inc(chain, 1)
                            link.n += 1
                    i.then_inc(chain, 1)
                    link.n += 1
                    for j in range(CH):
                        n = n0 + j
                        later = slice(j + 1, CH)
                        col = slice(j, j + 1)
                        dve.wait_ge(tau_made, n + 1)
                        dve.wait_ge(chain, link.base + link.n - (j == 0))
                        stt(y[:, col], tau[:, col], state[:, j, CH:CH + 1], floor[:, col], ALU.mult, ALU.max).then_inc(y_made, 1)
                        if j == RHO_STEP + 1:
                            dve.reciprocal(rho[:, 0:1], tau[:, RHO_STEP:RHO_STEP + 1]).then_inc(chain, 1)
                            link.n += 1
                        if j == RHO_STEP + 2:
                            dve.tensor_scalar(rho[:, 0:1], rho[:, 0:1], START_TAU, None, ALU.mult).then_inc(chain, 1)
                            link.n += 1
                        if j == RHO_READY:
                            tt(rho[:, 1:2], rho[:, 0:1], rho[:, 0:1], ALU.mult).then_inc(chain, 1)
                            link.n += 1
                            dve.tensor_scalar(rho_diag[:, :], ident[0:B, 0:B], rho[:, 0:1], None, ALU.mult).then_inc(rho_made, 1)
                        dve.wait_ge(y_made, n + 1)
                        stt(w_sq[:, col], floor[:, col], -1.0, y[:, col], ALU.mult, ALU.add).then_inc(w2_made, 1)
                        if j == 0:
                            dve.wait_ge(chain, link.base + link.n)
                        dve.wait_ge(w2_made, n + 1)
                        dve.wait_ge(var_now, n + 1)
                        stt(rest[:, col], w_sq[:, col], vc[:, half, 1, col], var_e[:, col], ALU.mult, ALU.add).then_inc(chain, 1)
                        link.n += 1
                        if j < CH - 1:
                            stt(state[:, later, CH + 2], zc[:, half, j, later, j], w_sq[:, col], state[:, later, CH + 2],
                                ALU.mult, ALU.add).then_inc(chain, 1)
                            link.n += 1
                        dve.wait_ge(chain, link.base + link.n - (j < CH - 1))
                        dve.wait_ge(w_made, n + 1)
                        if j == CH - 1:
                            dve.tensor_scalar(w_out[:, :, :], w[:, :].unsqueeze(1).to_broadcast([B, 2, CH]), rho[:, 0:1], None,
                                              ALU.mult).then_inc(w_scaled, 1)
                        stt(tau2[:, j + 1:j + 2], w[:, col], state[:, j, CH + 1:CH + 2], rest[:, col], ALU.mult, ALU.add)\
                            .then_inc(T_made, 1)
                        if j < CH - 1:
                            dve.wait_ge(chain, link.base + link.n)
                            stt(state[:, later, CH + 2], state[:, later, j], w[:, col], state[:, later, CH + 2], ALU.mult,
                                ALU.add).then_inc(chain, 1)
                            stt(state[:, later, j + 1:GC], zc[:, half, j, later, j + 1:GC], w[:, col],
                                state[:, later, j + 1:GC], ALU.mult, ALU.add).then_inc(chain, 1)
                            link.n += 2
                            dve.wait_ge(T_made, n + 1)
                            dve.wait_ge(chain, link.base + link.n - 1)
                            stt(floor[:, j + 1:j + 2], tau2[:, j + 1:j + 2], vc[:, half, 0, j + 1:j + 2],
                                state[:, j + 1, CH + 2:CH + 3], ALU.mult, ALU.add).then_inc(chain, 1)
                            link.n += 1
                    dve.wait_ge(cross_kept, c + 1)
                    dve.wait_ge(wT_done, c + 1)
                    dve.sem_inc(dve_seen, 1)
                    tt(xw[:, :, :], cross[:, :, :], banks[3][0:2 * CH, 0:B].unsqueeze(2).to_broadcast([2 * CH, B, 2 * CH]),
                       ALU.mult).then_inc(xw_made, 1)
                    dve.wait_ge(T_made, n0 + CH)
                    dve.wait_ge(tau_made, n0 + CH + 1)
                    dve.wait_ge(var_now, n0 + CH + 1)
                    dve.sem_inc(dve_seen, 1)
                    dve.tensor_scalar(tau2[:, 0:1], tau2[:, CH:CH + 1], rho[:, 1:2], None, ALU.mult)
                    dve.tensor_scalar(var_e[:, 0:1], var_e[:, CH:CH + 1], rho[:, 1:2], None, ALU.mult)
                    link(dve.tensor_scalar(tau[:, 0:1], tau[:, CH:CH + 1], rho[:, 0:1], None, ALU.mult))
            assert link.n == PER_HALF, link.n
            base = base + NCH * PER_HALF
            link.base, link.n = base, 0
            dve.sem_inc(tau_final, 1)
            dve.wait_ge(root_made, 1)
            dve.tensor_scalar(rho_diag[:, :], ident[0:B, 0:B], rho[:, 0:1], None, ALU.mult).then_inc(rho_made, 1)
            dve.wait_ge(memT_done, 1)
            dve.tensor_copy(flat(memT[:, :, :]), banks[5][:, 0:B * F]).then_inc(memT_kept, 1)
            dve.wait_ge(mw_done, 1)
            dve.wait_ge(rho_kept, NCH + 1)
            tt(mw[:, :, :], banks[4][0:F, :].rearrange("p (b d) -> p b d", b=B),
               rho_rep[:, :].unsqueeze(2).to_broadcast([F, B, D]), ALU.mult).then_inc(mw_kept, 1)
            dve.wait_ge(rows_stored, 2 * B + 1)
            for b in range(B):
                dve.wait_ge(mo_done, b + 1)
                dst = flat(x_rows[:, b * ST:(b + 1) * ST, :])
                dve.scalar_tensor_tensor(out=dst, in0=dst, scalar=2.0, in1=banks[b][:, :], op0=ALU.mult,
                                         op1=ALU.add).then_inc(mo_kept, 1)
            dve.wait_ge(mo_kept, B)
            with dve.Fori(0, B) as b:
                link.base, link.n = base + b * 2, 0
                norm_sequence(2, b)
            link.base, link.n = base + 2 * B, 0
            dve.wait_ge(logits_kept, 2 * B)
            dve.wait_ge(d_loaded, 6 * 16)
            link(dve.tensor_tensor(logits[:, :, :], logits[:, :, :], rb2[:, :].unsqueeze(1).to_broadcast([P, NT, EX]), ALU.add))
            make_gate(1)
            base = base + 2 * B + link.n
            dve.wait_ge(rows_stored, 3 * B + 1)
            with dve.Fori(0, B) as b:
                dve.wait_ge(be_done, b + 1)
                dst = flat(x_rows[:, ds(b * ST, ST), :])
                dve.scalar_tensor_tensor(out=dst, in0=dst, scalar=2.0, in1=pv_bank[:, :], op0=ALU.mult,
                                         op1=ALU.add).then_inc(be_kept, 1)
            dve.wait_ge(be_kept, B)
            dve.sem_inc(mix2.y_kept, 2)
            mixture(mix2)
            dve.wait_ge(mix2.y_kept, EX * B + 2)
            with dve.Fori(0, B) as b:
                link.base, link.n = base + b * 2, 0
                norm_sequence(3, b)

        @block.scalar
        def _(act):
            def keep_logits(n, b):
                act.wait_ge(logits_done, n * B + b + 2)
                act.sem_inc(act_seen, 1)
                act.activation(logits[:, ds(b * ST, ST), :], pv_bank[:, 0:ST * EX].rearrange("p (a d) -> p a d", d=EX),
                               ACT.Copy).then_inc(logits_kept, 1)

            act.preload_act_table(ACT.Exp)
            with act.Fori(0, B) as b:

                def keep_values(p):
                    act.wait_ge(proj_done, (b * (HP + 1) + p) * 3 + 4)
                    act.activation(flat(v_pair[:, :, :]), proj_bank[:, :], ACT.Copy).then_inc(proj_kept, 1)

                keep_values(0)
                with act.Fori(0, HP) as p:
                    it = b * HP + p

                    def exps(u):
                        W = unit_width(u)
                        act.wait_ge(masked_done, it * UNITS + (u + 1))
                        act.activation(probs[:, u % 3, 0:W], masked[:, u % 2, 0:W], ACT.Exp, bias=row_stats[:, u, 0:1],
                                       scale=-1.0, accum_out=row_stats[:, u, 1:2]).then_inc(exp_done, 1)

                    def keepT(u):
                        hh, qt = divmod(u, ST)
                        act.wait_ge(transposed, it * UNITS + (u + 1))
                        act.activation(probsT[:, hh, 0:qt + 1, qt * P:(qt + 1) * P],
                                       t_bank[u % 2][:, 0:unit_width(u)].rearrange("p (k q) -> p k q", q=P),
                                       ACT.Copy).then_inc(probsT_kept, 1)

                    for u in range(UNITS + 2):
                        if u < UNITS:
                            exps(u)
                        if u >= 2:
                            keepT(u - 2)
                    act.wait_ge(heads_done, it + 1)
                    keep_values(p + 1)
                act.wait_ge(xT_stored, b + 1)
                act.wait_ge(logits_done, b + 1)
                act.wait_ge(rows_T, b + 2)
                act.activation(seqT[:, :], y_bank[:, :], ACT.Copy).then_inc(seqT_kept, 1)
                keep_logits(0, b)
            act.wait_ge(shifted, 1)
            act.activation(gate[:, :, :], gate[:, :, :], ACT.Exp).then_inc(gate_exp, 1)

            def mixture(m):
                act.preload_act_table(m.func)
                act.sem_inc(m.h_kept, 4)
                with act.Fori(0, EX // 2) as ep:
                    for j in range(MIX_UNITS):
                        slot = j // B
                        for ft in range(m.tiles):
                            n = j * m.tiles + ft
                            if ft == 0:
                                act.wait_ge(m.y_done, ep * MIX_UNITS + max(j + FREE - 1, FREE))
                            act.wait_ge(m.h_done, ep * (MIX_UNITS * m.tiles) + n + 1)
                            if m is mix2:
                                act.sem_inc(act_seen, 1)
                                act.activation(hidden[:, j % 2, ft, :], banks[n % 4][:, :], m.func,
                                               bias=be1T[:, ds(ep * 2 + slot, 1), ft:ft + 1].rearrange("p a d -> p (a d)"))\
                                   .then_inc(m.h_kept, 1)
                            else:
                                act.activation(hidden[:, j % 2, ft, :], banks[n % 4][:, :], m.func).then_inc(m.h_kept, 1)

            mixture(mix1)
            act.wait_ge(mem_loaded, 7 * 16)
            act.preload_act_table(ACT.Exp)
            with act.Fori(0, B) as b:
                act.wait_ge(q_done, b + 1)
                act.wait_ge(rows_T, B + b + 2)
                act.activation(seqT[:, :], y_bank[:, :], ACT.Copy, scale=norm_w[:, 0:1]).then_inc(seqT_kept, 1)
                act.wait_ge(k_low, 2 * b + 1)
                act.activation(k_exp[:, :, :], k_exp[:, :, :], ACT.Exp).then_inc(k_exped, 1)
                act.wait_ge(k_low, 2 * b + 2)
                act.activation(q_exp[:, :, :], q_exp[:, :, :], ACT.Exp).then_inc(k_exped, 1)
                act.wait_ge(kv_sent, b * SENT + 1)
                act.wait_ge(gram_done, b + 2)
                act.activation(gram_kg[:, :], banks[0][0:2 * CH, :], ACT.Copy)
                act.activation(gram_v[:, :], banks[1][0:CH, :], ACT.Copy).then_inc(gram_kept, 1)
            act.preload_act_table(ACT.Sqrt)
            with act.Fori(0, NCH // 2) as cp:
                for n in range(2 * CH):
                    half, t = divmod(n, CH)
                    act.wait_ge(y_made, cp * (2 * CH) + n + 1)
                    act.activation(w[:, t:t + 1], floor[:, t:t + 1], ACT.Sqrt, bias=y[:, t:t + 1], scale=-1.0).then_inc(w_made, 1)
                    act.wait_ge(T_made, cp * (2 * CH) + n + 1)
                    act.activation(tau[:, t + 1:t + 2], tau2[:, t + 1:t + 2], ACT.Sqrt).then_inc(tau_made, 1)
                    for step, done, dst, src, kept in (
                            (1, mem_added, share[:, :], banks[4][0:F, :], share_kept),
                            (3, ggT_done, flat(ggT[:, :, :]), banks[7][0:F, 0:B * 2 * CH], ggT_kept),
                            (6, cross_done, flat(cross[:, :, :]), banks[7][0:2 * CH, B * 2 * CH:2 * B * 2 * CH], cross_kept),
                            (CH - 2, old_done, flat(old_qh[:, :, :]), banks[6][:, 0:B * 2 * CH], old_kept),
                            (CH - 1, xw_made, wT[:, :], banks[3][0:2 * CH, 0:B], wT_kept)):
                        if t == step:
                            act.wait_ge(done, cp * 2 + half + 1)
                            act.activation(dst, src, ACT.Copy).then_inc(kept, 1)
                    if t == RHO_READY + 1:
                        act.wait_ge(rho_out, cp * 2 + half + 1)
                        act.activation(rho_rep[:, :], banks[2][0:F, 0:B], ACT.Copy).then_inc(rho_kept, 1)
            act.wait_ge(mem_added, NCH + 1)
            act.activation(share[:, :], banks[4][0:F, :], ACT.Copy).then_inc(share_kept, 1)
            act.wait_ge(rho_out, NCH + 1)
            act.activation(rho_rep[:, :], banks[2][0:F, 0:B], ACT.Copy).then_inc(rho_kept, 1)
            act.preload_act_table(ACT.Silu)
            act.wait_ge(d_loaded, 6 * 16)
            with act.Fori(0, B) as b:
                act.wait_ge(xT_stored, B + b + 1)
                act.wait_ge(logits_done, B + b + 1)
                act.wait_ge(rows_T, 2 * B + b + 2)
                act.activation(seqT[:, :], y_bank[:, :], ACT.Copy).then_inc(seqT_kept, 1)
                act.wait_ge(h1_done, b + 1)
                act.activation(h1T[:, :], proj_bank[:, :], ACT.Silu, bias=rb1[:, 0:1]).then_inc(h1_kept, 1)
                keep_logits(1, b)
            act.wait_ge(shifted, 2)
            act.activation(gate[:, :, :], gate[:, :, :], ACT.Exp).then_inc(gate_exp, 1)
            with act.Fori(0, B) as b:
                act.wait_ge(gateT_done, b + 2)
                act.activation(flat(gateT[:, :, :]), proj_bank[0:EX, :], ACT.Copy).then_inc(gateT_kept, 1)
            mixture(mix2)


_OUT = (128, 16, 128)


def kernel(**inputs):
    import numpy as np
    import concourse.bacc as bacc
    from concourse import mybir as mb
    from concourse.bass_utils import run_bass_kernel_spmd

    g = {k: np.asarray(v) for k, v in inputs.items()}
    P = 128
    x = g["L0_attn_x"].reshape(2048, P)
    laid = {
        "ident": np.eye(P, dtype=np.float32),
        "mask": np.concatenate([np.zeros((P, 3 * P), np.float32),
                                np.where(np.triu(np.ones((P, P), bool), 1), np.float32(-8e9), np.float32(0))], 1),
        "iota8": np.tile(np.arange(8, dtype=np.float32), (P, 1)),
        "xT": x.T,
        "x_rows": x.reshape(16, P, P).transpose(1, 0, 2),
        "wq": g["L0_attn_wq"].transpose(1, 0, 2),
        "wk": g["L0_attn_wk"].transpose(1, 0, 2),
        "wvT": g["L0_attn_wv"].reshape(1024, P).T,
        "woT": g["L0_attn_wo"].T.reshape(8, P, P).transpose(1, 0, 2),
        "wg": g["L0_ffn_Wg"],
        "W1": g["L0_ffn_W1"].transpose(1, 0, 2),
        "W2": g["L0_ffn_W2"].reshape(8, 2, P, P).transpose(2, 0, 1, 3),
        "wkT": g["L1_attn_Wk"].T,
        "wqT": g["L1_attn_Wq"].T,
        "wvT1": g["L1_attn_Wv"].T,
        "woutT": g["L1_attn_Wout"].T,
        "norm_w": g["L1_attn_norm_weight"].reshape(P, 1),
        "eta": np.tile(g["L1_attn_eta"], (P, 1)),
        "eta_col": g["L1_attn_eta"].reshape(64, 1),
        "rw1": g["L1_ffn_rw1"],
        "rb1": g["L1_ffn_rb1"].reshape(P, 1),
        "rw2": g["L1_ffn_rw2"],
        "rb2": np.tile(g["L1_ffn_rb2"], (P, 1)),
        "we1": g["L1_ffn_we1"].transpose(1, 0, 2),
        "be1T": g["L1_ffn_be1"].reshape(8, 4, P).transpose(2, 0, 1),
        "we2": g["L1_ffn_we2"].reshape(8, 4, P, P).transpose(2, 0, 1, 3),
        "be2": g["L1_ffn_be2"],
    }
    nc = bacc.Bacc("TRN2", target_bir_lowering=False, num_devices=1)
    arrays, ins = {}, {}
    for name, a in laid.items():
        a = np.ascontiguousarray(a)
        arrays["in_" + name] = a
        ins[name] = nc.dram_tensor("in_" + name, a.shape, mb.dt.from_np(a.dtype), kind="ExternalInput").ap()
    scratch = {name: nc.dram_tensor("scratch_" + name, shape, mb.dt.float32, kind="Internal").ap()
               for name, shape in (("g", (2048, 64)), ("gm", (2048, 64)), ("vt", (2048, P)), ("means", (2048, 3)),
                                   ("gram_kg", (4, 32, 512)), ("gram_v", (4, 16, 512)), ("z", (P, 16 * 16 * 18)),
                                   ("r", (P, 512)), ("vc", (P, 32)))}
    out = nc.dram_tensor("out_0", (P, 16, P), mb.dt.float32, kind="ExternalOutput").ap()
    seq_postln_kernel(nc, ins, out, scratch)
    r = run_bass_kernel_spmd(nc, [arrays], core_ids=[0])
    return np.asarray(r.results[0]["out_0"]).transpose(1, 0, 2).reshape(4, 512, P)
```
